# Optimizing a Trainium2 kernel written in Bass

```python
import numpy as np
import jax
import jax.numpy as jnp

def _softmax(x, axis=-1):
    return jax.nn.softmax(x, axis=axis)

def _gelu(x):
    return jax.nn.gelu(x, approximate=True)

def _silu(x):
    return jax.nn.silu(x)

def _sigmoid(x):
    return jax.nn.sigmoid(x)

def _layernorm(x, axis=-1, eps=1e-05):
    m = jnp.mean(x, axis=axis, keepdims=True)
    v = jnp.var(x, axis=axis, keepdims=True)
    return (x - m) / jnp.sqrt(v + eps)

def _scatter_add(tgt, idx, src, axis=0):
    return tgt.at[idx].add(src)

def _segment_sum(src, seg, n):
    return jax.ops.segment_sum(src, seg, n)
kernel_name = 'mk_conv_preact_d4_conv_nhwc128_r2_ac10bd'

def setup_inputs(seed: int=0):
    np.random.seed(seed)
    _w = jnp.asarray

    def _rec_inputs():
        import jax
        import jax.numpy as jnp
        _gk = jax.random.key(seed)
        x = -0.0003482 + 1 * jax.random.normal(jax.random.fold_in(_gk, 1), (1, 192, 192, 64), jnp.float32)
        return x
    x = _rec_inputs()

    def _L0_conv_setup():
        import jax, jax.numpy as jnp
        import numpy as np
        DIM = 64
        HID = 64
        N = 192
        B = 1
        EPS = 1e-05

        def layer_norm(x, w, b):
            m = jnp.mean(x, axis=-1, keepdims=True)
            v = jnp.mean(jnp.square(x - m), axis=-1, keepdims=True)
            return (x - m) * jax.lax.rsqrt(v + EPS) * w + b
        key = jax.random.key(seed)
        ks = jax.random.split(key, 16)
        s = 0.02
        return {'x': jax.random.normal(ks[0], (B, N, N, DIM), jnp.float32), 'norm_w': jnp.ones((DIM,), jnp.float32), 'norm_b': jnp.zeros((DIM,), jnp.float32), 'left_w': jax.random.normal(ks[1], (HID, DIM), jnp.float32) * s, 'left_b': jnp.zeros((HID,), jnp.float32), 'right_w': jax.random.normal(ks[2], (HID, DIM), jnp.float32) * s, 'right_b': jnp.zeros((HID,), jnp.float32), 'lgate_w': jax.random.normal(ks[3], (HID, DIM), jnp.float32) * s, 'lgate_b': jnp.ones((HID,), jnp.float32), 'rgate_w': jax.random.normal(ks[4], (HID, DIM), jnp.float32) * s, 'rgate_b': jnp.ones((HID,), jnp.float32), 'ogate_w': jax.random.normal(ks[5], (HID, DIM), jnp.float32) * s, 'ogate_b': jnp.ones((HID,), jnp.float32), 'ton_w': jnp.ones((HID,), jnp.float32), 'ton_b': jnp.zeros((HID,), jnp.float32), 'out_w': jax.random.normal(ks[6], (DIM, HID), jnp.float32) * s, 'out_b': jnp.zeros((DIM,), jnp.float32)}
    _L0_conv_all = _L0_conv_setup()
    _L0_conv_in = {k: v for k, v in _L0_conv_all.items() if k in ('norm_w', 'norm_b', 'left_w', 'left_b', 'right_w', 'right_b', 'lgate_w', 'lgate_b', 'rgate_w', 'rgate_b', 'ogate_w', 'ogate_b', 'ton_w', 'ton_b', 'out_w', 'out_b')}
    del _L0_conv_all

    def _L1_conv_setup():
        import jax, jax.numpy as jnp
        import numpy as np
        D_MODEL = 64
        CHANNEL = 64
        EPS = 1e-05

        def _layernorm(x, gamma, beta):
            mu = jnp.mean(x, axis=-1, keepdims=True)
            var = jnp.var(x, axis=-1, keepdims=True)
            return (x - mu) * jax.lax.rsqrt(var + EPS) * gamma + beta
        key = jax.random.key(seed)
        ks = jax.random.split(key, 8)
        B, N = (1, 192)
        d, c = (D_MODEL, CHANNEL)
        x = jax.random.normal(ks[0], (B, N, N, d), dtype=jnp.float32)
        ln1_g = jnp.ones((d,), jnp.float32)
        ln1_b = jnp.zeros((d,), jnp.float32)
        W_proj = jax.random.normal(ks[1], (d, 4 * c), dtype=jnp.float32) / np.sqrt(d)
        W_gate = jax.random.normal(ks[2], (d, d), dtype=jnp.float32) / np.sqrt(d)
        ln2_g = jnp.ones((c,), jnp.float32)
        ln2_b = jnp.zeros((c,), jnp.float32)
        W_ab = jax.random.normal(ks[3], (c, d), dtype=jnp.float32) / np.sqrt(c)
        return {'x': x, 'ln1_g': ln1_g, 'ln1_b': ln1_b, 'W_proj': W_proj, 'W_gate': W_gate, 'ln2_g': ln2_g, 'ln2_b': ln2_b, 'W_ab': W_ab}
    _L1_conv_all = _L1_conv_setup()
    _L1_conv_in = {k: v for k, v in _L1_conv_all.items() if k in ('ln1_g', 'ln1_b', 'W_proj', 'W_gate', 'ln2_g', 'ln2_b', 'W_ab')}
    del _L1_conv_all

    def _L2_conv_setup():
        import jax, jax.numpy as jnp
        import numpy as np
        _FP8_MAX = 448.0
        _FP8 = jnp.float8_e4m3fn

        def _quantize_rowwise(x):
            scale = jnp.clip(jnp.max(jnp.abs(x), axis=-1, keepdims=True), 1e-12, None) / _FP8_MAX
            x_fp8 = (x / scale).astype(_FP8)
            return (x_fp8, scale)

        def _fp8_linear(x, w):
            xq, sx = _quantize_rowwise(x)
            wq, sw = _quantize_rowwise(w)
            y = jnp.matmul(xq.astype(jnp.float32), wq.astype(jnp.float32).T)
            return y * sx * sw.T
        key = jax.random.key(seed)
        k1, k2, k3 = jax.random.split(key, 3)
        dim, n = (64, 4)
        x = jax.random.normal(k1, (1, 192, 192, dim), dtype=jnp.float32)
        ln_w = jnp.ones((dim,), dtype=jnp.float32)
        ln_b = jnp.zeros((dim,), dtype=jnp.float32)
        w1 = jax.random.normal(k2, (2 * n * dim, dim), dtype=jnp.float32) * 0.02
        w2 = jax.random.normal(k3, (dim, n * dim), dtype=jnp.float32) * 0.02
        return {'x': x, 'ln_w': ln_w, 'ln_b': ln_b, 'w1': w1, 'w2': w2}
    _L2_conv_all = _L2_conv_setup()
    _L2_conv_in = {k: v for k, v in _L2_conv_all.items() if k in ('ln_w', 'ln_b', 'w1', 'w2')}
    del _L2_conv_all

    def _L3_conv_setup():
        import jax, jax.numpy as jnp
        import numpy as np
        EPS = 1e-05

        def layer_norm(x, g, b):
            m = jnp.mean(x, axis=-1, keepdims=True)
            v = jnp.mean(jnp.square(x - m), axis=-1, keepdims=True)
            return (x - m) * jax.lax.rsqrt(v + EPS) * g + b
        key = jax.random.key(seed)
        ks = jax.random.split(key, 12)
        B, N, D, C = (1, 192, 64, 64)
        s_in = 1.0 / np.sqrt(D)
        s_c = 1.0 / np.sqrt(C)
        return {'z': jax.random.normal(ks[0], (B, N, N, D), dtype=jnp.float32), 'mask': jnp.ones((B, N, N), dtype=jnp.float32), 'norm_g': jnp.ones((D,), jnp.float32), 'norm_b': jnp.zeros((D,), jnp.float32), 'norm_out_g': jnp.ones((C,), jnp.float32), 'norm_out_b': jnp.zeros((C,), jnp.float32), 'Wa': jax.random.normal(ks[1], (D, C), jnp.float32) * s_in, 'ba': jnp.zeros((C,), jnp.float32), 'Wb': jax.random.normal(ks[2], (D, C), jnp.float32) * s_in, 'bb': jnp.zeros((C,), jnp.float32), 'Wga': jax.random.normal(ks[3], (D, C), jnp.float32) * s_in, 'bga': jnp.zeros((C,), jnp.float32), 'Wgb': jax.random.normal(ks[4], (D, C), jnp.float32) * s_in, 'bgb': jnp.zeros((C,), jnp.float32), 'Wo': jax.random.normal(ks[5], (C, D), jnp.float32) * s_c, 'bo': jnp.zeros((D,), jnp.float32), 'Wgo': jax.random.normal(ks[6], (D, D), jnp.float32) * s_in, 'bgo': jnp.zeros((D,), jnp.float32)}
    _L3_conv_all = _L3_conv_setup()
    _L3_conv_in = {k: v for k, v in _L3_conv_all.items() if k in ('mask', 'norm_g', 'norm_b', 'norm_out_g', 'norm_out_b', 'Wa', 'ba', 'Wb', 'bb', 'Wga', 'bga', 'Wgb', 'bgb', 'Wo', 'bo', 'Wgo', 'bgo')}
    del _L3_conv_all
    return {'x': x, 'L0_conv_norm_w': _L0_conv_in['norm_w'], 'L0_conv_norm_b': _L0_conv_in['norm_b'], 'L0_conv_left_w': _L0_conv_in['left_w'], 'L0_conv_left_b': _L0_conv_in['left_b'], 'L0_conv_right_w': _L0_conv_in['right_w'], 'L0_conv_right_b': _L0_conv_in['right_b'], 'L0_conv_lgate_w': _L0_conv_in['lgate_w'], 'L0_conv_lgate_b': _L0_conv_in['lgate_b'], 'L0_conv_rgate_w': _L0_conv_in['rgate_w'], 'L0_conv_rgate_b': _L0_conv_in['rgate_b'], 'L0_conv_ogate_w': _L0_conv_in['ogate_w'], 'L0_conv_ogate_b': _L0_conv_in['ogate_b'], 'L0_conv_ton_w': _L0_conv_in['ton_w'], 'L0_conv_ton_b': _L0_conv_in['ton_b'], 'L0_conv_out_w': _L0_conv_in['out_w'], 'L0_conv_out_b': _L0_conv_in['out_b'], 'L1_conv_ln1_g': _L1_conv_in['ln1_g'], 'L1_conv_ln1_b': _L1_conv_in['ln1_b'], 'L1_conv_W_proj': _L1_conv_in['W_proj'], 'L1_conv_W_gate': _L1_conv_in['W_gate'], 'L1_conv_ln2_g': _L1_conv_in['ln2_g'], 'L1_conv_ln2_b': _L1_conv_in['ln2_b'], 'L1_conv_W_ab': _L1_conv_in['W_ab'], 'L2_conv_ln_w': _L2_conv_in['ln_w'], 'L2_conv_ln_b': _L2_conv_in['ln_b'], 'L2_conv_w1': _L2_conv_in['w1'], 'L2_conv_w2': _L2_conv_in['w2'], 'L3_conv_mask': _L3_conv_in['mask'], 'L3_conv_norm_g': _L3_conv_in['norm_g'], 'L3_conv_norm_b': _L3_conv_in['norm_b'], 'L3_conv_norm_out_g': _L3_conv_in['norm_out_g'], 'L3_conv_norm_out_b': _L3_conv_in['norm_out_b'], 'L3_conv_Wa': _L3_conv_in['Wa'], 'L3_conv_ba': _L3_conv_in['ba'], 'L3_conv_Wb': _L3_conv_in['Wb'], 'L3_conv_bb': _L3_conv_in['bb'], 'L3_conv_Wga': _L3_conv_in['Wga'], 'L3_conv_bga': _L3_conv_in['bga'], 'L3_conv_Wgb': _L3_conv_in['Wgb'], 'L3_conv_bgb': _L3_conv_in['bgb'], 'L3_conv_Wo': _L3_conv_in['Wo'], 'L3_conv_bo': _L3_conv_in['bo'], 'L3_conv_Wgo': _L3_conv_in['Wgo'], 'L3_conv_bgo': _L3_conv_in['bgo']}

def reference(x, L0_conv_norm_w, L0_conv_norm_b, L0_conv_left_w, L0_conv_left_b, L0_conv_right_w, L0_conv_right_b, L0_conv_lgate_w, L0_conv_lgate_b, L0_conv_rgate_w, L0_conv_rgate_b, L0_conv_ogate_w, L0_conv_ogate_b, L0_conv_ton_w, L0_conv_ton_b, L0_conv_out_w, L0_conv_out_b, L1_conv_ln1_g, L1_conv_ln1_b, L1_conv_W_proj, L1_conv_W_gate, L1_conv_ln2_g, L1_conv_ln2_b, L1_conv_W_ab, L2_conv_ln_w, L2_conv_ln_b, L2_conv_w1, L2_conv_w2, L3_conv_mask, L3_conv_norm_g, L3_conv_norm_b, L3_conv_norm_out_g, L3_conv_norm_out_b, L3_conv_Wa, L3_conv_ba, L3_conv_Wb, L3_conv_bb, L3_conv_Wga, L3_conv_bga, L3_conv_Wgb, L3_conv_bgb, L3_conv_Wo, L3_conv_bo, L3_conv_Wgo, L3_conv_bgo):
    import jax
    import jax.numpy as jnp

    def _L0_conv_ref(x, norm_w, norm_b, left_w, left_b, right_w, right_b, lgate_w, lgate_b, rgate_w, rgate_b, ogate_w, ogate_b, ton_w, ton_b, out_w, out_b):
        import jax, jax.numpy as jnp
        import numpy as np
        DIM = 64
        HID = 64
        N = 192
        B = 1
        EPS = 1e-05

        def layer_norm(x, w, b):
            m = jnp.mean(x, axis=-1, keepdims=True)
            v = jnp.mean(jnp.square(x - m), axis=-1, keepdims=True)
            return (x - m) * jax.lax.rsqrt(v + EPS) * w + b
        xn = layer_norm(x, norm_w, norm_b)
        lin = lambda w, b: jnp.einsum('bijd,ed->bije', xn, w) + b
        left = lin(left_w, left_b) * jax.nn.sigmoid(lin(lgate_w, lgate_b))
        right = lin(right_w, right_b) * jax.nn.sigmoid(lin(rgate_w, rgate_b))
        out_gate = jax.nn.sigmoid(lin(ogate_w, ogate_b))
        out = jnp.einsum('bkjd,bkid->bijd', left, right)
        out = layer_norm(out, ton_w, ton_b)
        out = jnp.einsum('bijh,dh->bijd', out, out_w) + out_b
        return out * out_gate

    def _L1_conv_ref(x, ln1_g, ln1_b, W_proj, W_gate, ln2_g, ln2_b, W_ab):
        import jax, jax.numpy as jnp
        import numpy as np
        D_MODEL = 64
        CHANNEL = 64
        EPS = 1e-05

        def _layernorm(x, gamma, beta):
            mu = jnp.mean(x, axis=-1, keepdims=True)
            var = jnp.var(x, axis=-1, keepdims=True)
            return (x - mu) * jax.lax.rsqrt(var + EPS) * gamma + beta
        xn = _layernorm(x, ln1_g, ln1_b)
        proj = xn @ W_proj
        a1, a2, b1, b2 = jnp.split(proj, 4, axis=-1)
        g = jax.nn.sigmoid(xn @ W_gate)
        a = jax.nn.sigmoid(a1) * a2
        b = jax.nn.sigmoid(b1) * b2
        ab = jnp.einsum('bikc,bjkc->bijc', a, b)
        out = _layernorm(ab, ln2_g, ln2_b) @ W_ab
        return g * out

    def _L2_conv_ref(x, ln_w, ln_b, w1, w2):
        import jax, jax.numpy as jnp
        import numpy as np
        _FP8_MAX = 448.0
        _FP8 = jnp.float8_e4m3fn

        def _quantize_rowwise(x):
            scale = jnp.clip(jnp.max(jnp.abs(x), axis=-1, keepdims=True), 1e-12, None) / _FP8_MAX
            x_fp8 = (x / scale).astype(_FP8)
            return (x_fp8, scale)

        def _fp8_linear(x, w):
            xq, sx = _quantize_rowwise(x)
            wq, sw = _quantize_rowwise(w)
            y = jnp.matmul(xq.astype(jnp.float32), wq.astype(jnp.float32).T)
            return y * sx * sw.T
        eps = 1e-05
        orig_shape = x.shape
        dim = orig_shape[-1]
        x2 = x.reshape(-1, dim)
        mu = jnp.mean(x2, axis=-1, keepdims=True)
        var = jnp.mean(jnp.square(x2 - mu), axis=-1, keepdims=True)
        h = (x2 - mu) * jax.lax.rsqrt(var + eps) * ln_w + ln_b
        ab = _fp8_linear(h, w1)
        a, b = jnp.split(ab, 2, axis=-1)
        g = jax.nn.relu(a) * b
        out = _fp8_linear(g, w2)
        return out.reshape(orig_shape)

    def _L3_conv_ref(z, mask, norm_g, norm_b, norm_out_g, norm_out_b, Wa, ba, Wb, bb, Wga, bga, Wgb, bgb, Wo, bo, Wgo, bgo):
        import jax, jax.numpy as jnp
        import numpy as np
        EPS = 1e-05

        def layer_norm(x, g, b):
            m = jnp.mean(x, axis=-1, keepdims=True)
            v = jnp.mean(jnp.square(x - m), axis=-1, keepdims=True)
            return (x - m) * jax.lax.rsqrt(v + EPS) * g + b
        z_norm = layer_norm(z, norm_g, norm_b)
        left = (z_norm @ Wa + ba) * jax.nn.sigmoid(z_norm @ Wga + bga)
        right = (z_norm @ Wb + bb) * jax.nn.sigmoid(z_norm @ Wgb + bgb)
        m = mask[..., None]
        left = left * m
        right = right * m
        z_out = jnp.einsum('bikc,bjkc->bijc', left, right)
        z_out = layer_norm(z_out, norm_out_g, norm_out_b)
        z_update = (z_out @ Wo + bo) * jax.nn.sigmoid(z_norm @ Wgo + bgo)
        return z_update

    def _gn(v, G=32, eps=1e-05):
        B_, H_, W_, C_ = v.shape
        g = v.reshape(B_, H_, W_, G, C_ // G)
        m = jnp.mean(g, axis=(1, 2, 4), keepdims=True)
        s = jnp.var(g, axis=(1, 2, 4), keepdims=True)
        return ((g - m) / jnp.sqrt(s + eps)).reshape(v.shape)

    def _ln_c(v, eps=1e-06):
        m = jnp.mean(v, axis=-1, keepdims=True)
        s = jnp.var(v, axis=-1, keepdims=True)
        return (v - m) / jnp.sqrt(s + eps)

    def _ln_t(v, eps=1e-05):
        m = jnp.mean(v, axis=-1, keepdims=True)
        s = jnp.var(v, axis=-1, keepdims=True)
        return (v - m) / jnp.sqrt(s + eps)

    def _to_tokens(v):
        B_, H_, W_, C_ = v.shape
        return v.reshape(B_, H_ * W_, C_)

    def _from_tokens(t, like):
        return t.reshape(like.shape)
    x = x + _L0_conv_ref(_gn(x), L0_conv_norm_w, L0_conv_norm_b, L0_conv_left_w, L0_conv_left_b, L0_conv_right_w, L0_conv_right_b, L0_conv_lgate_w, L0_conv_lgate_b, L0_conv_rgate_w, L0_conv_rgate_b, L0_conv_ogate_w, L0_conv_ogate_b, L0_conv_ton_w, L0_conv_ton_b, L0_conv_out_w, L0_conv_out_b)
    x = x + _L1_conv_ref(_gn(x), L1_conv_ln1_g, L1_conv_ln1_b, L1_conv_W_proj, L1_conv_W_gate, L1_conv_ln2_g, L1_conv_ln2_b, L1_conv_W_ab)
    x = x + _L2_conv_ref(_gn(x), L2_conv_ln_w, L2_conv_ln_b, L2_conv_w1, L2_conv_w2)
    x = x + _L3_conv_ref(_gn(x), L3_conv_mask, L3_conv_norm_g, L3_conv_norm_b, L3_conv_norm_out_g, L3_conv_norm_out_b, L3_conv_Wa, L3_conv_ba, L3_conv_Wb, L3_conv_bb, L3_conv_Wga, L3_conv_bga, L3_conv_Wgb, L3_conv_bgb, L3_conv_Wo, L3_conv_bo, L3_conv_Wgo, L3_conv_bgo)
    return x

_drawn_inputs = setup_inputs


def setup_inputs(seed=0):
    import zlib

    import numpy as np

    out = dict(_drawn_inputs(seed))
    spreads = {'L0_conv_norm_w': (1.0, 0.6),
     'L0_conv_norm_b': (0.0, 0.1),
     'L0_conv_left_b': (0.0, 0.1),
     'L0_conv_right_b': (0.0, 0.1),
     'L0_conv_lgate_b': (1.0, 0.6),
     'L0_conv_rgate_b': (1.0, 0.6),
     'L0_conv_ogate_b': (1.0, 0.6),
     'L0_conv_ton_w': (1.0, 0.2),
     'L0_conv_ton_b': (0.0, 0.407),
     'L0_conv_out_b': (0.0, 0.1),
     'L1_conv_ln1_g': (1.0, 0.2),
     'L1_conv_ln1_b': (0.0, 0.1),
     'L1_conv_ln2_g': (1.0, 0.2),
     'L1_conv_ln2_b': (0.0, 0.1),
     'L2_conv_ln_w': (1.0, 0.6),
     'L2_conv_ln_b': (0.0, 0.8),
     'L3_conv_norm_g': (1.0, 0.548),
     'L3_conv_norm_b': (0.0, 0.1),
     'L3_conv_norm_out_g': (1.0, 0.6),
     'L3_conv_norm_out_b': (0.0, 0.8),
     'L3_conv_ba': (0.0, 0.1),
     'L3_conv_bb': (0.0, 0.327),
     'L3_conv_bga': (0.0, 2.0),
     'L3_conv_bgb': (0.0, 2.0),
     'L3_conv_bo': (0.0, 0.8),
     'L3_conv_bgo': (0.0, 1.944)}
    factors = {'L0_conv_lgate_w': 8.0,
     'L0_conv_rgate_w': 8.0,
     'L0_conv_ogate_w': 6.437,
     'L2_conv_w1': 8.0,
     'L2_conv_w2': 8.0}
    for name, (base, spread) in spreads.items():
        noise = np.random.default_rng([zlib.crc32(name.encode()), seed]).standard_normal(out[name].shape)
        drawn = base * np.exp(spread * noise) if base else spread * noise
        out[name] = jnp.asarray(drawn.astype(out[name].dtype))
    for name, factor in factors.items():
        out[name] = (out[name] * factor).astype(out[name].dtype)
    return out
```

```python
from contextlib import ExitStack

import numpy as np

import concourse.bass as bass
from concourse import mybir

F32 = mybir.dt.float32
BF16 = mybir.dt.bfloat16
ALU = mybir.AluOpType
ACT = mybir.ActivationFunctionType
AX = mybir.AxisListType

P = 128
N = 192
C = 64
U = 8
ROW = U * C
TILES = N * N // (P * U)
TILES_A = N // U
COLS = TILES * U
GROUPS = C // 2
GN_COUNT = float(N * N * 2)
GN_EPS = 1e-5
LN_EPS = 1e-5
PAIRS = U // 2
PROJ = 5 * C
BLK = 4
BLOCKS = C // BLK
HID = 256
FP8_MAX = 448.0
SPLIT = float(2 ** 20)
SUBNORMAL = 1.5 * 2.0 ** 14
TRIANGLES = {0: 0, 1: 1, 3: 2}
LAST = 3


def pipeline(eng, stages, n=TILES):
    leads = [s for s, _ in stages]
    first, start, end = -max(leads), 2 - min(leads), n - min(leads)
    turns = (n - max(leads) - start) // 2

    def peeled(i):
        for s, f in stages:
            if 0 <= i + s < n:
                f(i + s, (i + s) % 2)

    for i in range(first, start):
        peeled(i)
    with eng.Fori(start, start + 2 * turns - 1, 2) as i:
        for j in range(2):
            for s, f in stages:
                f(i + (j + s), (start + j + s) % 2)
    for i in range(start + 2 * turns, end):
        peeled(i)


def wait_free(eng, semaphore, value):
    if not (isinstance(value, int) and value <= 0):
        eng.wait_ge(semaphore, value)


def build(nc, x_in, weights, biases, norms, mask, mlp_norm, w1, w2, out, layers=4):
    with ExitStack() as ctx:
        def sb(name, shape, dt=F32):
            return ctx.enter_context(nc.sbuf_tensor(name, shape, dt))

        def sem(name):
            return ctx.enter_context(nc.semaphore(name))

        x_nat = nc.dram_tensor("x_nat", (N, N, C), F32, kind="Internal").ap()
        x_mid = [nc.dram_tensor(f"x_mid{i}", (TILES, P, ROW), F32, kind="Internal").ap() for i in range(2)]
        gate_dram = nc.dram_tensor("gate_dram", (3 * TILES, P, ROW), F32, kind="Internal").ap()

        pairs = sb("pairs", [P, 2, C, COLS])
        work = sb("work", [P, 11264])

        def part(buf, lo, n, bufs=2):
            return buf[:, lo:lo + n * bufs].rearrange("p (b f) -> p b f", b=bufs)

        xin, cent, normed, xn, xnT = (part(work, 1024 * k, ROW) for k in range(5))
        sig = part(work, 6144, U * 3 * C)
        wbias = work[:, 9216:9216 + 3 * (PROJ + C)].rearrange("p (q e) -> p q e", q=3)
        stat_a, mov_a, stat_b, mov_b = (part(work, 2 * BLK * N * k, BLK * N).rearrange("p b (k n) -> p b k n", k=BLK)
                                        for k in range(4))
        xres, gate, prod = (part(work, 1024 * k, ROW) for k in range(3))
        xnew, shifted, squares = (part(work, 5120 + 1024 * k, ROW) for k in range(3))
        wide = pairs[:].rearrange("p a c n -> p (a c n)")
        h_norm, h_pre, h_act, h_scaled, h_magic, h_added = (part(wide, 1024 * k, ROW) for k in range(6))
        q_in = part(wide, 6144, ROW // 2).bitcast(BF16)
        hidden, scaled, magic, added = (part(wide, 4096 * k, U * HID) for k in range(4))
        q_hid = part(wide, 16384, U * HID // 2).bitcast(BF16)
        q_hidT = part(wide, 18432, U * HID // 2).bitcast(BF16)
        relu_a = part(wide, 20480, 2 * HID)
        q_all = wide[:, 21504:21504 + TILES * ROW // 2].bitcast(BF16).rearrange("p (t f) -> p t f", t=TILES)
        xres_m, prod_m = (part(wide, 30720 + 1024 * k, ROW) for k in range(2))
        qT = part(wide, 32768, ROW // 2).bitcast(BF16)
        wq_raw, wq_y, wq_magic, wq_added, wq_q = (wide[:, 768 * k:768 * (k + 1)] for k in range(5))
        w_rest = wide[:, 768 * 5:768 * 5 + 640]
        fold_tmp = wide[:, 8192:8192 + PROJ + C]

        ident = sb("ident", [P, P])
        ident16 = sb("ident16", [P, P], BF16)
        ones = sb("ones", [P, P])
        half_power = sb("half_power", [P, GROUPS])
        wfold = sb("wfold", [P, 3, PROJ + C])
        nrm = sb("nrm", [P, 3, 4])
        nrm_d = sb("nrm_d", [P, 3, 2])
        mlp_wb = sb("mlp_wb", [P, 2, C])
        mask_sb = sb("mask_sb", [P, COLS])
        mask_t = sb("mask_t", [P, 2, U])
        stats = sb("stats", [P, 2, U, 6])
        ln_s = sb("ln_s", [P, 2, 8, U])
        SUM2, DIFF, M2, DIFF2, V64, VAR, RSTD, SHIFT = range(8)
        tok = sb("tok", [P, 8, U])
        sx_all = sb("sx_all", [P, TILES, U])
        sg_all = sb("sg_all", [P, TILES, U])
        rescale = sb("rescale", [P, 2, U])
        wscale = sb("wscale", [P, 3, 5])
        anchor = sb("anchor", [P, C])
        gn_mean = sb("gn_mean", [P, C])
        gn_rstd = sb("gn_rstd", [P, C])
        gn_s = sb("gn_s", [P, 8, GROUPS])
        w1s = sb("w1s", [P, 3, 2 * HID], BF16)
        w2s = sb("w2s", [P, 3, 2 * C], BF16)

        ps = ctx.enter_context(nc.psum_tensor("ps", [P, 8, 512], F32))
        T_BANK, SUM, SQ = 4, 6, 7
        H_BANK, O_BANK = 4, 5

        (s_const,
         s_params,
         s_fold, s_fold_pe,
         s_quant, s_quant_abs, s_quant_pe,
         x_loaded,
         x_centred,
         x_scaled,
         ln_step,
         var_ready,
         rstd_ready,
         xn_ready,
         xnT_psum,
         xnT_ready,
         proj_ready,
         sig_ready,
         pair_stored,
         gate_stored,
         mask_ready,
         stat_staged, mov_staged, b_staged,
         chan_done,
         z_act, z_dve,
         res_loaded,
         out_ready,
         prod_ready,
         xnew_ready,
         xnew_stored,
         shift_ready,
         sq_ready,
         sums_ready,
         gn_step, gn_var, gn_pow, gn_ready,
         anchor_sum, anchor_step, anchor_ready,
         hw_ready, h_ready, h_step,
         hs_ready, habs_ready, hadd_step, hadd_ready, hq_ready,
         qT_psum, qT_ready, q_copied,
         acc_ready, relu_ready, acc_used,
         hid_step, hid_scale, hid_scaled, hid_abs, hid_max, hid_added, hid_q,
         hqT_psum, hqT_ready,
         mlp_out_ready, mres_loaded,
         s_apart) = [sem(f"sem_{k}") for k in range(68)]

        x_loaded, gate_stored, b_staged, res_loaded, xnew_stored, mres_loaded = [
            (one, sem(f"sem_odd_{k}")) for k, one in enumerate((x_loaded, gate_stored, b_staged, res_loaded, xnew_stored, mres_loaded))]

        tri_before = {l: sum(k in TRIANGLES for k in range(l)) for l in range(5)}

        def x_base(l):
            return TILES * l

        def sum_base(l):
            return TILES * (l + 1)

        def ln_base(l, side):
            return TILES * (l + tri_before[l] + side)

        def tr_base(l, side):
            return TILES * (2 * TRIANGLES[l] + side)

        def landed(each, n, b):
            return (n - b) * (each // 2) + each

        def tokens(ap):
            return ap.rearrange("p (u c) -> p u c", c=C)

        def over_tokens(ap):
            return ap.unsqueeze(1).to_broadcast([P, U, C])

        def over_channels(ap):
            return ap.unsqueeze(2).to_broadcast([P, U, C])

        def cols(t):
            return bass.ds(t * U, U)

        block = ctx.enter_context(nc.Block())

        @block.sync
        def _(sp):
            def load_natural(dst, t, free0, signal):
                sp.dma_start(tokens(dst)[0:64], free0[0]).then_inc(signal, 16)
                sp.dma_start(tokens(dst)[64:P], free0[1]).then_inc(signal, 16)

            def lane_rows(t, part_b):
                if part_b:
                    f = (t - TILES_A) * U
                    return [x_nat[bass.ds(f + h * (N // 2), U), P:N, :].rearrange("f l c -> l f c") for h in range(2)]
                return [x_nat[bass.ds(t * U, U), 64 * h:64 * h + 64, :].rearrange("f l c -> l f c") for h in range(2)]

            def lane_first_rows(t, part_b):
                if part_b:
                    f = (t - TILES_A) * U
                    return [x_nat[P:N, bass.ds(f + h * (N // 2), U), :] for h in range(2)]
                return [x_nat[64 * h:64 * h + 64, bass.ds(t * U, U), :] for h in range(2)]

            def halves(dram_tile):
                return [tokens(dram_tile[64 * h:64 * h + 64]) for h in range(2)]

            def x_source(l, t, part_b):
                if l == 0:
                    return halves(x_in[t])
                if l == 1:
                    return lane_rows(t, part_b)
                return halves(x_mid[l - 2][t])

            def x_target(l, t, part_b):
                if l == LAST:
                    return halves(out[t])
                if l == 0:
                    return lane_first_rows(t, part_b)
                return halves(x_mid[l - 1][t])

            def by_part(make_stages, natural):
                if not natural:
                    pipeline(sp, make_stages(False, 0))
                else:
                    pipeline(sp, make_stages(False, 0), TILES_A)
                    pipeline(sp, make_stages(True, TILES_A), TILES - TILES_A)

            for h in range(2):
                sp.dma_start(xin[64 * h:64 * h + 64, 0, :], x_in[0][64 * h:64 * h + 64]).then_inc(x_loaded[0], 16)
            sp.dma_start(wfold[:], weights).then_inc(s_params, 16)
            sp.dma_start(nrm[:], norms).then_inc(s_params, 16)
            sp.dma_start(wbias, biases.partition_broadcast(P)).then_inc(s_params, 16)
            sp.dma_start(mlp_wb[:], mlp_norm.partition_broadcast(P)).then_inc(s_params, 16)
            sp.dma_start(mask_sb[:], mask).then_inc(s_params, 16)
            sp.wait_ge(s_const, 1)
            sp.dma_start(wq_raw[:, 0:512], w1).then_inc(s_params, 16)
            sp.dma_start(wq_raw[0:C, 512:768], w2).then_inc(s_params, 16)

            def load_for_sums(t, b):
                if isinstance(t, int) and t == 0:
                    return
                wait_free(sp, shift_ready, t - 1)
                for h in range(2):
                    sp.dma_start(xin[64 * h:64 * h + 64, b, :], x_in[t][64 * h:64 * h + 64]).then_inc(x_loaded[b], 16)

            pipeline(sp, [(0, load_for_sums)])

            def load_x(l, t, b, part_b):
                wait_free(sp, x_centred, x_base(l) + t - 1)
                for h, src in enumerate(x_source(l, t, part_b)):
                    sp.dma_start(tokens(xin[64 * h:64 * h + 64, b, :]), src).then_inc(x_loaded[b], 16)

            def load_residual(l, q, t, b, part_b):
                wait_free(sp, xnew_ready, x_base(l) + t - 1)
                wait_free(sp, prod_ready, x_base(l) + t - 1)
                for h, src in enumerate(x_source(l, t, part_b)):
                    sp.dma_start(tokens(xres[64 * h:64 * h + 64, b, :]), src).then_inc(res_loaded[b], 16)
                sp.dma_start(gate[:, b, :], gate_dram[TILES * q + t]).then_inc(res_loaded[b], 16)

            def load_residual_mlp(l, t, b):
                wait_free(sp, xnew_ready, x_base(l) + t - 1)
                for h, src in enumerate(x_source(l, t, False)):
                    sp.dma_start(tokens(xres_m[64 * h:64 * h + 64, b, :]), src).then_inc(mres_loaded[b], 16)

            def store_x(l, t, b, part_b):
                sp.wait_ge(xnew_ready, x_base(l) + t + 1)
                for h, dst in enumerate(x_target(l, t, part_b)):
                    sp.dma_start(dst, tokens(xnew[64 * h:64 * h + 64, b, :])).then_inc(xnew_stored[b], 16)

            for l in range(layers):
                sp.wait_ge(shift_ready, TILES)
                if l:
                    for b in range(2):
                        sp.wait_ge(xnew_stored[b], 16 * x_base(l))
                if l in TRIANGLES:
                    q = TRIANGLES[l]

                    def input_stages(part_b, t0):
                        return [(0, lambda t, b: load_x(l, t + t0, b, part_b))]

                    by_part(input_stages, l == 1)
                    sp.wait_ge(pair_stored, PAIRS * TILES * (q + 1))

                    def stage_b(k, b):
                        wait_free(sp, chan_done, 2 * (BLOCKS * q + k - 1))
                        for side, dst in ((1, stat_b), (0, mov_b)):
                            for h in range(2):
                                sp.dma_start(dst[0:64, b, :, 96 * h:96 * h + 96],
                                             pairs[64 * h:64 * h + 64, side, bass.ds(k * BLK, BLK), N:COLS])\
                                    .then_inc(b_staged[b], 16)

                    pipeline(sp, [(0, stage_b)], BLOCKS)
                    sp.wait_ge(chan_done, 2 * BLOCKS * (q + 1))
                    for b in range(2):
                        sp.wait_ge(gate_stored[b], 8 * TILES * (q + 1))

                    def output_stages(part_b, t0):
                        return [(1, lambda t, b: load_residual(l, q, t + t0, b, part_b)),
                                (0, lambda t, b: store_x(l, t + t0, b, part_b))]

                    by_part(output_stages, l < 2)
                else:
                    pipeline(sp, [(0, lambda t, b: load_x(l, t, b, False))])
                    pipeline(sp, [(1, lambda t, b: load_residual_mlp(l, t, b)),
                                  (0, lambda t, b: store_x(l, t, b, False))])
            for b in range(2):
                sp.wait_ge(xnew_stored[b], 16 * x_base(layers))
                sp.wait_ge(gate_stored[b], 8 * TILES * tri_before[layers])

        @block.gpsimd
        def _(pool):
            pool.memset(wq_raw[:, 512:768], 0.0).then_inc(s_const, 1)
            pool.memset(ident[:], 0.0).then_inc(s_const, 1)
            pool.memset(ident16[:], 0.0).then_inc(s_const, 1)
            pool.memset(ones[:], 1.0).then_inc(s_const, 1)
            pool.memset(half_power[:], -0.5).then_inc(s_const, 1)
            pool.wait_ge(s_const, 5)
            for m in (ident, ident16):
                pool.affine_select(out=m[:], in_=m[:], compare_op=ALU.not_equal, fill=1.0, base=0,
                                   pattern=[[-1, P]], channel_multiplier=1).then_inc(s_const, 1)

            def shift(src, r, b):
                wait_free(pool, sums_ready, r - 1)
                pool.tensor_tensor(tokens(shifted[:, b, :]), tokens(src), over_tokens(anchor[:]), ALU.subtract)\
                    .then_inc(shift_ready, 1)

            def shift_input(t, b):
                pool.wait_ge(x_loaded[b], landed(32, t, b))
                shift(xin[:, b, :], t, b)

            pool.wait_ge(anchor_ready, 1)
            pipeline(pool, [(0, shift_input)])

            def group_rstd(l):
                pool.wait_ge(gn_var, l + 1)
                pool.tensor_tensor(gn_s[:, 6, :], gn_s[:, 5, :], half_power[:], ALU.pow).then_inc(gn_pow, 1)

            def scale(l, t, b):
                pool.wait_ge(x_centred, x_base(l) + t + 1)
                if isinstance(t, int) and t == 0:
                    pool.wait_ge(gn_ready, l + 1)
                wait_free(pool, xn_ready, ln_base(l, 0) + t - 1)
                pool.tensor_tensor(tokens(normed[:, b, :]), tokens(cent[:, b, :]), over_tokens(gn_rstd[:]), ALU.mult)\
                    .then_inc(x_scaled, 1)

            def token_rstd(l, side, t, b):
                n = ln_base(l, side) + t
                pool.wait_ge(var_ready, n + 1)
                wait_free(pool, xn_ready, n - 1)
                pool.tensor_tensor(ln_s[:, b, RSTD, :], ln_s[:, b, VAR, :], half_power[:, 0:U], ALU.pow)\
                    .then_inc(rstd_ready, 1)

            def update(l, res, upd, t, b):
                pool.wait_ge(prod_ready, x_base(l) + t + 1)
                wait_free(pool, xnew_stored[b], landed(32, x_base(l) + t - 2, b))
                pool.tensor_tensor(xnew[:, b, :], upd[:, b, :], res[:, b, :], ALU.add).then_inc(xnew_ready, 1)
                if l != LAST:
                    pool.wait_ge(xnew_ready, x_base(l) + t + 1)
                    shift(xnew[:, b, :], sum_base(l) + t, b)

            def h_bias(t, b):
                pool.wait_ge(hw_ready, t + 1)
                wait_free(pool, hs_ready, t - 1)
                pool.tensor_tensor(tokens(h_act[:, b, :]), tokens(h_pre[:, b, :]), over_tokens(mlp_wb[:, 1, :]), ALU.add)\
                    .then_inc(h_ready, 1)

            def h_round(t, b):
                pool.wait_ge(hadd_ready, t + 1)
                wait_free(pool, qT_psum, t - 1)
                pool.tensor_tensor(q_in[:, b, :], h_added[:, b, :], h_magic[:, b, :], ALU.subtract)\
                    .then_inc(hq_ready, 1)

            def hidden_round(t, b):
                pool.wait_ge(hid_added, t + 1)
                wait_free(pool, hqT_psum, 2 * (t - 1))
                pool.tensor_tensor(q_hid[:, b, :], added[:, b, :], magic[:, b, :], ALU.subtract).then_inc(hid_q, 1)

            for l in range(layers):
                group_rstd(l)
                if l in TRIANGLES:
                    pipeline(pool, [(3, lambda t, b: scale(l, t, b)),
                                    (2, lambda t, b: token_rstd(l, 0, t, b))])
                    pipeline(pool, [(2, lambda t, b: token_rstd(l, 1, t, b)),
                                    (0, lambda t, b: update(l, xres, prod, t, b))])
                else:
                    pipeline(pool, [(3, lambda t, b: scale(l, t, b)),
                                    (2, lambda t, b: token_rstd(l, 0, t, b)),
                                    (1, h_bias),
                                    (-1, h_round)])
                    pipeline(pool, [(-2, hidden_round),
                                    (-4, lambda t, b: update(l, xres_m, prod_m, t, b))])

        @block.vector
        def _(dve):
            dve.wait_ge(anchor_sum, 1)
            dve.tensor_reduce(gn_s[:, 7, :], ps[:, 0, :].rearrange("p (u g e) -> p g u e", u=U, e=2), AX.XY, ALU.add)\
                .then_inc(anchor_step, 1)
            dve.wait_ge(anchor_step, 1)
            dve.tensor_scalar(anchor[:].rearrange("p (g e) -> p g e", e=2),
                              gn_s[:, 7, :].unsqueeze(2).to_broadcast([P, GROUPS, 2]),
                              1.0 / (P * U * 2), None, ALU.mult).then_inc(anchor_ready, 1)

            dve.wait_ge(s_params, 16 * 7)
            dve.tensor_tensor(nrm_d[:], nrm[:, :, 1:4:2], nrm[:, :, 0:3:2], ALU.subtract).then_inc(s_fold, 1)
            for q in range(3):
                step = 4 * q + 1
                dve.wait_ge(s_fold, step)
                dve.tensor_scalar(fold_tmp[:, 0:PROJ], wfold[:, q, 0:PROJ], nrm_d[:, q, 0:1], None, ALU.mult)
                dve.tensor_scalar(fold_tmp[:, PROJ:], wfold[:, q, PROJ:], nrm_d[:, q, 1:2], None, ALU.mult).then_inc(s_fold, 1)
                dve.tensor_scalar(wfold[:, q, 0:PROJ], wfold[:, q, 0:PROJ], nrm[:, q, 0:1], None, ALU.mult)
                dve.tensor_scalar(wfold[:, q, PROJ:], wfold[:, q, PROJ:], nrm[:, q, 2:3], None, ALU.mult).then_inc(s_fold, 1)
                dve.wait_ge(s_fold_pe, q + 1)
                dve.tensor_tensor(fold_tmp, ps[:, 1, 0:PROJ + C], wbias[:, q, :], ALU.add).then_inc(s_fold, 1)
                dve.wait_ge(s_fold, step + 3)
                dve.scalar_tensor_tensor(out=wfold[:, q, :], in0=fold_tmp, scalar=1.0 / C, in1=wfold[:, q, :],
                                         op0=ALU.mult, op1=ALU.add).then_inc(s_fold, 1)

            def chain(ins, n):
                ins.then_inc(s_quant, 1)
                dve.wait_ge(s_quant, n)

            w1_rows = lambda ap: ap[:, 0:512].rearrange("p (k c) -> p k c", k=4)
            chain(dve.tensor_reduce(wscale[:, 0, 0:4], w1_rows(wq_raw)[:, :, 0:C], AX.X, ALU.max,
                                    apply_absolute_value=True), 1)
            chain(dve.tensor_reduce(wscale[:, 0, 4:5], wq_raw[:, 512:768], AX.X, ALU.max,
                                    apply_absolute_value=True), 2)
            chain(dve.tensor_scalar(wscale[:, 1, :], wscale[:, 0, :], 1e-12, 1.0 / FP8_MAX, ALU.max, ALU.mult), 3)
            chain(dve.reciprocal(wscale[:, 2, :], wscale[:, 1, :]), 4)

            def by_row_scale(dst, src, k):
                for j in range(4):
                    dve.tensor_scalar(dst[:, j * P:(j + 1) * P], src[:, j * P:(j + 1) * P], wscale[:, k, j:j + 1], None, ALU.mult)
                return dve.tensor_scalar(dst[:, 512:768], src[:, 512:768], wscale[:, k, 4:5], None, ALU.mult)

            chain(by_row_scale(wq_y, wq_raw, 2), 5)
            dve.wait_ge(s_quant_abs, 1)
            chain(dve.tensor_scalar(wq_magic, wq_magic, SUBNORMAL, None, ALU.max), 6)
            chain(dve.tensor_tensor(wq_added, wq_magic, wq_y, ALU.add), 7)
            chain(dve.tensor_tensor(wq_q, wq_added, wq_magic, ALU.subtract), 8)
            chain(by_row_scale(wq_y, wq_q, 1), 9)
            dve.wait_ge(s_quant_pe, 1)
            n = 9
            for bank, dst, width in ((2, w1s, 2 * HID), (3, w2s, 2 * C)):
                rest = w_rest[:, 0:width]
                n += 5
                chain(dve.tensor_copy(dst[:, 0, :], ps[:, bank, 0:width]), n - 4)
                chain(dve.tensor_tensor(rest, ps[:, bank, 0:width], dst[:, 0, :], ALU.subtract), n - 3)
                chain(dve.tensor_copy(dst[:, 1, :], rest), n - 2)
                chain(dve.tensor_tensor(rest, rest, dst[:, 1, :], ALU.subtract), n - 1)
                chain(dve.tensor_copy(dst[:, 2, :], rest), n)

            def group_norm(l):
                base = 5 * l

                def step(ins, k):
                    ins.then_inc(gn_step, 1)
                    dve.wait_ge(gn_step, base + k)

                dve.wait_ge(sums_ready, sum_base(l))
                dve.tensor_reduce(gn_s[:, 0, :], ps[:, SUM, :].rearrange("p (u g e) -> p g u e", u=U, e=2), AX.XY, ALU.add)
                step(dve.tensor_reduce(gn_s[:, 1, :], ps[:, SQ, :].rearrange("p (u g e) -> p g u e", u=U, e=2), AX.XY, ALU.add), 1)
                step(dve.tensor_scalar(gn_s[:, 2, :], gn_s[:, 0, :], 1.0 / GN_COUNT, None, ALU.mult), 2)
                step(dve.tensor_tensor(gn_s[:, 3, :], gn_s[:, 2, :], gn_s[:, 2, :], ALU.mult), 3)
                step(dve.scalar_tensor_tensor(out=gn_s[:, 4, :], in0=gn_s[:, 1, :], scalar=1.0 / GN_COUNT, in1=gn_s[:, 3, :],
                                              op0=ALU.mult, op1=ALU.subtract), 4)
                dve.tensor_scalar(gn_s[:, 5, :], gn_s[:, 4, :], 0.0, GN_EPS, ALU.max, ALU.add).then_inc(gn_var, 1)
                step(dve.tensor_tensor(gn_mean[:].rearrange("p (g e) -> p g e", e=2), anchor[:].rearrange("p (g e) -> p g e", e=2),
                                       gn_s[:, 2, :].unsqueeze(2).to_broadcast([P, GROUPS, 2]), ALU.add), 5)
                dve.wait_ge(gn_pow, l + 1)
                dve.tensor_copy(gn_rstd[:].rearrange("p (g e) -> p g e", e=2),
                                gn_s[:, 6, :].unsqueeze(2).to_broadcast([P, GROUPS, 2])).then_inc(gn_ready, 1)

            def centre(l, t, b):
                dve.wait_ge(x_loaded[b], landed(32, TILES + x_base(l) + t, b))
                wait_free(dve, x_scaled, x_base(l) + t - 1)
                dve.tensor_tensor(tokens(cent[:, b, :]), tokens(xin[:, b, :]), over_tokens(gn_mean[:]), ALU.subtract)\
                    .then_inc(x_centred, 1)

            def ln_source(side, t, b):
                if side == 0:
                    return lambda u: normed[:, b, u * C:(u + 1) * C]
                return lambda u: pairs[:, 0, :, bass.ds(t * U + u, 1)].rearrange("p c o -> p (c o)")

            def ln_stats(l, side, t, b):
                n = ln_base(l, side) + t
                src = ln_source(side, t, b)
                s = lambda k: ln_s[:, b, k, :]
                st = lambda k: stats[:, b, :, k]
                if side == 0:
                    dve.wait_ge(x_scaled, x_base(l) + t + 1)
                for u in range(U):
                    last = dve.bn_stats(stats[:, b, u, :], src(u))
                last.then_inc(ln_step, 1)
                dve.wait_ge(ln_step, 6 * n + 1)
                dve.tensor_tensor(s(SUM2), st(1), st(4), ALU.add)
                dve.tensor_tensor(s(DIFF), st(1), st(4), ALU.subtract)
                dve.tensor_tensor(s(M2), st(2), st(5), ALU.add).then_inc(ln_step, 1)
                dve.wait_ge(ln_step, 6 * n + 2)
                dve.tensor_tensor(s(DIFF2), s(DIFF), s(DIFF), ALU.mult).then_inc(ln_step, 1)
                dve.wait_ge(ln_step, 6 * n + 3)
                dve.scalar_tensor_tensor(out=s(V64), in0=s(DIFF2), scalar=C / 4.0, in1=s(M2),
                                         op0=ALU.mult, op1=ALU.add).then_inc(ln_step, 1)
                dve.wait_ge(ln_step, 6 * n + 4)
                dve.tensor_scalar(s(VAR), s(V64), 1.0 / C, LN_EPS, ALU.mult, ALU.add).then_inc(var_ready, 1)

            def normalise(l, side, t, b, dst, plus):
                n = ln_base(l, side) + t
                src = ln_source(side, t, b)
                dve.wait_ge(rstd_ready, n + 1)
                dve.scalar_tensor_tensor(out=ln_s[:, b, SHIFT, :], in0=ln_s[:, b, SUM2, :], scalar=-0.5,
                                         in1=ln_s[:, b, RSTD, :], op0=ALU.mult, op1=ALU.mult).then_inc(ln_step, 1)
                dve.wait_ge(ln_step, 6 * n + 5)
                dve.tensor_scalar(ln_s[:, b, SHIFT, :], ln_s[:, b, SHIFT, :], plus, None, ALU.add).then_inc(ln_step, 1)
                dve.wait_ge(ln_step, 6 * n + 6)
                if l in TRIANGLES:
                    wait_free(dve, xnT_psum, tr_base(l, side) + t - 1)
                for u in range(U):
                    last = dve.tensor_scalar(dst[:, b, u * C:(u + 1) * C], src(u), ln_s[:, b, RSTD, u:u + 1],
                                             ln_s[:, b, SHIFT, u:u + 1], ALU.mult, ALU.add)
                last.then_inc(xn_ready, 1)

            def store_pairs(l, t, b):
                q = TRIANGLES[l]
                dst = pairs[:].rearrange("p s c n -> p (s c) n")
                gates = sig[:, b, :].rearrange("p (u g) -> p u g", u=U)
                if l == 3:
                    dve.tensor_copy(mask_t[:, b, :], mask_sb[:, cols(t)]).then_inc(mask_ready, 1)
                    dve.wait_ge(mask_ready, t + 1)
                for pp in range(PAIRS):
                    k = PAIRS * (TILES * q + t) + pp
                    dve.wait_ge(sig_ready, k + 1)
                    bank = 2 * (pp % 2)
                    u = 2 * pp
                    if l == 3:
                        for h in range(2):
                            last = dve.scalar_tensor_tensor(
                                out=dst[:, :, bass.ds(t * U + (u + h), 1)].rearrange("p k o -> p (k o)"),
                                in0=ps[:, bank + h, 0:2 * C], scalar=mask_t[:, b, u + h:u + h + 1],
                                in1=gates[:, u + h, 0:2 * C], op0=ALU.mult, op1=ALU.mult)
                    else:
                        last = dve.tensor_tensor(dst[:, :, bass.ds(t * U + u, 2)].rearrange("p k u -> p u k"),
                                                 ps[:, bank:bank + 2, 0:2 * C], gates[:, u:u + 2, 0:2 * C], ALU.mult)
                    last.then_inc(pair_stored, 1)

            def stage_stationary(q, k, b):
                wait_free(dve, chan_done, 2 * (BLOCKS * q + k - 1))
                dve.tensor_copy(stat_a[:, b, :, :], pairs[:, 1, bass.ds(k * BLK, BLK), 0:N]).then_inc(stat_staged, 1)

            def move_products(q, k, b):
                dve.wait_ge(chan_done, 2 * (BLOCKS * q + k) + 2)
                dve.tensor_copy(pairs[:, 0, bass.ds(k * BLK + 2, 2), :], ps[:, 2:4, 0:COLS]).then_inc(z_dve, 1)

            def gated(l, t, b):
                q = TRIANGLES[l]
                dve.wait_ge(out_ready, TILES * q + t + 1)
                dve.wait_ge(res_loaded[b], landed(48, TILES * q + t, b))
                wait_free(dve, xnew_ready, x_base(l) + t - 1)
                dve.tensor_tensor(prod[:, b, :].rearrange("p (k h c) -> p h k c", h=2, c=C),
                                  ps[:, 2 * b:2 * b + 2, 0:PAIRS * C].rearrange("p h (k c) -> p h k c", c=C),
                                  gate[:, b, :].rearrange("p (k h c) -> p h k c", h=2, c=C), ALU.mult).then_inc(prod_ready, 1)

            def h_weight(t, b):
                dve.wait_ge(xn_ready, ln_base(2, 0) + t + 1)
                wait_free(dve, h_ready, t - 1)
                dve.tensor_tensor(tokens(h_pre[:, b, :]), tokens(h_norm[:, b, :]), over_tokens(mlp_wb[:, 0, :]), ALU.mult)\
                    .then_inc(hw_ready, 1)

            def row_scale(amax, scale_out, semaphore, n):
                dve.tensor_scalar(scale_out, amax, 1e-12, 1.0 / FP8_MAX, ALU.max, ALU.mult).then_inc(semaphore, 1)
                dve.wait_ge(semaphore, n + 1)

            def h_scale(t, b):
                n = 3 * t
                dve.wait_ge(h_ready, t + 1)
                dve.tensor_reduce(tok[:, 0, :], tokens(h_act[:, b, :]), AX.X, ALU.max, apply_absolute_value=True)\
                    .then_inc(h_step, 1)
                dve.wait_ge(h_step, n + 1)
                row_scale(tok[:, 0, :], tok[:, 1, :], h_step, n + 1)
                dve.tensor_copy(sx_all[:, bass.ds(t, 1), :].rearrange("p o u -> p (o u)"), tok[:, 1, :])
                dve.reciprocal(tok[:, 2, :], tok[:, 1, :]).then_inc(h_step, 1)
                dve.wait_ge(h_step, n + 3)
                dve.tensor_tensor(tokens(h_scaled[:, b, :]), tokens(h_act[:, b, :]), over_channels(tok[:, 2, :]), ALU.mult)\
                    .then_inc(hs_ready, 1)

            def h_add(t, b):
                dve.wait_ge(habs_ready, t + 1)
                dve.tensor_scalar(h_magic[:, b, :], h_magic[:, b, :], SUBNORMAL, None, ALU.max).then_inc(hadd_step, 1)
                dve.wait_ge(hadd_step, t + 1)
                wait_free(dve, hq_ready, t - 1)
                dve.tensor_tensor(h_added[:, b, :], h_magic[:, b, :], h_scaled[:, b, :], ALU.add).then_inc(hadd_ready, 1)

            def copy_q(t, b):
                if isinstance(t, int) and t == 0:
                    dve.wait_ge(qT_ready, TILES)
                wait_free(dve, acc_ready, PAIRS * (t - 1))
                dve.tensor_copy(qT[:, b, :], q_all[:, bass.ds(t, 1), :].rearrange("p o f -> p (o f)")).then_inc(q_copied, 1)

            def hidden_product(t, b):
                rows = hidden[:, b, :].rearrange("p (u f) -> p u f", f=HID)
                wait_free(dve, hid_scaled, t - 1)
                for pp in range(PAIRS):
                    dve.wait_ge(relu_ready, PAIRS * t + pp + 1)
                    bank = 2 * (pp % 2)
                    dve.tensor_tensor(rows[:, 2 * pp:2 * pp + 2, :], ps[:, bank:bank + 2, HID:2 * HID],
                                      relu_a[:, pp % 2, :].rearrange("p (u f) -> p u f", f=HID), ALU.mult).then_inc(acc_used, 1)
                dve.wait_ge(acc_used, PAIRS * (t + 1))
                n = 7 * t
                sx = sx_all[:, bass.ds(t, 1), :].rearrange("p o u -> p (o u)")

                def step(ins, k):
                    ins.then_inc(hid_step, 1)
                    dve.wait_ge(hid_step, n + k)

                step(dve.tensor_reduce(tok[:, 3, :], rows, AX.X, ALU.max, apply_absolute_value=True), 1)
                step(dve.tensor_tensor(tok[:, 4, :], sx, sx, ALU.mult), 2)
                step(dve.tensor_tensor(tok[:, 5, :], tok[:, 3, :], tok[:, 4, :], ALU.mult), 3)
                step(dve.tensor_scalar(tok[:, 6, :], tok[:, 5, :], 1e-12, 1.0 / FP8_MAX, ALU.max, ALU.mult), 4)
                step(dve.tensor_copy(sg_all[:, bass.ds(t, 1), :].rearrange("p o u -> p (o u)"), tok[:, 6, :]), 5)
                step(dve.reciprocal(tok[:, 7, :], tok[:, 6, :]), 6)
                step(dve.tensor_tensor(rescale[:, b, :], tok[:, 7, :], tok[:, 4, :], ALU.mult), 7)

            def hidden_add(t, b):
                dve.wait_ge(hid_abs, t + 1)
                dve.tensor_scalar(magic[:, b, :], magic[:, b, :], SUBNORMAL, None, ALU.max).then_inc(hid_max, 1)
                dve.wait_ge(hid_max, t + 1)
                wait_free(dve, hid_q, t - 1)
                dve.tensor_tensor(added[:, b, :], magic[:, b, :], scaled[:, b, :], ALU.add).then_inc(hid_added, 1)

            def mlp_update(l, t, b):
                dve.wait_ge(mlp_out_ready, t + 1)
                wait_free(dve, xnew_ready, x_base(l) + t - 1)
                dve.wait_ge(mres_loaded[b], landed(32, t, b))
                dve.tensor_tensor(tokens(prod_m[:, b, :]), tokens(ps[:, O_BANK, :]),
                                  sg_all[:, bass.ds(t, 1), :].rearrange("p o u -> p (o u)").unsqueeze(2).to_broadcast([P, U, C]),
                                  ALU.mult).then_inc(prod_ready, 1)

            for l in range(layers):
                group_norm(l)
                dve.wait_ge(gn_ready, l + 1)
                if l in TRIANGLES:
                    q = TRIANGLES[l]
                    pipeline(dve, [(1, lambda t, b: normalise(l, 0, t, b, xn, 1.0)),
                                   (3, lambda t, b: centre(l, t, b)),
                                   (2, lambda t, b: ln_stats(l, 0, t, b)),
                                   (0, lambda t, b: store_pairs(l, t, b))])
                    dve.wait_ge(pair_stored, PAIRS * TILES * (q + 1))
                    pipeline(dve, [(1, lambda k, b: stage_stationary(q, k, b)),
                                   (0, lambda k, b: move_products(q, k, b))], BLOCKS)
                    dve.wait_ge(z_act, BLOCKS * (q + 1))
                    dve.wait_ge(z_dve, BLOCKS * (q + 1))
                    pipeline(dve, [(1, lambda t, b: normalise(l, 1, t, b, xn, 1.0)),
                                   (2, lambda t, b: ln_stats(l, 1, t, b)),
                                   (0, lambda t, b: gated(l, t, b))])
                else:
                    pipeline(dve, [(1, lambda t, b: normalise(l, 0, t, b, h_norm, 0.0)),
                                   (1, h_weight),
                                   (3, lambda t, b: centre(l, t, b)),
                                   (2, lambda t, b: ln_stats(l, 0, t, b)),
                                   (-1, h_add),
                                   (0, h_scale)])
                    pipeline(dve, [(1, copy_q),
                                   (-4, lambda t, b: mlp_update(l, t, b)),
                                   (-2, hidden_add),
                                   (0, hidden_product)])

        @block.scalar
        def _(act):
            def square(r, b):
                act.wait_ge(shift_ready, r + 1)
                wait_free(act, sums_ready, r - 1)
                act.activation(squares[:, b, :], shifted[:, b, :], ACT.Square).then_inc(sq_ready, 1)

            def apart():
                act.sem_inc(s_apart, 1)

            act.wait_ge(s_quant, 5)
            act.activation(wq_magic, wq_y, ACT.Abs, scale=SPLIT).then_inc(s_quant_abs, 1)
            pipeline(act, [(0, lambda t, b: square(t, b))])

            def evacuate_xnT(m, t, b, free_sem, free_value):
                act.wait_ge(xnT_psum, m + 1)
                if not (isinstance(t, int) and t < 2):
                    wait_free(act, free_sem, free_value)
                act.activation(xnT[:, b, :], ps[:, T_BANK + b, :], ACT.Copy).then_inc(xnT_ready, 1)

            def gates(q, t, b):
                n = TILES * q + t
                wait_free(act, gate_stored[b], landed(16, n - 2, b))
                wait_free(act, pair_stored, PAIRS * (n - 1))
                for pp in range(PAIRS):
                    act.wait_ge(proj_ready, PAIRS * n + pp + 1)
                    bank = 2 * (pp % 2)
                    act.activation(sig[:, b, :].rearrange("p (u g) -> p u g", u=U)[:, 2 * pp:2 * pp + 2, :],
                                   ps[:, bank:bank + 2, 2 * C:PROJ], ACT.Sigmoid).then_inc(sig_ready, 1)

            def store_gate(q, t, b):
                act.wait_ge(sig_ready, PAIRS * (TILES * q + t + 1))
                act.dma_start(tokens(gate_dram[TILES * q + t]),
                             sig[:, b, :].rearrange("p (u g) -> p u g", u=U)[:, :, 2 * C:3 * C]).then_inc(gate_stored[b], 16)

            def stage_moving(q, k, b):
                wait_free(act, chan_done, 2 * (BLOCKS * q + k - 1))
                apart()
                act.activation(mov_a[:, b, :, :], pairs[:, 0, bass.ds(k * BLK, BLK), 0:N], ACT.Copy).then_inc(mov_staged, 1)

            def move_products(q, k, b):
                act.wait_ge(chan_done, 2 * (BLOCKS * q + k) + 1)
                apart()
                act.activation(pairs[:, 0, bass.ds(k * BLK, 2), :], ps[:, 0:2, 0:COLS], ACT.Copy).then_inc(z_act, 1)

            def h_abs(t, b):
                act.wait_ge(hs_ready, t + 1)
                wait_free(act, hq_ready, t - 1)
                act.activation(h_magic[:, b, :], h_scaled[:, b, :], ACT.Abs, scale=SPLIT).then_inc(habs_ready, 1)

            def evacuate_qT(t, b):
                act.wait_ge(qT_psum, t + 1)
                apart()
                act.activation(q_all[:, bass.ds(t, 1), :].rearrange("p o f -> p (o f)"),
                               ps[:, T_BANK + b, 0:ROW // 2].bitcast(BF16), ACT.Copy).then_inc(qT_ready, 1)

            def relu(t, b):
                for pp in range(PAIRS):
                    k = PAIRS * t + pp
                    act.wait_ge(acc_ready, k + 1)
                    wait_free(act, acc_used, k - 1)
                    bank = 2 * (pp % 2)
                    act.activation(relu_a[:, pp % 2, :].rearrange("p (u f) -> p u f", f=HID),
                                   ps[:, bank:bank + 2, 0:HID], ACT.Relu).then_inc(relu_ready, 1)

            def hidden_scale(t, b):
                act.wait_ge(hid_step, 7 * (t + 1))
                wait_free(act, hid_added, t - 1)
                for u in range(U):
                    last = act.activation(scaled[:, b, u * HID:(u + 1) * HID], hidden[:, b, u * HID:(u + 1) * HID],
                                          ACT.Copy, scale=rescale[:, b, u:u + 1])
                last.then_inc(hid_scaled, 1)
                act.wait_ge(hid_scaled, t + 1)
                wait_free(act, hid_q, t - 1)
                act.activation(magic[:, b, :], scaled[:, b, :], ACT.Abs, scale=SPLIT).then_inc(hid_abs, 1)

            def evacuate_hqT(t, b):
                for half in range(2):
                    act.wait_ge(hqT_psum, 2 * t + half + 1)
                    if half == 0:
                        wait_free(act, mlp_out_ready, t - 1)
                    act.activation(q_hidT[:, b, half * 1024:(half + 1) * 1024], ps[:, H_BANK, :].bitcast(BF16), ACT.Copy)\
                        .then_inc(hqT_ready, 1)

            for l in range(layers):
                if l in TRIANGLES:
                    q = TRIANGLES[l]
                    pipeline(act, [(1, lambda t, b: evacuate_xnT(tr_base(l, 0) + t, t, b, proj_ready, PAIRS * (TILES * q + t - 1))),
                                   (0, lambda t, b: gates(q, t, b)),
                                   (-1, lambda t, b: store_gate(q, t, b))])
                    act.wait_ge(pair_stored, PAIRS * TILES * (q + 1))
                    pipeline(act, [(1, lambda k, b: stage_moving(q, k, b)),
                                   (0, lambda k, b: move_products(q, k, b))], BLOCKS)
                    tail = [] if l == LAST else [(-1, lambda t, b: square(sum_base(l) + t, b))]
                    pipeline(act, [(1, lambda t, b: evacuate_xnT(tr_base(l, 1) + t, t, b, out_ready, TILES * q + t - 1))] + tail)
                else:
                    pipeline(act, [(0, h_abs), (-2, evacuate_qT)])
                    pipeline(act, [(0, relu), (-1, hidden_scale), (-3, evacuate_hqT),
                                   (-4, lambda t, b: square(sum_base(l) + t, b))])

        @block.tensor
        def _(pe):
            pe.wait_ge(s_const, 7)
            pe.wait_ge(x_loaded[0], 32)
            pe.matmul(ps[:, 0, :], ones[:], xin[:, 0, :], start=True, stop=True).then_inc(anchor_sum, 1)
            for q in range(3):
                pe.wait_ge(s_fold, 4 * q + 2)
                pe.matmul(ps[:, 1, 0:PROJ + C], ones[0:C, :], fold_tmp[0:C, :], start=True, stop=True).then_inc(s_fold_pe, 1)
            pe.wait_ge(s_quant, 9)
            for k in range(4):
                pe.transpose(ps[:, 2, k * P:(k + 1) * P], wq_y[:, k * P:(k + 1) * P], ident[:])
            for k in range(2):
                last = pe.transpose(ps[:, 3, k * C:(k + 1) * C], wq_y[0:C, 512 + k * P:512 + (k + 1) * P], ident[0:C, 0:C])
            last.then_inc(s_quant_pe, 1)

            def add_to_sums(t, r, b):
                pe.wait_ge(sq_ready, r + 1)
                first = isinstance(t, int) and t == 0
                end = isinstance(t, int) and t == TILES - 1
                pe.matmul(ps[:, SUM, :], ones[:], shifted[:, b, :], start=first, stop=end, skip_group_check=True)
                pe.matmul(ps[:, SQ, :], ones[:], squares[:, b, :], start=first, stop=end, skip_group_check=True)\
                    .then_inc(sums_ready, 1)

            pipeline(pe, [(0, lambda t, b: add_to_sums(t, t, b))])
            pe.wait_ge(s_fold, 13)

            def transpose_xn(l, side, t, b):
                m = tr_base(l, side) + t
                pe.wait_ge(xn_ready, ln_base(l, side) + t + 1)
                wait_free(pe, xnT_ready, m - 1)
                for k in range(PAIRS):
                    last = pe.transpose(ps[:, T_BANK + b, k * P:(k + 1) * P], xn[:, b, k * P:(k + 1) * P], ident[:])
                last.then_inc(xnT_psum, 1)

            def project(l, t, b):
                q = TRIANGLES[l]
                pe.wait_ge(xnT_ready, tr_base(l, 0) + t + 1)
                for pp in range(PAIRS):
                    k = PAIRS * (TILES * q + t) + pp
                    wait_free(pe, pair_stored, k - 1)
                    for h in range(2):
                        rows = slice(C * h, C * h + C)
                        last = pe.matmul(ps[:, 2 * (pp % 2) + h, 0:PROJ], xnT[rows, b, pp * P:(pp + 1) * P],
                                         wfold[rows, q, 0:PROJ], start=True, stop=True)
                    last.then_inc(proj_ready, 1)

            def multiply(q, k, b):
                n = BLOCKS * q + k
                pe.wait_ge(stat_staged, n + 1)
                pe.wait_ge(mov_staged, n + 1)
                pe.wait_ge(b_staged[b], landed(64, n, b))
                for c in range(BLK):
                    if c == 0:
                        wait_free(pe, z_act, n)
                    if c == 2:
                        wait_free(pe, z_dve, n)
                    sa, ma, s_b, m_b = stat_a[:, b, c, :], mov_a[:, b, c, :], stat_b[0:64, b, c, :], mov_b[0:64, b, c, :]
                    pe.matmul(ps[:, c, 0:N], sa[:, 0:P], ma, start=True, stop=False)
                    pe.matmul(ps[:, c, 0:N], s_b[:, 0:P], m_b, start=False, stop=True)
                    for h in range(2):
                        o, j = ps[64 * h:64 * h + 64, c, N:COLS], slice(96 * h, 96 * h + 96)
                        pe.matmul(o, sa[:, P:N], ma[:, j], start=True, stop=False)
                        last = pe.matmul(o, s_b[:, P:N], m_b[:, j], start=False, stop=True)
                    if c % 2:
                        last.then_inc(chan_done, 1)

            def project_out(l, t, b):
                q = TRIANGLES[l]
                pe.wait_ge(xnT_ready, tr_base(l, 1) + t + 1)
                wait_free(pe, prod_ready, x_base(l) + t - 1)
                for u in range(U):
                    h, k = u % 2, u // 2
                    rows = slice(C * h, C * h + C)
                    last = pe.matmul(ps[:, 2 * b + h, k * C:(k + 1) * C], xnT[rows, b, k * P:(k + 1) * P],
                                     wfold[rows, q, PROJ:PROJ + C], start=True, stop=True)
                last.then_inc(out_ready, 1)

            def transpose_q(t, b):
                pe.wait_ge(hq_ready, t + 1)
                wait_free(pe, qT_ready, t - 1)
                for k in range(PAIRS):
                    last = pe.transpose(ps[:, T_BANK + b, 0:ROW // 2].bitcast(BF16)[:, k * P:(k + 1) * P],
                                        q_in[:, b, k * P:(k + 1) * P], ident16[:])
                last.then_inc(qT_psum, 1)

            def hidden_layer(t, b):
                pe.wait_ge(q_copied, t + 1)
                for pp in range(PAIRS):
                    k = PAIRS * t + pp
                    wait_free(pe, acc_used, k - 1)
                    for h in range(2):
                        rows = slice(C * h, C * h + C)
                        for part_ in range(3):
                            last = pe.matmul(ps[:, 2 * (pp % 2) + h, :], qT[rows, b, pp * P:(pp + 1) * P],
                                             w1s[rows, part_, :], start=(part_ == 0), stop=(part_ == 2))
                    last.then_inc(acc_ready, 1)

            def transpose_hidden(t, b):
                pe.wait_ge(hid_q, t + 1)
                for half in range(2):
                    wait_free(pe, hqT_ready, 2 * t + half)
                    for k in range(8):
                        last = pe.transpose(ps[:, H_BANK, :].bitcast(BF16)[:, k * P:(k + 1) * P],
                                            q_hid[:, b, (8 * half + k) * P:(8 * half + k + 1) * P], ident16[:])
                    last.then_inc(hqT_psum, 1)

            def mlp_out(l, t, b):
                pe.wait_ge(hqT_ready, 2 * (t + 1))
                wait_free(pe, prod_ready, x_base(l) + t)
                for u in range(U):
                    for part_ in range(3):
                        for chunk in range(2):
                            last = pe.matmul(ps[:, O_BANK, u * C:(u + 1) * C], q_hidT[:, b, (2 * u + chunk) * P:(2 * u + chunk + 1) * P],
                                             w2s[:, part_, chunk * C:(chunk + 1) * C],
                                             start=(part_ == 0 and chunk == 0), stop=(part_ == 2 and chunk == 1))
                last.then_inc(mlp_out_ready, 1)

            for l in range(layers):
                if l in TRIANGLES:
                    q = TRIANGLES[l]
                    pipeline(pe, [(1, lambda t, b: transpose_xn(l, 0, t, b)),
                                  (0, lambda t, b: project(l, t, b))])
                    pipeline(pe, [(0, lambda k, b: multiply(q, k, b))], BLOCKS)
                    tail = [] if l == LAST else [(-1, lambda t, b: add_to_sums(t, sum_base(l) + t, b))]
                    pipeline(pe, [(1, lambda t, b: transpose_xn(l, 1, t, b)),
                                  (0, lambda t, b: project_out(l, t, b))] + tail)
                else:
                    pipeline(pe, [(-1, transpose_q)])
                    pipeline(pe, [(0, hidden_layer), (-3, transpose_hidden),
                                  (-3, lambda t, b: mlp_out(l, t, b)),
                                  (-4, lambda t, b: add_to_sums(t, sum_base(l) + t, b))])


def tiles_of(a):
    rest = a.shape[2:]
    part_a = a[:, :P].reshape(TILES_A, U, P, *rest).swapaxes(1, 2)
    part_b = a[:, P:].reshape(2, TILES - TILES_A, U, N - P, *rest)
    part_b = np.moveaxis(part_b, (0, 3), (1, 2)).reshape(TILES - TILES_A, P, U, *rest)
    return np.ascontiguousarray(np.concatenate([part_a, part_b]))


def image_of(tiles):
    part_a = tiles[:TILES_A].swapaxes(1, 2).reshape(N, P, C)
    part_b = tiles[TILES_A:].reshape(TILES - TILES_A, 2, N - P, U, C)
    part_b = np.moveaxis(part_b, (1, 2), (0, 3)).reshape(N, N - P, C)
    return np.ascontiguousarray(np.concatenate([part_a, part_b], axis=1))


def kernel(**inputs):
    import concourse.bacc as bacc
    from concourse.bass_utils import run_bass_kernel_spmd

    a = {k: np.asarray(v) for k, v in inputs.items()}
    zeros = np.zeros(C, np.float32)
    g = lambda l, names: [a[f"L{l}_conv_{n}"] for n in names.split()]
    w_l0 = [w.T for w in g(0, "left_w right_w lgate_w rgate_w ogate_w out_w")]
    proj = a["L1_conv_W_proj"]
    w_l1 = [proj[:, C:2 * C], proj[:, 3 * C:], proj[:, :C], proj[:, 2 * C:3 * C], *g(1, "W_gate W_ab")]
    w_l3 = g(3, "Wa Wb Wga Wgb Wgo Wo")
    w = np.stack([np.concatenate(x, 1) for x in (w_l0, w_l1, w_l3)], 1)
    b = [g(0, "left_b right_b lgate_b rgate_b ogate_b out_b"), [zeros] * 6, g(3, "ba bb bga bgb bgo bo")]
    n = [g(0, "norm_w norm_b ton_w ton_b"), g(1, "ln1_g ln1_b ln2_g ln2_b"), g(3, "norm_g norm_b norm_out_g norm_out_b")]
    norms = np.stack([np.stack(x, 1) for x in n], 1)
    w1 = a["L2_conv_w1"].reshape(4, P, 1, C)
    arrays = {
        "x_in": tiles_of(a["x"][0].swapaxes(0, 1)).reshape(TILES, P, ROW),
        "weights": np.concatenate([w, w]),
        "biases": np.stack([np.concatenate(x) for x in b]),
        "norms": np.concatenate([norms, norms]),
        "mask": tiles_of(a["L3_conv_mask"][0]).swapaxes(0, 1).reshape(P, COLS),
        "mlp_norm": np.stack(g(2, "ln_w ln_b")),
        "w1": np.concatenate([w1, w1], 2).swapaxes(0, 1).reshape(P, 4 * P),
        "w2": a["L2_conv_w2"],
    }
    arrays = {f"in_{k}": np.ascontiguousarray(v) for k, v in arrays.items()}
    nc = bacc.Bacc("TRN2", target_bir_lowering=False, num_devices=1)
    args = [nc.dram_tensor(k, v.shape, mybir.dt.from_np(v.dtype), kind="ExternalInput").ap() for k, v in arrays.items()]
    args.append(nc.dram_tensor("out_x", (TILES, P, ROW), F32, kind="ExternalOutput").ap())
    build(nc, *args)
    r = run_bass_kernel_spmd(nc, [arrays], core_ids=[0])
    return image_of(r.results[0]["out_x"].reshape(TILES, P, U, C))[None]
```

```python
from contextlib import ExitStack

import numpy as np

import concourse.bass as bass
from concourse import mybir

F32 = mybir.dt.float32
BF16 = mybir.dt.bfloat16
ALU = mybir.AluOpType
ACT = mybir.ActivationFunctionType
AX = mybir.AxisListType

P = 128
N = 192
C = 64
U = 8
ROW = U * C
TILES = N * N // (P * U)
TILES_A = N // U
COLS = TILES * U
GROUPS = C // 2
GN_COUNT = float(N * N * 2)
GN_EPS = 1e-5
LN_EPS = 1e-5
PAIRS = U // 2
HALF = U // 2
VALUES = 4 * C
GATES = 6 * C
PROJ = 5 * C
BLK = 4
BLOCKS = C // BLK
HID = 256
FP8_MAX = 448.0
SPLIT = float(2 ** 20)
SUBNORMAL = 1.5 * 2.0 ** 14
TRIANGLES = {0: 0, 1: 1, 3: 2}
LAST = 3
DVE_TOKENS = {(l, side): (2 if side or l == 2 else 4) for l in range(4) for side in range(2)}


def pipeline(eng, stages, n=TILES):
    leads = [s for s, _ in stages]
    first, start, end = -max(leads), 2 - min(leads), n - min(leads)
    turns = (n - max(leads) - start) // 2

    def peeled(i):
        for s, f in stages:
            if 0 <= i + s < n:
                f(i + s, (i + s) % 2)

    for i in range(first, start):
        peeled(i)
    with eng.Fori(start, start + 2 * turns - 1, 2) as i:
        for j in range(2):
            for s, f in stages:
                f(i + (j + s), (start + j + s) % 2)
    for i in range(start + 2 * turns, end):
        peeled(i)


def wait_free(eng, semaphore, value):
    if not (isinstance(value, int) and value <= 0):
        eng.wait_ge(semaphore, value)


def build(nc, x_in, weights, biases, norms, mask, mlp_norm, w1, w2, out, layers=4):
    with ExitStack() as ctx:
        def sb(name, shape, dt=F32):
            return ctx.enter_context(nc.sbuf_tensor(name, shape, dt))

        def sem(name):
            return ctx.enter_context(nc.semaphore(name))

        x_nat = nc.dram_tensor("x_nat", (N, N, C), F32, kind="Internal").ap()
        x_mid = [nc.dram_tensor(f"x_mid{i}", (TILES, P, ROW), F32, kind="Internal").ap() for i in range(2)]
        gate_dram = nc.dram_tensor("gate_dram", (3 * TILES, P, ROW), F32, kind="Internal").ap()

        pairs = sb("pairs", [P, 2, C, COLS])
        work = sb("work", [P, 11264])

        def part(buf, lo, n, bufs=2):
            return buf[:, lo:lo + n * bufs].rearrange("p (b f) -> p b f", b=bufs)

        xin, cent, normed, xn, xnT = (part(work, 1024 * k, ROW) for k in range(5))
        sig = part(work, 6144, U * 3 * C)
        wbias = work[:, 9216:9216 + 3 * (PROJ + C)].rearrange("p (q e) -> p q e", q=3)
        wpair = work[:, 9216:9216 + 2 * (PROJ + C)]
        stat_a, mov_a, stat_b, mov_b = (part(work, 2 * BLK * N * k, BLK * N).rearrange("p b (k n) -> p b k n", k=BLK)
                                        for k in range(4))
        xres, gate, prod = (part(work, 1024 * k, ROW) for k in range(3))
        xnew, shifted, squares = (part(work, 5120 + 1024 * k, ROW) for k in range(3))
        wide = pairs[:].rearrange("p a c n -> p (a c n)")
        h_norm, h_pre, h_act, h_scaled, h_magic, h_added = (part(wide, 1024 * k, ROW) for k in range(6))
        q_in = part(wide, 6144, ROW // 2).bitcast(BF16)
        hidden, scaled, magic, added = (part(wide, 4096 * k, U * HID) for k in range(4))
        q_hid = part(wide, 16384, U * HID // 2).bitcast(BF16)
        q_hidT = part(wide, 18432, U * HID // 2).bitcast(BF16)
        relu_a = part(wide, 20480, 2 * HID)
        q_all = wide[:, 21504:21504 + TILES * ROW // 2].bitcast(BF16).rearrange("p (t f) -> p t f", t=TILES)
        xres_m, prod_m = (part(wide, 30720 + 1024 * k, ROW) for k in range(2))
        qT = part(wide, 32768, ROW // 2).bitcast(BF16)
        wq_raw, wq_y, wq_magic, wq_added, wq_q = (wide[:, 768 * k:768 * (k + 1)] for k in range(5))
        w_rest = wide[:, 768 * 5:768 * 5 + 640]
        fold_tmp = wide[:, 8192:8192 + PROJ + C]

        ident = sb("ident", [P, P])
        ident16 = sb("ident16", [P, P], BF16)
        ones = sb("ones", [P, P])
        half_power = sb("half_power", [P, GROUPS])
        wfold = sb("wfold", [P, 3, PROJ + C])
        nrm = sb("nrm", [P, 3, 4])
        nrm_d = sb("nrm_d", [P, 3, 2])
        mlp_wb = sb("mlp_wb", [P, 2, C])
        mask_sb = sb("mask_sb", [P, COLS])
        mask_t = sb("mask_t", [P, 2, U])
        stats = sb("stats", [P, 2, U, 6])
        ln_s = sb("ln_s", [P, 2, 8, U])
        SUM2, DIFF, M2, DIFF2, V64, VAR, RSTD, SHIFT = range(8)
        tok = sb("tok", [P, 8, U])
        sx_all = sb("sx_all", [P, TILES, U])
        sg_all = sb("sg_all", [P, TILES, U])
        rescale = sb("rescale", [P, 2, U])
        wscale = sb("wscale", [P, 3, 5])
        anchor = sb("anchor", [P, C])
        gn_mean = sb("gn_mean", [P, C])
        gn_rstd = sb("gn_rstd", [P, C])
        gn_s = sb("gn_s", [P, 8, GROUPS])
        w1s = sb("w1s", [P, 3, 2 * HID], BF16)
        w2s = sb("w2s", [P, 3, 2 * C], BF16)

        ps = ctx.enter_context(nc.psum_tensor("ps", [P, 8, 512], F32))
        T_BANK, SUM, SQ = 4, 6, 7
        GATE_BANK = (2, 6)
        H_BANK, O_BANK = 4, 5

        (s_const,
         s_params,
         s_fold, s_fold_pe,
         s_quant, s_quant_abs, s_quant_pe,
         x_loaded,
         x_centred,
         x_scaled,
         ln_step,
         shift_step,
         var_ready,
         rstd_ready,
         xn_ready,
         xn_act,
         w_step,
         b_padded,
         xnT_psum,
         xnT_ready,
         gates_ready, proj_ready,
         sig_ready,
         pair_stored,
         gate_stored,
         mask_ready,
         stat_staged, mov_staged, b_staged,
         chan_done,
         z_act, z_dve,
         res_loaded,
         out_ready,
         prod_ready,
         xnew_ready,
         xnew_stored,
         shift_ready,
         sq_ready,
         sums_ready,
         gn_step, gn_var, gn_pow, gn_ready,
         anchor_sum, anchor_step, anchor_ready,
         hw_ready, h_ready, h_step,
         hs_ready, habs_ready, hadd_step, hadd_ready, hq_ready,
         qT_psum, qT_ready, q_copied,
         acc_ready, relu_ready, acc_used,
         hid_step, hid_scale, hid_scaled, hid_abs, hid_max, hid_added, hid_q,
         hqT_psum, hqT_ready,
         mlp_out_ready, mres_loaded,
         s_apart) = [sem(f"sem_{k}") for k in range(73)]

        x_loaded, gate_stored, b_staged, res_loaded, xnew_stored, mres_loaded = [
            (one, sem(f"sem_odd_{k}")) for k, one in enumerate((x_loaded, gate_stored, b_staged, res_loaded, xnew_stored, mres_loaded))]

        tri_before = {l: sum(k in TRIANGLES for k in range(l)) for l in range(5)}

        def x_base(l):
            return TILES * l

        def sum_base(l):
            return TILES * (l + 1)

        def ln_base(l, side):
            return TILES * (l + tri_before[l] + side)

        def tr_base(l, side):
            return TILES * (2 * TRIANGLES[l] + side)

        def landed(each, n, b):
            return (n - b) * (each // 2) + each

        def tokens(ap):
            return ap.rearrange("p (u c) -> p u c", c=C)

        def over_tokens(ap):
            return ap.unsqueeze(1).to_broadcast([P, U, C])

        def over_channels(ap):
            return ap.unsqueeze(2).to_broadcast([P, U, C])

        def cols(t):
            return bass.ds(t * U, U)

        block = ctx.enter_context(nc.Block())

        @block.sync
        def _(sp):
            def load_natural(dst, t, free0, signal):
                sp.dma_start(tokens(dst)[0:64], free0[0]).then_inc(signal, 16)
                sp.dma_start(tokens(dst)[64:P], free0[1]).then_inc(signal, 16)

            def lane_rows(t, part_b):
                if part_b:
                    f = (t - TILES_A) * U
                    return [x_nat[bass.ds(f + h * (N // 2), U), P:N, :].rearrange("f l c -> l f c") for h in range(2)]
                return [x_nat[bass.ds(t * U, U), 64 * h:64 * h + 64, :].rearrange("f l c -> l f c") for h in range(2)]

            def lane_first_rows(t, part_b):
                if part_b:
                    f = (t - TILES_A) * U
                    return [x_nat[P:N, bass.ds(f + h * (N // 2), U), :] for h in range(2)]
                return [x_nat[64 * h:64 * h + 64, bass.ds(t * U, U), :] for h in range(2)]

            def halves(dram_tile):
                return [tokens(dram_tile[64 * h:64 * h + 64]) for h in range(2)]

            def x_source(l, t, part_b):
                if l == 0:
                    return halves(x_in[t])
                if l == 1:
                    return lane_rows(t, part_b)
                return halves(x_mid[l - 2][t])

            def x_target(l, t, part_b):
                if l == LAST:
                    return halves(out[t])
                if l == 0:
                    return lane_first_rows(t, part_b)
                return halves(x_mid[l - 1][t])

            def by_part(make_stages, natural):
                if not natural:
                    pipeline(sp, make_stages(False, 0))
                else:
                    pipeline(sp, make_stages(False, 0), TILES_A)
                    pipeline(sp, make_stages(True, TILES_A), TILES - TILES_A)

            for h in range(2):
                sp.dma_start(xin[64 * h:64 * h + 64, 0, :], x_in[0][64 * h:64 * h + 64]).then_inc(x_loaded[0], 16)
            sp.dma_start(wfold[:], weights).then_inc(s_params, 16)
            sp.dma_start(nrm[:], norms).then_inc(s_params, 16)
            sp.dma_start(wbias, biases.partition_broadcast(P)).then_inc(s_params, 16)
            sp.dma_start(mlp_wb[:], mlp_norm.partition_broadcast(P)).then_inc(s_params, 16)
            sp.dma_start(mask_sb[:], mask).then_inc(s_params, 16)
            sp.wait_ge(s_const, 1)
            sp.dma_start(wq_raw[:, 0:512], w1).then_inc(s_params, 16)
            sp.dma_start(wq_raw[0:C, 512:768], w2).then_inc(s_params, 16)

            def load_for_sums(t, b):
                if isinstance(t, int) and t == 0:
                    return
                wait_free(sp, shift_ready, t - 1)
                for h in range(2):
                    sp.dma_start(xin[64 * h:64 * h + 64, b, :], x_in[t][64 * h:64 * h + 64]).then_inc(x_loaded[b], 16)

            pipeline(sp, [(0, load_for_sums)])

            def load_x(l, t, b, part_b):
                wait_free(sp, x_centred, x_base(l) + t - 1)
                for h, src in enumerate(x_source(l, t, part_b)):
                    sp.dma_start(tokens(xin[64 * h:64 * h + 64, b, :]), src).then_inc(x_loaded[b], 16)

            def load_residual(l, q, t, b, part_b):
                wait_free(sp, xnew_ready, x_base(l) + t - 1)
                wait_free(sp, prod_ready, x_base(l) + t - 1)
                for h, src in enumerate(x_source(l, t, part_b)):
                    sp.dma_start(tokens(xres[64 * h:64 * h + 64, b, :]), src).then_inc(res_loaded[b], 16)
                sp.dma_start(gate[:, b, :], gate_dram[TILES * q + t]).then_inc(res_loaded[b], 16)

            def load_residual_mlp(l, t, b):
                wait_free(sp, xnew_ready, x_base(l) + t - 1)
                for h, src in enumerate(x_source(l, t, False)):
                    sp.dma_start(tokens(xres_m[64 * h:64 * h + 64, b, :]), src).then_inc(mres_loaded[b], 16)

            def store_x(l, t, b, part_b):
                sp.wait_ge(xnew_ready, x_base(l) + t + 1)
                for h, dst in enumerate(x_target(l, t, part_b)):
                    sp.dma_start(dst, tokens(xnew[64 * h:64 * h + 64, b, :])).then_inc(xnew_stored[b], 16)

            for l in range(layers):
                sp.wait_ge(shift_ready, TILES)
                if l:
                    for b in range(2):
                        sp.wait_ge(xnew_stored[b], 16 * x_base(l))
                if l in TRIANGLES:
                    q = TRIANGLES[l]

                    def input_stages(part_b, t0):
                        return [(0, lambda t, b: load_x(l, t + t0, b, part_b))]

                    by_part(input_stages, l == 1)
                    sp.wait_ge(pair_stored, 2 * TILES * (q + 1))

                    def stage_b(k, b):
                        wait_free(sp, chan_done, 2 * (BLOCKS * q + k - 1))
                        for side, dst in ((1, stat_b), (0, mov_b)):
                            for h in range(2):
                                sp.dma_start(dst[0:64, b, :, 96 * h:96 * h + 96],
                                             pairs[64 * h:64 * h + 64, side, bass.ds(k * BLK, BLK), N:COLS])\
                                    .then_inc(b_staged[b], 16)

                    pipeline(sp, [(0, stage_b)], BLOCKS)
                    sp.wait_ge(chan_done, 2 * BLOCKS * (q + 1))
                    for b in range(2):
                        sp.wait_ge(gate_stored[b], 8 * TILES * (q + 1))

                    def output_stages(part_b, t0):
                        return [(1, lambda t, b: load_residual(l, q, t + t0, b, part_b)),
                                (0, lambda t, b: store_x(l, t + t0, b, part_b))]

                    by_part(output_stages, l < 2)
                else:
                    pipeline(sp, [(0, lambda t, b: load_x(l, t, b, False))])
                    pipeline(sp, [(1, lambda t, b: load_residual_mlp(l, t, b)),
                                  (0, lambda t, b: store_x(l, t, b, False))])
            for b in range(2):
                sp.wait_ge(xnew_stored[b], 16 * x_base(layers))
                sp.wait_ge(gate_stored[b], 8 * TILES * tri_before[layers])

        @block.gpsimd
        def _(pool):
            pool.memset(wq_raw[:, 512:768], 0.0).then_inc(s_const, 1)
            pool.memset(ident[:], 0.0).then_inc(s_const, 1)
            pool.memset(ident16[:], 0.0).then_inc(s_const, 1)
            pool.memset(ones[:], 1.0).then_inc(s_const, 1)
            pool.memset(half_power[:], -0.5).then_inc(s_const, 1)
            pool.wait_ge(s_const, 5)
            for m in (ident, ident16):
                pool.affine_select(out=m[:], in_=m[:], compare_op=ALU.not_equal, fill=1.0, base=0,
                                   pattern=[[-1, P]], channel_multiplier=1).then_inc(s_const, 1)

            def shift(src, r, b):
                wait_free(pool, sums_ready, r - 1)
                pool.tensor_tensor(tokens(shifted[:, b, :]), tokens(src), over_tokens(anchor[:]), ALU.subtract)\
                    .then_inc(shift_ready, 1)

            def shift_input(t, b):
                pool.wait_ge(x_loaded[b], landed(32, t, b))
                shift(xin[:, b, :], t, b)

            pool.wait_ge(anchor_ready, 1)
            pipeline(pool, [(0, shift_input)])

            def group_rstd(l):
                pool.wait_ge(gn_var, l + 1)
                pool.tensor_tensor(gn_s[:, 6, :], gn_s[:, 5, :], half_power[:], ALU.pow).then_inc(gn_pow, 1)

            def centre(l, t, b):
                pool.wait_ge(x_loaded[b], landed(32, TILES + x_base(l) + t, b))
                if isinstance(t, int) and t == 0:
                    pool.wait_ge(gn_ready, l + 1)
                wait_free(pool, x_scaled, x_base(l) + t - 1)
                pool.tensor_tensor(tokens(cent[:, b, :]), tokens(xin[:, b, :]), over_tokens(gn_mean[:]), ALU.subtract)\
                    .then_inc(x_centred, 1)

            def scale(l, t, b):
                pool.wait_ge(x_centred, x_base(l) + t + 1)
                if isinstance(t, int) and t == 0:
                    pool.wait_ge(gn_ready, l + 1)
                wait_free(pool, xn_ready, ln_base(l, 0) + t - 1)
                wait_free(pool, xn_act, ln_base(l, 0) + t - 1)
                pool.tensor_tensor(tokens(normed[:, b, :]), tokens(cent[:, b, :]), over_tokens(gn_rstd[:]), ALU.mult)\
                    .then_inc(x_scaled, 1)

            def token_rstd(l, side, t, b):
                n = ln_base(l, side) + t
                pool.wait_ge(var_ready, n + 1)
                wait_free(pool, xn_ready, n - 1)
                wait_free(pool, xn_act, n - 1)
                pool.tensor_tensor(ln_s[:, b, RSTD, :], ln_s[:, b, VAR, :], half_power[:, 0:U], ALU.pow)\
                    .then_inc(rstd_ready, 1)

            def update_mlp(l, t, b):
                pool.wait_ge(prod_ready, x_base(l) + t + 1)
                wait_free(pool, xnew_stored[b], landed(32, x_base(l) + t - 2, b))
                pool.tensor_tensor(xnew[:, b, :], prod_m[:, b, :], xres_m[:, b, :], ALU.add).then_inc(xnew_ready, 1)

            def shift_new(l, t, b):
                pool.wait_ge(xnew_ready, x_base(l) + t + 1)
                shift(xnew[:, b, :], sum_base(l) + t, b)

            def pad_operands(q):
                pool.wait_ge(pair_stored, 2 * TILES * (q + 1))
                pool.memset(stat_b[64:P], 0.0).then_inc(b_padded, 1)
                pool.memset(mov_b[64:P], 0.0).then_inc(b_padded, 1)

            def h_bias(t, b):
                pool.wait_ge(hw_ready, t + 1)
                wait_free(pool, hs_ready, t - 1)
                pool.tensor_tensor(tokens(h_act[:, b, :]), tokens(h_pre[:, b, :]), over_tokens(mlp_wb[:, 1, :]), ALU.add)\
                    .then_inc(h_ready, 1)

            def h_round(t, b):
                pool.wait_ge(hadd_ready, t + 1)
                wait_free(pool, qT_psum, t - 1)
                pool.tensor_tensor(q_in[:, b, :], h_added[:, b, :], h_magic[:, b, :], ALU.subtract)\
                    .then_inc(hq_ready, 1)

            def hidden_round(t, b):
                pool.wait_ge(hid_added, t + 1)
                wait_free(pool, hqT_psum, 2 * (t - 1))
                pool.tensor_tensor(q_hid[:, b, :], added[:, b, :], magic[:, b, :], ALU.subtract).then_inc(hid_q, 1)

            for l in range(layers):
                group_rstd(l)
                if l in TRIANGLES:
                    pipeline(pool, [(5, lambda t, b: centre(l, t, b)),
                                    (3, lambda t, b: token_rstd(l, 0, t, b)),
                                    (4, lambda t, b: scale(l, t, b))])
                    pad_operands(TRIANGLES[l])
                    tail = [] if l == LAST else [(0, lambda t, b: shift_new(l, t, b))]
                    pipeline(pool, [(3, lambda t, b: token_rstd(l, 1, t, b))] + tail)
                else:
                    pipeline(pool, [(3, lambda t, b: scale(l, t, b)),
                                    (2, lambda t, b: token_rstd(l, 0, t, b)),
                                    (1, h_bias),
                                    (-1, h_round)])
                    pipeline(pool, [(-2, hidden_round),
                                    (-4, lambda t, b: update_mlp(l, t, b)),
                                    (-4, lambda t, b: shift_new(l, t, b))])

        @block.vector
        def _(dve):
            dve.wait_ge(anchor_sum, 1)
            dve.tensor_reduce(gn_s[:, 7, :], ps[:, 0, :].rearrange("p (u g e) -> p g u e", u=U, e=2), AX.XY, ALU.add)\
                .then_inc(anchor_step, 1)
            dve.wait_ge(anchor_step, 1)
            dve.tensor_scalar(anchor[:].rearrange("p (g e) -> p g e", e=2),
                              gn_s[:, 7, :].unsqueeze(2).to_broadcast([P, GROUPS, 2]),
                              1.0 / (P * U * 2), None, ALU.mult).then_inc(anchor_ready, 1)

            dve.wait_ge(s_params, 16 * 7)
            dve.tensor_tensor(nrm_d[:], nrm[:, :, 1:4:2], nrm[:, :, 0:3:2], ALU.subtract).then_inc(s_fold, 1)
            for q in range(3):
                step = 4 * q + 1
                dve.wait_ge(s_fold, step)
                dve.tensor_scalar(fold_tmp[:, 0:PROJ], wfold[:, q, 0:PROJ], nrm_d[:, q, 0:1], None, ALU.mult)
                dve.tensor_scalar(fold_tmp[:, PROJ:], wfold[:, q, PROJ:], nrm_d[:, q, 1:2], None, ALU.mult).then_inc(s_fold, 1)
                dve.tensor_scalar(wfold[:, q, 0:PROJ], wfold[:, q, 0:PROJ], nrm[:, q, 0:1], None, ALU.mult)
                dve.tensor_scalar(wfold[:, q, PROJ:], wfold[:, q, PROJ:], nrm[:, q, 2:3], None, ALU.mult).then_inc(s_fold, 1)
                dve.wait_ge(s_fold_pe, q + 1)
                dve.tensor_tensor(fold_tmp, ps[:, 1, 0:PROJ + C], wbias[:, q, :], ALU.add).then_inc(s_fold, 1)
                dve.wait_ge(s_fold, step + 3)
                dve.scalar_tensor_tensor(out=wfold[:, q, :], in0=fold_tmp, scalar=1.0 / C, in1=wfold[:, q, :],
                                         op0=ALU.mult, op1=ALU.add).then_inc(s_fold, 1)

            def chain(ins, n):
                ins.then_inc(s_quant, 1)
                dve.wait_ge(s_quant, n)

            w1_rows = lambda ap: ap[:, 0:512].rearrange("p (k c) -> p k c", k=4)
            chain(dve.tensor_reduce(wscale[:, 0, 0:4], w1_rows(wq_raw)[:, :, 0:C], AX.X, ALU.max,
                                    apply_absolute_value=True), 1)
            chain(dve.tensor_reduce(wscale[:, 0, 4:5], wq_raw[:, 512:768], AX.X, ALU.max,
                                    apply_absolute_value=True), 2)
            chain(dve.tensor_scalar(wscale[:, 1, :], wscale[:, 0, :], 1e-12, 1.0 / FP8_MAX, ALU.max, ALU.mult), 3)
            chain(dve.reciprocal(wscale[:, 2, :], wscale[:, 1, :]), 4)

            def by_row_scale(dst, src, k):
                for j in range(4):
                    dve.tensor_scalar(dst[:, j * P:(j + 1) * P], src[:, j * P:(j + 1) * P], wscale[:, k, j:j + 1], None, ALU.mult)
                return dve.tensor_scalar(dst[:, 512:768], src[:, 512:768], wscale[:, k, 4:5], None, ALU.mult)

            chain(by_row_scale(wq_y, wq_raw, 2), 5)
            dve.wait_ge(s_quant_abs, 1)
            chain(dve.tensor_scalar(wq_magic, wq_magic, SUBNORMAL, None, ALU.max), 6)
            chain(dve.tensor_tensor(wq_added, wq_magic, wq_y, ALU.add), 7)
            chain(dve.tensor_tensor(wq_q, wq_added, wq_magic, ALU.subtract), 8)
            chain(by_row_scale(wq_y, wq_q, 1), 9)
            dve.wait_ge(s_quant_pe, 1)
            n = 9
            for bank, dst, width in ((2, w1s, 2 * HID), (3, w2s, 2 * C)):
                rest = w_rest[:, 0:width]
                n += 5
                chain(dve.tensor_copy(dst[:, 0, :], ps[:, bank, 0:width]), n - 4)
                chain(dve.tensor_tensor(rest, ps[:, bank, 0:width], dst[:, 0, :], ALU.subtract), n - 3)
                chain(dve.tensor_copy(dst[:, 1, :], rest), n - 2)
                chain(dve.tensor_tensor(rest, rest, dst[:, 1, :], ALU.subtract), n - 1)
                chain(dve.tensor_copy(dst[:, 2, :], rest), n)

            def group_norm(l):
                base = 5 * l

                def step(ins, k):
                    ins.then_inc(gn_step, 1)
                    dve.wait_ge(gn_step, base + k)

                dve.wait_ge(sums_ready, sum_base(l))
                dve.tensor_reduce(gn_s[:, 0, :], ps[:, SUM, :].rearrange("p (u g e) -> p g u e", u=U, e=2), AX.XY, ALU.add)
                step(dve.tensor_reduce(gn_s[:, 1, :], ps[:, SQ, :].rearrange("p (u g e) -> p g u e", u=U, e=2), AX.XY, ALU.add), 1)
                step(dve.tensor_scalar(gn_s[:, 2, :], gn_s[:, 0, :], 1.0 / GN_COUNT, None, ALU.mult), 2)
                step(dve.tensor_tensor(gn_s[:, 3, :], gn_s[:, 2, :], gn_s[:, 2, :], ALU.mult), 3)
                step(dve.scalar_tensor_tensor(out=gn_s[:, 4, :], in0=gn_s[:, 1, :], scalar=1.0 / GN_COUNT, in1=gn_s[:, 3, :],
                                              op0=ALU.mult, op1=ALU.subtract), 4)
                dve.tensor_scalar(gn_s[:, 5, :], gn_s[:, 4, :], 0.0, GN_EPS, ALU.max, ALU.add).then_inc(gn_var, 1)
                step(dve.tensor_tensor(gn_mean[:].rearrange("p (g e) -> p g e", e=2), anchor[:].rearrange("p (g e) -> p g e", e=2),
                                       gn_s[:, 2, :].unsqueeze(2).to_broadcast([P, GROUPS, 2]), ALU.add), 5)
                dve.wait_ge(gn_pow, l + 1)
                dve.tensor_copy(gn_rstd[:].rearrange("p (g e) -> p g e", e=2),
                                gn_s[:, 6, :].unsqueeze(2).to_broadcast([P, GROUPS, 2])).then_inc(gn_ready, 1)

            def centre(l, t, b):
                dve.wait_ge(x_loaded[b], landed(32, TILES + x_base(l) + t, b))
                wait_free(dve, x_scaled, x_base(l) + t - 1)
                dve.tensor_tensor(tokens(cent[:, b, :]), tokens(xin[:, b, :]), over_tokens(gn_mean[:]), ALU.subtract)\
                    .then_inc(x_centred, 1)

            def ln_source(side, t, b):
                if side == 0:
                    return lambda u: normed[:, b, u * C:(u + 1) * C]
                return lambda u: pairs[:, 0, :, bass.ds(t * U + u, 1)].rearrange("p c o -> p (c o)")

            def pair_weights(q):
                if q == 0:
                    dve.wait_ge(s_fold, 13)
                    dve.memset(wpair, 0.0).then_inc(w_step, 1)
                    dve.wait_ge(w_step, 1)
                for h in range(2):
                    rows = slice(C * h, C * h + C)
                    for lo, src, width in ((0, 0, VALUES // 2), (VALUES, 2 * C, GATES // 2), (2 * PROJ, PROJ, C)):
                        last = dve.tensor_copy(wpair[rows, lo + h * width:lo + (h + 1) * width], wfold[rows, q, src:src + width])
                last.then_inc(w_step, 1)

            def ln_moments(l, side, t, b):
                src = ln_source(side, t, b)
                if side == 0:
                    dve.wait_ge(x_scaled, x_base(l) + t + 1)
                for u in range(U):
                    last = dve.bn_stats(stats[:, b, u, :], src(u))
                last.then_inc(ln_step, 1)

            def small(b, k):
                return ln_s[:, b, k, :]

            def ln_combine(l, side, t, b):
                st = lambda k: stats[:, b, :, k]
                dve.wait_ge(ln_step, 4 * (ln_base(l, side) + t) + 1)
                wait_free(dve, xn_act, ln_base(l, side) + t - 1)
                dve.tensor_tensor(small(b, SUM2), st(1), st(4), ALU.add)
                dve.tensor_tensor(small(b, DIFF), st(1), st(4), ALU.subtract)
                dve.tensor_tensor(small(b, M2), st(2), st(5), ALU.add).then_inc(ln_step, 1)

            def ln_diff2(l, side, t, b):
                dve.wait_ge(ln_step, 4 * (ln_base(l, side) + t) + 2)
                dve.tensor_tensor(small(b, DIFF2), small(b, DIFF), small(b, DIFF), ALU.mult).then_inc(ln_step, 1)

            def ln_v64(l, side, t, b):
                dve.wait_ge(ln_step, 4 * (ln_base(l, side) + t) + 3)
                dve.scalar_tensor_tensor(out=small(b, V64), in0=small(b, DIFF2), scalar=C / 4.0, in1=small(b, M2),
                                         op0=ALU.mult, op1=ALU.add).then_inc(ln_step, 1)

            def ln_var(l, side, t, b):
                dve.wait_ge(ln_step, 4 * (ln_base(l, side) + t) + 4)
                dve.tensor_scalar(small(b, VAR), small(b, V64), 1.0 / C, LN_EPS, ALU.mult, ALU.add).then_inc(var_ready, 1)

            def ln_shift(l, side, t, b):
                n = ln_base(l, side) + t
                dve.wait_ge(rstd_ready, n + 1)
                wait_free(dve, xn_act, n - 1)
                dve.scalar_tensor_tensor(out=small(b, SHIFT), in0=small(b, SUM2), scalar=-0.5, in1=small(b, RSTD),
                                         op0=ALU.mult, op1=ALU.mult).then_inc(shift_step, 1)

            def ln_plus(l, side, plus, t, b):
                n = ln_base(l, side) + t
                dve.wait_ge(shift_step, 2 * n + 1)
                dve.tensor_scalar(small(b, SHIFT), small(b, SHIFT), plus, None, ALU.add).then_inc(shift_step, 1)

            def normalise(l, side, dst, t, b):
                n = ln_base(l, side) + t
                src = ln_source(side, t, b)
                dve.wait_ge(shift_step, 2 * n + 2)
                if l in TRIANGLES:
                    wait_free(dve, xnT_psum, tr_base(l, side) + t - 1)
                for u in range(DVE_TOKENS[l, side]):
                    last = dve.tensor_scalar(dst[:, b, u * C:(u + 1) * C], src(u), small(b, RSTD)[:, u:u + 1],
                                             small(b, SHIFT)[:, u:u + 1], ALU.mult, ALU.add)
                last.then_inc(xn_ready, 1)

            def layer_norm(l, side, dst, plus, lead, big=()):
                big = list(big)
                at = lambda f: lambda t, b: f(l, side, t, b)
                return [(lead + 1, at(ln_moments)), (lead, at(ln_shift)), (lead + 1, at(ln_combine)),
                        (lead, lambda t, b: ln_plus(l, side, plus, t, b)), (lead + 1, at(ln_diff2)),
                        (lead, lambda t, b: normalise(l, side, dst, t, b)), (lead + 1, at(ln_v64)),
                        *big[:1], (lead + 1, at(ln_var)), *big[1:]]

            def store_pairs(l, half, t, b):
                q = TRIANGLES[l]
                k = 2 * (TILES * q + t) + half
                dst = pairs[:].rearrange("p s c n -> p (s c) n")
                gates = sig[:, b, :].rearrange("p (u g) -> p u g", u=U)
                values = ps[:, half, :].rearrange("p (u k) -> p u k", u=HALF)
                u0 = HALF * half
                if l == 3 and half == 0:
                    dve.tensor_copy(mask_t[:, b, :], mask_sb[:, cols(t)]).then_inc(mask_ready, 1)
                    dve.wait_ge(mask_ready, t + 1)
                dve.wait_ge(proj_ready, k + 1)
                dve.wait_ge(sig_ready, k + 1)
                if l == 3:
                    for u in range(HALF):
                        last = dve.scalar_tensor_tensor(
                            out=dst[:, :, bass.ds(t * U + (u0 + u), 1)].rearrange("p k o -> p (k o)"),
                            in0=values[:, u, :], scalar=mask_t[:, b, u0 + u:u0 + u + 1],
                            in1=gates[:, u0 + u, 0:2 * C], op0=ALU.mult, op1=ALU.mult)
                else:
                    last = dve.tensor_tensor(dst[:, :, bass.ds(t * U + u0, HALF)].rearrange("p k u -> p u k"),
                                             values, gates[:, u0:u0 + HALF, 0:2 * C], ALU.mult)
                last.then_inc(pair_stored, 1)

            def stage_stationary(q, k, b):
                wait_free(dve, chan_done, 2 * (BLOCKS * q + k - 1))
                dve.tensor_copy(stat_a[:, b, :, :], pairs[:, 1, bass.ds(k * BLK, BLK), 0:N]).then_inc(stat_staged, 1)

            def move_products(q, k, b):
                dve.wait_ge(chan_done, 2 * (BLOCKS * q + k) + 2)
                dve.tensor_copy(pairs[:, 0, bass.ds(k * BLK + 2, 2), :], ps[:, 2:4, 0:COLS]).then_inc(z_dve, 1)

            def gated(l, t, b):
                q = TRIANGLES[l]
                dve.wait_ge(out_ready, TILES * q + t + 1)
                dve.wait_ge(res_loaded[b], landed(48, TILES * q + t, b))
                wait_free(dve, xnew_ready, x_base(l) + t - 1)
                dve.tensor_tensor(prod[:, b, :], ps[:, b, :], gate[:, b, :], ALU.mult).then_inc(prod_ready, 1)

            def update(l, t, b):
                dve.wait_ge(prod_ready, x_base(l) + t + 1)
                wait_free(dve, xnew_stored[b], landed(32, x_base(l) + t - 2, b))
                if l != LAST:
                    wait_free(dve, shift_ready, sum_base(l) + t - 1)
                dve.tensor_tensor(xnew[:, b, :], prod[:, b, :], xres[:, b, :], ALU.add).then_inc(xnew_ready, 1)

            def h_weight(t, b):
                dve.wait_ge(xn_ready, ln_base(2, 0) + t + 1)
                dve.wait_ge(xn_act, ln_base(2, 0) + t + 1)
                wait_free(dve, h_ready, t - 1)
                dve.tensor_tensor(tokens(h_pre[:, b, :]), tokens(h_norm[:, b, :]), over_tokens(mlp_wb[:, 0, :]), ALU.mult)\
                    .then_inc(hw_ready, 1)

            def row_scale(amax, scale_out, semaphore, n):
                dve.tensor_scalar(scale_out, amax, 1e-12, 1.0 / FP8_MAX, ALU.max, ALU.mult).then_inc(semaphore, 1)
                dve.wait_ge(semaphore, n + 1)

            def h_scale(t, b):
                n = 3 * t
                dve.wait_ge(h_ready, t + 1)
                dve.tensor_reduce(tok[:, 0, :], tokens(h_act[:, b, :]), AX.X, ALU.max, apply_absolute_value=True)\
                    .then_inc(h_step, 1)
                dve.wait_ge(h_step, n + 1)
                row_scale(tok[:, 0, :], tok[:, 1, :], h_step, n + 1)
                dve.tensor_copy(sx_all[:, bass.ds(t, 1), :].rearrange("p o u -> p (o u)"), tok[:, 1, :])
                dve.reciprocal(tok[:, 2, :], tok[:, 1, :]).then_inc(h_step, 1)
                dve.wait_ge(h_step, n + 3)
                dve.tensor_tensor(tokens(h_scaled[:, b, :]), tokens(h_act[:, b, :]), over_channels(tok[:, 2, :]), ALU.mult)\
                    .then_inc(hs_ready, 1)

            def h_add(t, b):
                dve.wait_ge(habs_ready, t + 1)
                dve.tensor_scalar(h_magic[:, b, :], h_magic[:, b, :], SUBNORMAL, None, ALU.max).then_inc(hadd_step, 1)
                dve.wait_ge(hadd_step, t + 1)
                wait_free(dve, hq_ready, t - 1)
                dve.tensor_tensor(h_added[:, b, :], h_magic[:, b, :], h_scaled[:, b, :], ALU.add).then_inc(hadd_ready, 1)

            def copy_q(t, b):
                if isinstance(t, int) and t == 0:
                    dve.wait_ge(qT_ready, TILES)
                wait_free(dve, acc_ready, PAIRS * (t - 1))
                dve.tensor_copy(qT[:, b, :], q_all[:, bass.ds(t, 1), :].rearrange("p o f -> p (o f)")).then_inc(q_copied, 1)

            def hidden_product(t, b):
                rows = hidden[:, b, :].rearrange("p (u f) -> p u f", f=HID)
                wait_free(dve, hid_scaled, t - 1)
                for pp in range(PAIRS):
                    dve.wait_ge(relu_ready, PAIRS * t + pp + 1)
                    bank = 2 * (pp % 2)
                    dve.tensor_tensor(rows[:, 2 * pp:2 * pp + 2, :], ps[:, bank:bank + 2, HID:2 * HID],
                                      relu_a[:, pp % 2, :].rearrange("p (u f) -> p u f", f=HID), ALU.mult).then_inc(acc_used, 1)
                dve.wait_ge(acc_used, PAIRS * (t + 1))
                n = 7 * t
                sx = sx_all[:, bass.ds(t, 1), :].rearrange("p o u -> p (o u)")

                def step(ins, k):
                    ins.then_inc(hid_step, 1)
                    dve.wait_ge(hid_step, n + k)

                step(dve.tensor_reduce(tok[:, 3, :], rows, AX.X, ALU.max, apply_absolute_value=True), 1)
                step(dve.tensor_tensor(tok[:, 4, :], sx, sx, ALU.mult), 2)
                step(dve.tensor_tensor(tok[:, 5, :], tok[:, 3, :], tok[:, 4, :], ALU.mult), 3)
                step(dve.tensor_scalar(tok[:, 6, :], tok[:, 5, :], 1e-12, 1.0 / FP8_MAX, ALU.max, ALU.mult), 4)
                step(dve.tensor_copy(sg_all[:, bass.ds(t, 1), :].rearrange("p o u -> p (o u)"), tok[:, 6, :]), 5)
                step(dve.reciprocal(tok[:, 7, :], tok[:, 6, :]), 6)
                step(dve.tensor_tensor(rescale[:, b, :], tok[:, 7, :], tok[:, 4, :], ALU.mult), 7)

            def hidden_add(t, b):
                dve.wait_ge(hid_abs, t + 1)
                dve.tensor_scalar(magic[:, b, :], magic[:, b, :], SUBNORMAL, None, ALU.max).then_inc(hid_max, 1)
                dve.wait_ge(hid_max, t + 1)
                wait_free(dve, hid_q, t - 1)
                dve.tensor_tensor(added[:, b, :], magic[:, b, :], scaled[:, b, :], ALU.add).then_inc(hid_added, 1)

            def mlp_update(l, t, b):
                dve.wait_ge(mlp_out_ready, t + 1)
                wait_free(dve, xnew_ready, x_base(l) + t - 1)
                dve.wait_ge(mres_loaded[b], landed(32, t, b))
                dve.tensor_tensor(tokens(prod_m[:, b, :]), tokens(ps[:, O_BANK, :]),
                                  sg_all[:, bass.ds(t, 1), :].rearrange("p o u -> p (o u)").unsqueeze(2).to_broadcast([P, U, C]),
                                  ALU.mult).then_inc(prod_ready, 1)

            for l in range(layers):
                group_norm(l)
                dve.wait_ge(gn_ready, l + 1)
                if l in TRIANGLES:
                    q = TRIANGLES[l]
                    pair_weights(q)
                    pipeline(dve, layer_norm(l, 0, xn, 1.0, 2, [(0, lambda t, b: store_pairs(l, 0, t, b)),
                                                                (0, lambda t, b: store_pairs(l, 1, t, b))]))
                    dve.wait_ge(pair_stored, 2 * TILES * (q + 1))
                    pipeline(dve, [(1, lambda k, b: stage_stationary(q, k, b)),
                                   (0, lambda k, b: move_products(q, k, b))], BLOCKS)
                    dve.wait_ge(z_act, BLOCKS * (q + 1))
                    dve.wait_ge(z_dve, BLOCKS * (q + 1))
                    pipeline(dve, layer_norm(l, 1, xn, 1.0, 2, [(0, lambda t, b: gated(l, t, b)),
                                                                (0, lambda t, b: update(l, t, b))]))
                else:
                    pipeline(dve, layer_norm(l, 0, h_norm, 0.0, 1) + [
                                   (1, h_weight),
                                   (3, lambda t, b: centre(l, t, b)),
                                   (-1, h_add),
                                   (0, h_scale)])
                    pipeline(dve, [(1, copy_q),
                                   (-4, lambda t, b: mlp_update(l, t, b)),
                                   (-2, hidden_add),
                                   (0, hidden_product)])

        @block.scalar
        def _(act):
            def square(r, b):
                act.wait_ge(shift_ready, r + 1)
                wait_free(act, sums_ready, r - 1)
                act.activation(squares[:, b, :], shifted[:, b, :], ACT.Square).then_inc(sq_ready, 1)

            def apart():
                act.sem_inc(s_apart, 1)

            act.wait_ge(s_quant, 5)
            act.activation(wq_magic, wq_y, ACT.Abs, scale=SPLIT).then_inc(s_quant_abs, 1)
            pipeline(act, [(0, lambda t, b: square(t, b))])

            def evacuate_xnT(m, t, b, free_sem, free_value):
                act.wait_ge(xnT_psum, m + 1)
                if not (isinstance(t, int) and t < 2):
                    wait_free(act, free_sem, free_value)
                act.activation(xnT[:, b, :], ps[:, T_BANK + b, :], ACT.Copy).then_inc(xnT_ready, 1)

            def normalise(l, side, dst, dst_used, t, b):
                n = ln_base(l, side) + t
                act.wait_ge(shift_step, 2 * n + 2)
                dst_used(t)
                apart()
                for u in range(DVE_TOKENS[l, side], U):
                    if side == 0:
                        src = normed[:, b, u * C:(u + 1) * C]
                    else:
                        src = pairs[:, 0, :, bass.ds(t * U + u, 1)].rearrange("p c o -> p (c o)")
                    last = act.activation(dst[:, b, u * C:(u + 1) * C], src, ACT.Identity,
                                          scale=ln_s[:, b, RSTD, u:u + 1], bias=ln_s[:, b, SHIFT, u:u + 1])
                last.then_inc(xn_act, 1)

            def gates(q, half, t, b):
                n = TILES * q + t
                if half == 0:
                    wait_free(act, gate_stored[b], landed(16, n - 2, b))
                    wait_free(act, pair_stored, 2 * (n - 1))
                act.wait_ge(gates_ready, 2 * n + half + 1)
                bank = GATE_BANK[half]
                act.activation(sig[:, b, :].rearrange("p (k g) -> p k g", k=PAIRS)[:, 2 * half:2 * half + 2, :],
                               ps[:, bank:bank + 2, 0:GATES], ACT.Sigmoid).then_inc(sig_ready, 1)

            def store_gate(q, t, b):
                act.wait_ge(sig_ready, 2 * (TILES * q + t + 1))
                act.dma_start(tokens(gate_dram[TILES * q + t]),
                             sig[:, b, :].rearrange("p (u g) -> p u g", u=U)[:, :, 2 * C:3 * C]).then_inc(gate_stored[b], 16)

            def stage_moving(q, k, b):
                wait_free(act, chan_done, 2 * (BLOCKS * q + k - 1))
                apart()
                act.activation(mov_a[:, b, :, :], pairs[:, 0, bass.ds(k * BLK, BLK), 0:N], ACT.Copy).then_inc(mov_staged, 1)

            def move_products(q, k, b):
                act.wait_ge(chan_done, 2 * (BLOCKS * q + k) + 1)
                apart()
                act.activation(pairs[:, 0, bass.ds(k * BLK, 2), :], ps[:, 0:2, 0:COLS], ACT.Copy).then_inc(z_act, 1)

            def h_abs(t, b):
                act.wait_ge(hs_ready, t + 1)
                wait_free(act, hq_ready, t - 1)
                act.activation(h_magic[:, b, :], h_scaled[:, b, :], ACT.Abs, scale=SPLIT).then_inc(habs_ready, 1)

            def evacuate_qT(t, b):
                act.wait_ge(qT_psum, t + 1)
                apart()
                act.activation(q_all[:, bass.ds(t, 1), :].rearrange("p o f -> p (o f)"),
                               ps[:, T_BANK + b, 0:ROW // 2].bitcast(BF16), ACT.Copy).then_inc(qT_ready, 1)

            def relu(t, b):
                for pp in range(PAIRS):
                    k = PAIRS * t + pp
                    act.wait_ge(acc_ready, k + 1)
                    wait_free(act, acc_used, k - 1)
                    bank = 2 * (pp % 2)
                    act.activation(relu_a[:, pp % 2, :].rearrange("p (u f) -> p u f", f=HID),
                                   ps[:, bank:bank + 2, 0:HID], ACT.Relu).then_inc(relu_ready, 1)

            def hidden_scale(t, b):
                act.wait_ge(hid_step, 7 * (t + 1))
                wait_free(act, hid_added, t - 1)
                for u in range(U):
                    last = act.activation(scaled[:, b, u * HID:(u + 1) * HID], hidden[:, b, u * HID:(u + 1) * HID],
                                          ACT.Copy, scale=rescale[:, b, u:u + 1])
                last.then_inc(hid_scaled, 1)
                act.wait_ge(hid_scaled, t + 1)
                wait_free(act, hid_q, t - 1)
                act.activation(magic[:, b, :], scaled[:, b, :], ACT.Abs, scale=SPLIT).then_inc(hid_abs, 1)

            def evacuate_hqT(t, b):
                for half in range(2):
                    act.wait_ge(hqT_psum, 2 * t + half + 1)
                    if half == 0:
                        wait_free(act, mlp_out_ready, t - 1)
                    act.activation(q_hidT[:, b, half * 1024:(half + 1) * 1024], ps[:, H_BANK, :].bitcast(BF16), ACT.Copy)\
                        .then_inc(hqT_ready, 1)

            for l in range(layers):
                if l in TRIANGLES:
                    q = TRIANGLES[l]
                    xn_transposed = lambda side: lambda t: wait_free(act, xnT_psum, tr_base(l, side) + t - 1)
                    pipeline(act, [(0, lambda t, b: gates(q, 0, t, b)),
                                   (1, lambda t, b: evacuate_xnT(tr_base(l, 0) + t, t, b, proj_ready, 2 * (TILES * q + t - 1))),
                                   (0, lambda t, b: gates(q, 1, t, b)),
                                   (2, lambda t, b: normalise(l, 0, xn, xn_transposed(0), t, b)),
                                   (-1, lambda t, b: store_gate(q, t, b))])
                    act.wait_ge(pair_stored, 2 * TILES * (q + 1))
                    pipeline(act, [(1, lambda k, b: stage_moving(q, k, b)),
                                   (0, lambda k, b: move_products(q, k, b))], BLOCKS)
                    tail = [] if l == LAST else [(-1, lambda t, b: square(sum_base(l) + t, b))]
                    act.wait_ge(z_dve, BLOCKS * (q + 1))
                    act.wait_ge(z_act, BLOCKS * (q + 1))
                    pipeline(act, [(1, lambda t, b: evacuate_xnT(tr_base(l, 1) + t, t, b, out_ready, TILES * q + t - 1)),
                                   (2, lambda t, b: normalise(l, 1, xn, xn_transposed(1), t, b))] + tail)
                else:
                    pipeline(act, [(1, lambda t, b: normalise(l, 0, h_norm, lambda t: wait_free(act, hw_ready, t - 1), t, b)),
                                   (0, h_abs), (-2, evacuate_qT)])
                    pipeline(act, [(0, relu), (-1, hidden_scale), (-3, evacuate_hqT),
                                   (-4, lambda t, b: square(sum_base(l) + t, b))])

        @block.tensor
        def _(pe):
            pe.wait_ge(s_const, 7)
            pe.wait_ge(x_loaded[0], 32)
            pe.matmul(ps[:, 0, :], ones[:], xin[:, 0, :], start=True, stop=True).then_inc(anchor_sum, 1)
            for q in range(3):
                pe.wait_ge(s_fold, 4 * q + 2)
                pe.matmul(ps[:, 1, 0:PROJ + C], ones[0:C, :], fold_tmp[0:C, :], start=True, stop=True).then_inc(s_fold_pe, 1)
            pe.wait_ge(s_quant, 9)
            for k in range(4):
                pe.transpose(ps[:, 2, k * P:(k + 1) * P], wq_y[:, k * P:(k + 1) * P], ident[:])
            for k in range(2):
                last = pe.transpose(ps[:, 3, k * C:(k + 1) * C], wq_y[0:C, 512 + k * P:512 + (k + 1) * P], ident[0:C, 0:C])
            last.then_inc(s_quant_pe, 1)

            def add_to_sums(t, r, b):
                pe.wait_ge(sq_ready, r + 1)
                first = isinstance(t, int) and t == 0
                end = isinstance(t, int) and t == TILES - 1
                pe.matmul(ps[:, SUM, :], ones[:], shifted[:, b, :], start=first, stop=end, skip_group_check=True)
                pe.matmul(ps[:, SQ, :], ones[:], squares[:, b, :], start=first, stop=end, skip_group_check=True)\
                    .then_inc(sums_ready, 1)

            pipeline(pe, [(0, lambda t, b: add_to_sums(t, t, b))])
            pe.wait_ge(s_fold, 13)

            def transpose_xn(l, side, t, b):
                m = tr_base(l, side) + t
                pe.wait_ge(xn_ready, ln_base(l, side) + t + 1)
                pe.wait_ge(xn_act, ln_base(l, side) + t + 1)
                wait_free(pe, xnT_ready, m - 1)
                for k in range(PAIRS):
                    last = pe.transpose(ps[:, T_BANK + b, k * P:(k + 1) * P], xn[:, b, k * P:(k + 1) * P], ident[:])
                last.then_inc(xnT_psum, 1)

            def project(l, half, t, b):
                n = 2 * (TILES * TRIANGLES[l] + t) + half
                if half == 0:
                    pe.wait_ge(xnT_ready, tr_base(l, 0) + t + 1)
                wait_free(pe, sig_ready, n - 1)
                for k in range(2):
                    last = pe.matmul(ps[:, GATE_BANK[half] + k, 0:GATES], xnT[:, b, (2 * half + k) * P:(2 * half + k + 1) * P],
                                     wpair[:, VALUES:VALUES + GATES], start=True, stop=True)
                last.then_inc(gates_ready, 1)
                wait_free(pe, pair_stored, n - 1)
                for k in range(2):
                    last = pe.matmul(ps[:, half, k * VALUES:(k + 1) * VALUES], xnT[:, b, (2 * half + k) * P:(2 * half + k + 1) * P],
                                     wpair[:, 0:VALUES], start=True, stop=True)
                last.then_inc(proj_ready, 1)

            def multiply(q, k, b):
                n = BLOCKS * q + k
                pe.wait_ge(stat_staged, n + 1)
                pe.wait_ge(mov_staged, n + 1)
                pe.wait_ge(b_staged[b], landed(64, n, b))
                if isinstance(k, int) and k == 0:
                    pe.wait_ge(b_padded, 2 * (q + 1))
                for c in range(BLK):
                    if c == 0:
                        wait_free(pe, z_act, n)
                    if c == 2:
                        wait_free(pe, z_dve, n)
                    sa, ma, s_b, m_b = stat_a[:, b, c, :], mov_a[:, b, c, :], stat_b[:, b, c, :], mov_b[:, b, c, :]
                    pe.matmul(ps[:, c, 0:N], sa[:, 0:P], ma, start=True, stop=False)
                    pe.matmul(ps[:, c, 0:N], s_b[:, 0:P], m_b, start=False, stop=True)
                    for h in range(2):
                        o, j = ps[64 * h:64 * h + 64, c, N:COLS], slice(96 * h, 96 * h + 96)
                        pe.matmul(o, sa[:, P:N], ma[:, j], start=True, stop=False)
                        last = pe.matmul(o, s_b[:, P:N], m_b[:, j], start=False, stop=True)
                    if c % 2:
                        last.then_inc(chan_done, 1)

            def project_out(l, t, b):
                q = TRIANGLES[l]
                pe.wait_ge(xnT_ready, tr_base(l, 1) + t + 1)
                wait_free(pe, prod_ready, x_base(l) + t - 1)
                for k in range(PAIRS):
                    last = pe.matmul(ps[:, b, k * P:(k + 1) * P], xnT[:, b, k * P:(k + 1) * P],
                                     wpair[:, 2 * PROJ:], start=True, stop=True)
                last.then_inc(out_ready, 1)

            def transpose_q(t, b):
                pe.wait_ge(hq_ready, t + 1)
                wait_free(pe, qT_ready, t - 1)
                for k in range(PAIRS):
                    last = pe.transpose(ps[:, T_BANK + b, 0:ROW // 2].bitcast(BF16)[:, k * P:(k + 1) * P],
                                        q_in[:, b, k * P:(k + 1) * P], ident16[:])
                last.then_inc(qT_psum, 1)

            def hidden_layer(t, b):
                pe.wait_ge(q_copied, t + 1)
                for pp in range(PAIRS):
                    k = PAIRS * t + pp
                    wait_free(pe, acc_used, k - 1)
                    for h in range(2):
                        rows = slice(C * h, C * h + C)
                        for part_ in range(3):
                            last = pe.matmul(ps[:, 2 * (pp % 2) + h, :], qT[rows, b, pp * P:(pp + 1) * P],
                                             w1s[rows, part_, :], start=(part_ == 0), stop=(part_ == 2))
                    last.then_inc(acc_ready, 1)

            def transpose_hidden(t, b):
                pe.wait_ge(hid_q, t + 1)
                for half in range(2):
                    wait_free(pe, hqT_ready, 2 * t + half)
                    for k in range(8):
                        last = pe.transpose(ps[:, H_BANK, :].bitcast(BF16)[:, k * P:(k + 1) * P],
                                            q_hid[:, b, (8 * half + k) * P:(8 * half + k + 1) * P], ident16[:])
                    last.then_inc(hqT_psum, 1)

            def mlp_out(l, t, b):
                pe.wait_ge(hqT_ready, 2 * (t + 1))
                wait_free(pe, prod_ready, x_base(l) + t)
                for u in range(U):
                    for part_ in range(3):
                        for chunk in range(2):
                            last = pe.matmul(ps[:, O_BANK, u * C:(u + 1) * C], q_hidT[:, b, (2 * u + chunk) * P:(2 * u + chunk + 1) * P],
                                             w2s[:, part_, chunk * C:(chunk + 1) * C],
                                             start=(part_ == 0 and chunk == 0), stop=(part_ == 2 and chunk == 1))
                last.then_inc(mlp_out_ready, 1)

            for l in range(layers):
                if l in TRIANGLES:
                    q = TRIANGLES[l]
                    pe.wait_ge(w_step, q + 2)
                    pipeline(pe, [(0, lambda t, b: project(l, 0, t, b)),
                                  (1, lambda t, b: transpose_xn(l, 0, t, b)),
                                  (0, lambda t, b: project(l, 1, t, b))])
                    pipeline(pe, [(0, lambda k, b: multiply(q, k, b))], BLOCKS)
                    tail = [] if l == LAST else [(-1, lambda t, b: add_to_sums(t, sum_base(l) + t, b))]
                    pipeline(pe, [(0, lambda t, b: project_out(l, t, b)),
                                  (1, lambda t, b: transpose_xn(l, 1, t, b))] + tail)
                else:
                    pipeline(pe, [(-1, transpose_q)])
                    pipeline(pe, [(0, hidden_layer), (-3, transpose_hidden),
                                  (-3, lambda t, b: mlp_out(l, t, b)),
                                  (-4, lambda t, b: add_to_sums(t, sum_base(l) + t, b))])


def tiles_of(a):
    rest = a.shape[2:]
    part_a = a[:, :P].reshape(TILES_A, U, P, *rest).swapaxes(1, 2)
    part_b = a[:, P:].reshape(2, TILES - TILES_A, U, N - P, *rest)
    part_b = np.moveaxis(part_b, (0, 3), (1, 2)).reshape(TILES - TILES_A, P, U, *rest)
    return np.ascontiguousarray(np.concatenate([part_a, part_b]))


def image_of(tiles):
    part_a = tiles[:TILES_A].swapaxes(1, 2).reshape(N, P, C)
    part_b = tiles[TILES_A:].reshape(TILES - TILES_A, 2, N - P, U, C)
    part_b = np.moveaxis(part_b, (1, 2), (0, 3)).reshape(N, N - P, C)
    return np.ascontiguousarray(np.concatenate([part_a, part_b], axis=1))


def kernel(**inputs):
    import concourse.bacc as bacc
    from concourse.bass_utils import run_bass_kernel_spmd

    a = {k: np.asarray(v) for k, v in inputs.items()}
    zeros = np.zeros(C, np.float32)
    g = lambda l, names: [a[f"L{l}_conv_{n}"] for n in names.split()]
    w_l0 = [w.T for w in g(0, "left_w right_w lgate_w rgate_w ogate_w out_w")]
    proj = a["L1_conv_W_proj"]
    w_l1 = [proj[:, C:2 * C], proj[:, 3 * C:], proj[:, :C], proj[:, 2 * C:3 * C], *g(1, "W_gate W_ab")]
    w_l3 = g(3, "Wa Wb Wga Wgb Wgo Wo")
    w = np.stack([np.concatenate(x, 1) for x in (w_l0, w_l1, w_l3)], 1)
    b = [g(0, "left_b right_b lgate_b rgate_b ogate_b out_b"), [zeros] * 6, g(3, "ba bb bga bgb bgo bo")]
    n = [g(0, "norm_w norm_b ton_w ton_b"), g(1, "ln1_g ln1_b ln2_g ln2_b"), g(3, "norm_g norm_b norm_out_g norm_out_b")]
    norms = np.stack([np.stack(x, 1) for x in n], 1)
    w1 = a["L2_conv_w1"].reshape(4, P, 1, C)
    arrays = {
        "x_in": tiles_of(a["x"][0].swapaxes(0, 1)).reshape(TILES, P, ROW),
        "weights": np.concatenate([w, w]),
        "biases": np.stack([np.concatenate(x) for x in b]),
        "norms": np.concatenate([norms, norms]),
        "mask": tiles_of(a["L3_conv_mask"][0]).swapaxes(0, 1).reshape(P, COLS),
        "mlp_norm": np.stack(g(2, "ln_w ln_b")),
        "w1": np.concatenate([w1, w1], 2).swapaxes(0, 1).reshape(P, 4 * P),
        "w2": a["L2_conv_w2"],
    }
    arrays = {f"in_{k}": np.ascontiguousarray(v) for k, v in arrays.items()}
    nc = bacc.Bacc("TRN2", target_bir_lowering=False, num_devices=1)
    args = [nc.dram_tensor(k, v.shape, mybir.dt.from_np(v.dtype), kind="ExternalInput").ap() for k, v in arrays.items()]
    args.append(nc.dram_tensor("out_x", (TILES, P, ROW), F32, kind="ExternalOutput").ap())
    build(nc, *args)
    r = run_bass_kernel_spmd(nc, [arrays], core_ids=[0])
    return image_of(r.results[0]["out_x"].reshape(TILES, P, U, C))[None]
```

```python
from contextlib import ExitStack

import numpy as np

import concourse.bass as bass
from concourse import mybir

F32 = mybir.dt.float32
BF16 = mybir.dt.bfloat16
ALU = mybir.AluOpType
ACT = mybir.ActivationFunctionType
AX = mybir.AxisListType

P = 128
N = 192
C = 64
U = 8
ROW = U * C
TILES = N * N // (P * U)
TILES_A = N // U
COLS = TILES * U
GROUPS = C // 2
QUARTERS = 4
GPQ = GROUPS // QUARTERS
GN_COUNT = float(N * N * 2)
GN_EPS = 1e-5
LN_EPS = 1e-5
ROOT_C = 8.0
PAIRS = U // 2
HALF = U // 2
VALUES = 4 * C
GATES = 6 * C
PROJ = 5 * C
BLK = 4
BLOCKS = C // BLK
HID = 256
FP8_MAX = 448.0
SPLIT = float(2 ** 20)
SUBNORMAL = 1.5 * 2.0 ** 14
TRIANGLES = {0: 0, 1: 1, 3: 2}
LAST = 3
FIRST = 2
RING = 4
WHOLE = [(0, 1), (1, 6), (6, 12), (12, 18), (18, 24), (24, 30), (30, 36)]
SUM_PARTS = [(0, 4), (4, 8), (8, 12), (12, 16), (16, 36)]
X_LOADS, RES_LOADS, X_STORES = (1, 2, 1, 1), (2, 3, 0, 2), (2, 1, 1, 1)
DVE_TOKENS = {(0, 0): 5, (0, 1): 2, (1, 0): 5, (1, 1): 2, (2, 0): 1, (3, 0): 3, (3, 1): 2}


def pipeline(eng, stages, n=TILES, t0=0):
    leads = [stage[0] for stage in stages]
    turn = RING if any(len(stage) > 2 for stage in stages) else 2
    first, start, end = t0 - max(leads), t0 + 2 - min(leads), t0 + n - min(leads)
    turns = max(t0 + n - max(leads) - start, 0) // turn

    def step(i, buffer, which):
        for lead, f, *ring in stages:
            if which(lead):
                t, m = i(lead), buffer + lead
                f(t, m % 2, m % RING) if ring else f(t, m % 2)

    def peeled(i):
        step(lambda lead: i + lead, i, lambda lead: t0 <= i + lead < t0 + n)

    for i in range(first, start):
        peeled(i)
    if turns:
        with eng.Fori(start, start + turn * (turns - 1) + 1, turn) as i:
            for j in range(turn):
                step(lambda lead: i + (j + lead), start + j, lambda lead: True)
    for i in range(start + turn * turns, end):
        peeled(i)


def wait_free(eng, semaphore, value):
    if not (isinstance(value, int) and value <= 0):
        eng.wait_ge(semaphore, value)


def build(nc, x_in, weights, biases, norms, mask, mlp_norm, w1, w2, out, layers=4):
    with ExitStack() as ctx:
        def sb(name, shape, dt=F32):
            return ctx.enter_context(nc.sbuf_tensor(name, shape, dt))

        def sem(name):
            return ctx.enter_context(nc.semaphore(name))

        x_nat = nc.dram_tensor("x_nat", (N, N, C), F32, kind="Internal").ap()
        x_mid = [nc.dram_tensor(f"x_mid{i}", (TILES, P, ROW), F32, kind="Internal").ap() for i in range(2)]
        gate_dram = nc.dram_tensor("gate_dram", (3 * TILES, P, ROW), F32, kind="Internal").ap()

        pairs = sb("pairs", [P, 2, C, COLS])
        work = sb("work", [P, 11264])

        def part(buf, lo, n, bufs=2):
            return buf[:, lo:lo + n * bufs].rearrange("p (b f) -> p b f", b=bufs)

        xin, _, _, xn, xnT = (part(work, 1024 * k, ROW) for k in range(5))
        normed = part(work, 1024, ROW, RING)
        sig = part(work, 6144, U * 3 * C)
        wbias = work[:, 9216:9216 + 3 * (PROJ + C)].rearrange("p (q e) -> p q e", q=3)
        wpair = work[:, 10368:10368 + 2 * (PROJ + C)]
        stat_a, mov_a, stat_b, mov_b = (part(work, 2 * BLK * N * k, BLK * N).rearrange("p b (k n) -> p b k n", k=BLK)
                                        for k in range(4))
        xres, gate = part(work, 0, ROW, RING), part(work, 8192, ROW, RING)
        xn_out = part(work, 2048, ROW, RING)
        xnew, shifted, squares = (part(work, 5120 + 1024 * k, ROW) for k in range(3))
        acc = work[:, 6144:6144 + ROW]
        x_all = pairs[:].rearrange("p a c n -> p (a c n)")[:, 0:TILES * ROW].rearrange("p (t f) -> p t f", t=TILES)
        wide = pairs[:].rearrange("p a c n -> p (a c n)")
        h_norm, h_pre, h_act, h_scaled, h_magic, h_added = (part(wide, 1024 * k, ROW) for k in range(6))
        q_in = part(wide, 6144, ROW // 2).bitcast(BF16)
        hidden = part(wide, 0, U * HID, RING)
        scaled, magic = (part(wide, 8192 + 4096 * k, U * HID) for k in range(2))
        relu_a = part(wide, 16384, 2 * HID)
        q_all = wide[:, 17408:17408 + TILES * ROW].bitcast(BF16).rearrange("p (t f) -> p t f", t=TILES)
        q_hid = part(work, 0, U * HID // 2).bitcast(BF16)
        q_hidT = part(work, 2048, U * HID // 2).bitcast(BF16)
        xres_m, prod_m = part(work, 8192, ROW), part(wide, 17408 + TILES * ROW, ROW)
        wq_raw, wq_y, wq_magic, wq_added, wq_q = (wide[:, TILES * ROW + 768 * k:TILES * ROW + 768 * (k + 1)] for k in range(5))
        w_rest = wide[:, TILES * ROW + 768 * 5:TILES * ROW + 768 * 5 + 640]
        fold_tmp = wide[:, 24576:24576 + PROJ + C]

        ident = sb("ident", [P, P])
        ident16 = sb("ident16", [P, P], BF16)
        ones = sb("ones", [P, P])
        half_power = sb("half_power", [P, U])
        wfold = sb("wfold", [P, 3, PROJ + C])
        nrm = sb("nrm", [P, 3, 4])
        nrm_d = sb("nrm_d", [P, 3, 2])
        mlp_wb = sb("mlp_wb", [P, 2, C])
        mask_sb = sb("mask_sb", [P, COLS])
        mask_t = sb("mask_t", [P, 2, U])
        stats = sb("stats", [P, 2, U, 6])
        ln_s = sb("ln_s", [P, 2, 8, U])
        SUM2, M2, DIFF, DIFF2, VAR, RSTD, SHIFT, _ = range(8)
        tok = sb("tok", [P, 8, U])
        sx_all = sb("sx_all", [P, TILES, U])
        sg_all = sb("sg_all", [P, TILES, U])
        rescale = sb("rescale", [P, 2, U])
        wscale = sb("wscale", [P, 3, 5])
        anchor = sb("anchor", [P, C])
        gn_mean = sb("gn_mean", [P, C])
        gn_rstd = sb("gn_rstd", [P, C])
        gn_s = sb("gn_s", [P, 8, GROUPS])
        gn_roots = sb("gn_roots", [P, GROUPS])
        w1s = sb("w1s", [P, 3, 2 * HID], BF16)
        w2s = sb("w2s", [P, 3, 2 * C], BF16)

        ps = ctx.enter_context(nc.psum_tensor("ps", [P, 8, 512], F32))
        T_BANK, SUM, SQ = 4, 6, 7
        GATE_BANK = (2, 6)
        H_BANK, O_BANK = 4, 5

        (s_const,
         s_params,
         s_fold, s_fold_pe,
         s_quant, s_quant_abs, s_quant_pe,
         x_loaded,
         x_centred,
         x_scaled,
         ln_step,
         shift_step,
         var_ready,
         rstd_ready,
         xn_ready,
         xn_act,
         w_step,
         b_padded,
         xnT_psum,
         xnT_ready,
         gates_ready, proj_ready,
         sig_ready,
         pair_stored,
         gate_stored,
         mask_ready,
         stat_staged, mov_staged, b_staged,
         chan_done,
         z_act, z_dve,
         res_loaded,
         out_ready,
         prod_ready,
         xnew_ready,
         xnew_stored,
         shift_ready,
         sq_ready,
         sums_ready,
         input_acc, input_summed,
         gn_step, gn_var, gn_pow,
         gn_picked, gn_spread, gn_ready,
         anchor_sum, anchor_step, anchor_ready,
         hw_ready, h_ready, h_step,
         hs_ready, habs_ready, hadd_step, hadd_ready, hq_ready,
         qT_psum, qT_ready,
         acc_ready, relu_ready, acc_used,
         hid_step, hid_scaled, hid_abs, hid_max, hid_added, hid_q,
         hqT_psum, hqT_ready,
         mlp_out_ready, mres_loaded,
         s_apart, s_pe_apart) = [sem(f"sem_{k}") for k in range(76)]

        x_loaded, gate_stored, b_staged, xnew_stored, mres_loaded = [
            (one, sem(f"sem_odd_{k}")) for k, one in enumerate((x_loaded, gate_stored, b_staged, xnew_stored, mres_loaded))]
        res_loaded = [res_loaded] + [sem(f"sem_res_{k}") for k in range(1, RING)]

        x_whole = [sem(f"sem_whole_{k}") for k in range(len(WHOLE))]

        tri_before = {l: sum(k in TRIANGLES for k in range(l)) for l in range(5)}

        def x_base(l):
            return TILES * l

        def sum_base(l):
            return TILES * (l + 1)

        def ln_base(l, side):
            return TILES * (l + tri_before[l] + side)

        def tr_base(l, side):
            return TILES * (2 * TRIANGLES[l] + side)

        def landed(each, n, b):
            return (n - b) * (each // 2) + each

        def tile_landed(dmas, l, t, b, ring=2):
            each = 16 * dmas[l]
            return (t - b) * (each // ring) + (each + all_landed(dmas, l, ring))

        def all_landed(dmas, l, ring=2):
            return TILES // ring * 16 * sum(dmas[:l])

        def tokens(ap):
            return ap.rearrange("p (u c) -> p u c", c=C)

        def over_tokens(ap):
            return ap.unsqueeze(1).to_broadcast([P, U, C])

        def over_channels(ap):
            return ap.unsqueeze(2).to_broadcast([P, U, C])

        def whole_tile(t):
            return x_all[:, bass.ds(t, 1), :].rearrange("p o f -> p (o f)")

        def cols(t):
            return bass.ds(t * U, U)

        block = ctx.enter_context(nc.Block())

        @block.sync
        def _(sp):
            def load_natural(dst, t, free0, signal):
                sp.dma_start(tokens(dst)[0:64], free0[0]).then_inc(signal, 16)
                sp.dma_start(tokens(dst)[64:P], free0[1]).then_inc(signal, 16)

            def lane_rows(t, part_b):
                if part_b:
                    f = (t - TILES_A) * U
                    return [x_nat[bass.ds(f + h * (N // 2), U), P:N, :].rearrange("f l c -> l f c") for h in range(2)]
                return [x_nat[bass.ds(t * U, U), 64 * h:64 * h + 64, :].rearrange("f l c -> l f c") for h in range(2)]

            def lane_first_rows(t, part_b):
                if part_b:
                    f = (t - TILES_A) * U
                    return [x_nat[P:N, bass.ds(f + h * (N // 2), U), :] for h in range(2)]
                return [x_nat[64 * h:64 * h + 64, bass.ds(t * U, U), :] for h in range(2)]

            def rows_of(buffer, pieces):
                size = P // len(pieces)
                return [(tokens(buffer[size * h:size * h + size]), piece) for h, piece in enumerate(pieces)]

            def x_source(l, t, part_b):
                if l == 0:
                    return [tokens(x_in[t])]
                if l == 1:
                    return lane_rows(t, part_b)
                return [tokens(x_mid[l - 2][t])]

            def x_target(l, t, part_b):
                if l == LAST:
                    return [tokens(out[t])]
                if l == 0:
                    return lane_first_rows(t, part_b)
                return [tokens(x_mid[l - 1][t])]

            def by_part(make_stages, natural):
                if not natural:
                    pipeline(sp, make_stages(False, 0))
                else:
                    pipeline(sp, make_stages(False, 0), TILES_A)
                    pipeline(sp, make_stages(True, TILES_A), TILES - TILES_A)

            sp.dma_start(x_all[:, 0, :], x_in[0]).then_inc(x_whole[0], 16)
            sp.dma_start(wfold[:], weights).then_inc(s_params, 16)
            sp.dma_start(nrm[:], norms).then_inc(s_params, 16)
            sp.dma_start(wbias, biases.partition_broadcast(P)).then_inc(s_params, 16)
            sp.dma_start(mlp_wb[:], mlp_norm.partition_broadcast(P)).then_inc(s_params, 16)
            sp.dma_start(mask_sb[:], mask).then_inc(s_params, 16)
            sp.wait_ge(s_const, 1)
            sp.dma_start(wq_raw[:, 0:512], w1).then_inc(s_params, 16)
            sp.dma_start(wq_raw[0:C, 512:768], w2).then_inc(s_params, 16)

            for k, (lo, hi) in enumerate(WHOLE[1:]):
                sp.dma_start(x_all[:, lo:hi, :], x_in[lo:hi].rearrange("t p f -> p t f")).then_inc(x_whole[k + 1], 16)

            def load_x(l, t, b, part_b):
                wait_free(sp, x_centred, x_base(l) + t - 1)
                for dst, src in rows_of(xin[:, b, :], x_source(l, t, part_b)):
                    sp.dma_start(dst, src).then_inc(x_loaded[b], 16)

            def load_residual(l, q, t, r, part_b):
                wait_free(sp, xnew_ready, x_base(l) + t - 3)
                for dst, src in rows_of(xres[:, r, :], x_source(l, t, part_b)):
                    sp.dma_start(dst, src).then_inc(res_loaded[r], 16)
                sp.dma_start(gate[:, r, :], gate_dram[TILES * q + t]).then_inc(res_loaded[r], 16)

            def load_residual_mlp(l, t, b):
                wait_free(sp, xnew_ready, x_base(l) + t - 1)
                for dst, src in rows_of(xres_m[:, b, :], x_source(l, t, False)):
                    sp.dma_start(dst, src).then_inc(mres_loaded[b], 16)

            def store_x(l, t, b, part_b):
                sp.wait_ge(xnew_ready, x_base(l) + t + 1)
                for src, dst in rows_of(xnew[:, b, :], x_target(l, t, part_b)):
                    sp.dma_start(dst, src).then_inc(xnew_stored[b], 16)

            for l in range(layers):
                if l:
                    for b in range(2):
                        sp.wait_ge(xnew_stored[b], all_landed(X_STORES, l))
                if l in TRIANGLES:
                    q = TRIANGLES[l]

                    def input_stages(part_b, t0):
                        return [(0, lambda t, b: load_x(l, t + t0, b, part_b))]

                    by_part(input_stages, l == 1)
                    sp.wait_ge(pair_stored, 2 * TILES * (q + 1))

                    def stage_b(k, b):
                        wait_free(sp, chan_done, 2 * (BLOCKS * q + k - 1))
                        for side, dst in ((1, stat_b), (0, mov_b)):
                            for h in range(2):
                                sp.dma_start(dst[0:64, b, :, 96 * h:96 * h + 96],
                                             pairs[64 * h:64 * h + 64, side, bass.ds(k * BLK, BLK), N:COLS])\
                                    .then_inc(b_staged[b], 16)

                    pipeline(sp, [(0, stage_b)], BLOCKS)
                    sp.wait_ge(chan_done, 2 * BLOCKS * (q + 1))
                    for b in range(2):
                        sp.wait_ge(gate_stored[b], 8 * TILES * (q + 1))

                    def output_stages(part_b, t0):
                        return [(3, lambda t, b, r: load_residual(l, q, t + t0, r, part_b), RING),
                                (0, lambda t, b: store_x(l, t + t0, b, part_b))]

                    by_part(output_stages, l < 2)
                else:
                    pipeline(sp, [(0, lambda t, b: load_x(l, t, b, False))])
                    pipeline(sp, [(1, lambda t, b: load_residual_mlp(l, t, b)),
                                  (0, lambda t, b: store_x(l, t, b, False))])
            for b in range(2):
                sp.wait_ge(xnew_stored[b], all_landed(X_STORES, layers))
                sp.wait_ge(gate_stored[b], 8 * TILES * tri_before[layers])

        @block.gpsimd
        def _(pool):
            pool.memset(wq_raw[:, 512:768], 0.0).then_inc(s_const, 1)
            pool.memset(ident[:], 0.0).then_inc(s_const, 1)
            pool.memset(ident16[:], 0.0).then_inc(s_const, 1)
            pool.memset(ones[:], 1.0).then_inc(s_const, 1)
            pool.memset(half_power[:], -0.5).then_inc(s_const, 1)
            pool.memset(gn_roots[:], 0.0).then_inc(s_const, 1)
            pool.wait_ge(s_const, 6)
            for m in (ident, ident16):
                pool.affine_select(out=m[:], in_=m[:], compare_op=ALU.not_equal, fill=1.0, base=0,
                                   pattern=[[-1, P]], channel_multiplier=1).then_inc(s_const, 1)

            def shift(src, r, b):
                wait_free(pool, sums_ready, r - 1)
                pool.tensor_tensor(tokens(shifted[:, b, :]), tokens(src), over_tokens(anchor[:]), ALU.subtract)\
                    .then_inc(shift_ready, 1)

            def shift_input(t, b):
                pool.tensor_tensor(tokens(whole_tile(t)), tokens(whole_tile(t)), over_tokens(anchor[:]), ALU.subtract)\
                    .then_inc(shift_ready, 1)

            pool.wait_ge(anchor_ready, 1)
            for k, (lo, hi) in enumerate(WHOLE):
                pool.wait_ge(x_whole[k], 16)
                pipeline(pool, [(0, shift_input)], hi - lo, lo)

            def group_rstd(l):
                pool.wait_ge(gn_var, l + 1)
                pool.tensor_tensor(gn_s[:, 6, 0:GPQ], gn_s[:, 7, 0:GPQ], half_power[:, 0:GPQ], ALU.pow).then_inc(gn_pow, 1)

            def centre(l, t, b, r):
                if isinstance(t, int) and t < FIRST:
                    return
                pool.wait_ge(x_loaded[b], tile_landed(X_LOADS, l, t, b))
                if isinstance(t, int) and t == 0:
                    pool.wait_ge(gn_ready, l + 1)
                wait_free(pool, xn_ready, ln_base(l, 0) + t - 3)
                wait_free(pool, xn_act, ln_base(l, 0) + t - 3)
                pool.tensor_tensor(tokens(normed[:, r, :]), tokens(xin[:, b, :]), over_tokens(gn_mean[:]), ALU.subtract)\
                    .then_inc(x_centred, 1)

            def scale(l, t, b, r):
                pool.wait_ge(x_centred, x_base(l) + t + 1)
                if isinstance(t, int) and t == 0:
                    pool.wait_ge(gn_ready, l + 1)
                pool.tensor_tensor(tokens(normed[:, r, :]), tokens(normed[:, r, :]), over_tokens(gn_rstd[:]), ALU.mult)\
                    .then_inc(x_scaled, 1)

            def token_rstd(l, side, t, b):
                n = ln_base(l, side) + t
                pool.wait_ge(var_ready, n + 1)
                wait_free(pool, xn_ready, n - 1)
                wait_free(pool, xn_act, n - 1)
                pool.tensor_tensor(ln_s[:, b, RSTD, :], ln_s[:, b, VAR, :], half_power[:, 0:U], ALU.pow)\
                    .then_inc(rstd_ready, 1)

            def update_mlp(l, t, b):
                pool.wait_ge(prod_ready, x_base(l) + t + 1)
                wait_free(pool, xnew_stored[b], tile_landed(X_STORES, l, t - 2, b))
                pool.tensor_tensor(xnew[:, b, :], prod_m[:, b, :], xres_m[:, b, :], ALU.add).then_inc(xnew_ready, 1)

            def shift_new(l, t, b):
                pool.wait_ge(xnew_ready, x_base(l) + t + 1)
                shift(xnew[:, b, :], sum_base(l) + t, b)

            def square_new(l, t, b):
                r = sum_base(l) + t
                pool.wait_ge(shift_ready, r + 1)
                wait_free(pool, sums_ready, r - 1)
                pool.tensor_tensor(squares[:, b, :], shifted[:, b, :], shifted[:, b, :], ALU.mult).then_inc(sq_ready, 1)

            def pad_operands(q):
                pool.wait_ge(pair_stored, 2 * TILES * (q + 1))
                pool.memset(stat_b[64:P], 0.0).then_inc(b_padded, 1)
                pool.memset(mov_b[64:P], 0.0).then_inc(b_padded, 1)

            def h_bias(t, b):
                pool.wait_ge(hw_ready, t + 1)
                wait_free(pool, hs_ready, t - 1)
                pool.tensor_tensor(tokens(h_act[:, b, :]), tokens(h_pre[:, b, :]), over_tokens(mlp_wb[:, 1, :]), ALU.add)\
                    .then_inc(h_ready, 1)

            def h_round(t, b):
                pool.wait_ge(hadd_ready, t + 1)
                wait_free(pool, qT_psum, t - 1)
                pool.tensor_tensor(q_in[:, b, :], h_added[:, b, :], h_magic[:, b, :], ALU.subtract)\
                    .then_inc(hq_ready, 1)

            def hidden_round(half, t, b):
                part_ = slice(half * HALF * HID, (half + 1) * HALF * HID)
                pool.wait_ge(hid_added, 2 * t + half + 1)
                if half == 0:
                    wait_free(pool, hqT_psum, 2 * (t - 1))
                pool.tensor_tensor(q_hid[:, b, part_], scaled[:, b, part_], magic[:, b, part_], ALU.subtract).then_inc(hid_q, 1)

            for l in range(layers):
                group_rstd(l)
                if l in TRIANGLES:
                    pipeline(pool, [(4, lambda t, b, r: scale(l, t, b, r), RING),
                                    (5, lambda t, b, r: centre(l, t, b, r), RING),
                                    (3, lambda t, b: token_rstd(l, 0, t, b))])
                    pad_operands(TRIANGLES[l])
                    tail = [] if l == LAST else [(0, lambda t, b: shift_new(l, t, b))]
                    pipeline(pool, [(4, lambda t, b: token_rstd(l, 1, t, b))] + tail)
                else:
                    pipeline(pool, [(4, lambda t, b, r: scale(l, t, b, r), RING),
                                    (3, lambda t, b: token_rstd(l, 0, t, b)),
                                    (1, h_bias),
                                    (-1, h_round)])
                    pipeline(pool, [(-6, lambda t, b: update_mlp(l, t, b)),
                                    (-6, lambda t, b: shift_new(l, t, b)),
                                    (-3, lambda t, b: hidden_round(0, t, b)),
                                    (-3, lambda t, b: hidden_round(1, t, b)),
                                    (-6, lambda t, b: square_new(l, t, b))])

        @block.vector
        def _(dve):
            dve.wait_ge(anchor_sum, 1)
            dve.tensor_reduce(gn_s[:, 7, :], ps[:, 0, :].rearrange("p (u g e) -> p g u e", u=U, e=2), AX.XY, ALU.add)\
                .then_inc(anchor_step, 1)
            dve.wait_ge(anchor_step, 1)
            dve.tensor_scalar(anchor[:].rearrange("p (g e) -> p g e", e=2),
                              gn_s[:, 7, :].unsqueeze(2).to_broadcast([P, GROUPS, 2]),
                              1.0 / (P * U * 2), None, ALU.mult).then_inc(anchor_ready, 1)

            dve.wait_ge(s_params, 16 * 7)
            dve.tensor_scalar(mlp_wb[:, 0, :], mlp_wb[:, 0, :], ROOT_C, None, ALU.mult)
            def chain(ins, n):
                ins.then_inc(s_quant, 1)
                dve.wait_ge(s_quant, n)

            w1_rows = lambda ap: ap[:, 0:512].rearrange("p (k c) -> p k c", k=4)
            chain(dve.tensor_reduce(wscale[:, 0, 0:4], w1_rows(wq_raw)[:, :, 0:C], AX.X, ALU.max,
                                    apply_absolute_value=True), 1)
            chain(dve.tensor_reduce(wscale[:, 0, 4:5], wq_raw[:, 512:768], AX.X, ALU.max,
                                    apply_absolute_value=True), 2)
            chain(dve.tensor_scalar(wscale[:, 1, :], wscale[:, 0, :], 1e-12, 1.0 / FP8_MAX, ALU.max, ALU.mult), 3)
            chain(dve.reciprocal(wscale[:, 2, :], wscale[:, 1, :]), 4)

            def by_row_scale(dst, src, k):
                for j in range(4):
                    dve.tensor_scalar(dst[:, j * P:(j + 1) * P], src[:, j * P:(j + 1) * P], wscale[:, k, j:j + 1], None, ALU.mult)
                return dve.tensor_scalar(dst[:, 512:768], src[:, 512:768], wscale[:, k, 4:5], None, ALU.mult)

            chain(by_row_scale(wq_y, wq_raw, 2), 5)
            dve.wait_ge(s_quant_abs, 1)
            chain(dve.tensor_scalar(wq_magic, wq_magic, SUBNORMAL, None, ALU.max), 6)
            chain(dve.tensor_tensor(wq_added, wq_magic, wq_y, ALU.add), 7)
            chain(dve.tensor_tensor(wq_q, wq_added, wq_magic, ALU.subtract), 8)
            chain(by_row_scale(wq_y, wq_q, 1), 9)
            dve.tensor_tensor(nrm_d[:], nrm[:, :, 1:4:2], nrm[:, :, 0:3:2], ALU.subtract).then_inc(s_fold, 1)
            for q in range(3):
                step = 4 * q + 1
                dve.wait_ge(s_fold, step)
                dve.tensor_scalar(fold_tmp[:, 0:PROJ], wfold[:, q, 0:PROJ], nrm_d[:, q, 0:1], None, ALU.mult)
                dve.tensor_scalar(fold_tmp[:, PROJ:], wfold[:, q, PROJ:], nrm_d[:, q, 1:2], None, ALU.mult).then_inc(s_fold, 1)
                dve.tensor_scalar(wfold[:, q, 0:PROJ], wfold[:, q, 0:PROJ], nrm[:, q, 0:1], ROOT_C, ALU.mult, ALU.mult)
                dve.tensor_scalar(wfold[:, q, PROJ:], wfold[:, q, PROJ:], nrm[:, q, 2:3], ROOT_C, ALU.mult, ALU.mult).then_inc(s_fold, 1)
                dve.wait_ge(s_fold_pe, q + 1)
                dve.tensor_tensor(fold_tmp, ps[:, 1, 0:PROJ + C], wbias[:, q, :], ALU.add).then_inc(s_fold, 1)
                dve.wait_ge(s_fold, step + 3)
                dve.scalar_tensor_tensor(out=wfold[:, q, :], in0=fold_tmp, scalar=ROOT_C / C, in1=wfold[:, q, :],
                                         op0=ALU.mult, op1=ALU.add).then_inc(s_fold, 1)

            dve.wait_ge(s_quant_pe, 1)
            n = 9
            for bank, dst, width in ((2, w1s, 2 * HID), (3, w2s, 2 * C)):
                rest = w_rest[:, 0:width]
                n += 5
                chain(dve.tensor_copy(dst[:, 0, :], ps[:, bank, 0:width]), n - 4)
                chain(dve.tensor_tensor(rest, ps[:, bank, 0:width], dst[:, 0, :], ALU.subtract), n - 3)
                chain(dve.tensor_copy(dst[:, 1, :], rest), n - 2)
                chain(dve.tensor_tensor(rest, rest, dst[:, 1, :], ALU.subtract), n - 1)
                chain(dve.tensor_copy(dst[:, 2, :], rest), n)
            dve.tensor_copy(w1s[C:P, 0, :], w1s[C:P, 1, :]).then_inc(s_quant, 1)

            def accumulate(t, b):
                dve.wait_ge(shift_ready, t + 1)
                if isinstance(t, int) and t == 1:
                    dve.tensor_tensor(acc, x_all[:, 0, :], x_all[:, 1, :], ALU.add).then_inc(input_acc, 1)
                else:
                    dve.wait_ge(input_acc, t - 1)
                    dve.tensor_tensor(acc, acc, whole_tile(t), ALU.add).then_inc(input_acc, 1)

            pipeline(dve, [(0, accumulate)], TILES - 1, 1)

            def group_norm(l):
                base = 6 * l

                def step(ins, k):
                    ins.then_inc(gn_step, 1)
                    dve.wait_ge(gn_step, base + k)

                dve.wait_ge(sums_ready, sum_base(l))
                if l == 0:
                    dve.wait_ge(input_summed, 1)
                dve.tensor_reduce(gn_s[:, 0, :], ps[:, SUM, :].rearrange("p (u g e) -> p g u e", u=U, e=2), AX.XY, ALU.add)
                step(dve.tensor_reduce(gn_s[:, 1, :], ps[:, SQ, :].rearrange("p (u g e) -> p g u e", u=U, e=2), AX.XY, ALU.add), 1)
                step(dve.tensor_scalar(gn_s[:, 2, :], gn_s[:, 0, :], 1.0 / GN_COUNT, None, ALU.mult), 2)
                step(dve.tensor_tensor(gn_s[:, 3, :], gn_s[:, 2, :], gn_s[:, 2, :], ALU.mult), 3)
                step(dve.scalar_tensor_tensor(out=gn_s[:, 4, :], in0=gn_s[:, 1, :], scalar=1.0 / GN_COUNT, in1=gn_s[:, 3, :],
                                              op0=ALU.mult, op1=ALU.subtract), 4)
                step(dve.tensor_scalar(gn_s[:, 5, :], gn_s[:, 4, :], 0.0, GN_EPS, ALU.max, ALU.add), 5)
                for k in range(QUARTERS):
                    last = dve.tensor_copy(gn_s[32 * k:32 * k + 32, 7, 0:GPQ], gn_s[32 * k:32 * k + 32, 5, GPQ * k:GPQ * (k + 1)])
                last.then_inc(gn_var, 1)
                step(dve.tensor_tensor(gn_mean[:].rearrange("p (g e) -> p g e", e=2), anchor[:].rearrange("p (g e) -> p g e", e=2),
                                       gn_s[:, 2, :].unsqueeze(2).to_broadcast([P, GROUPS, 2]), ALU.add), 6)
                if l in TRIANGLES:
                    for t in range(FIRST):
                        centre(l, t, t % 2, t)
                dve.wait_ge(gn_pow, l + 1)
                for k in range(QUARTERS):
                    last = dve.tensor_copy(gn_roots[32 * k:32 * k + 1, GPQ * k:GPQ * (k + 1)], gn_s[32 * k:32 * k + 1, 6, 0:GPQ])
                last.then_inc(gn_picked, 1)
                dve.wait_ge(gn_spread, l + 1)
                dve.tensor_copy(gn_rstd[:].rearrange("p (g e) -> p g e", e=2),
                                ps[:, 0, 0:GROUPS].unsqueeze(2).to_broadcast([P, GROUPS, 2])).then_inc(gn_ready, 1)

            def centre(l, t, b, r):
                dve.wait_ge(x_loaded[b], tile_landed(X_LOADS, l, t, b))
                if l not in TRIANGLES:
                    wait_free(dve, xn_act, ln_base(l, 0) + t - 3)
                dve.tensor_tensor(tokens(normed[:, r, :]), tokens(xin[:, b, :]), over_tokens(gn_mean[:]), ALU.subtract)\
                    .then_inc(x_centred, 1)

            def ln_source(side, t, r):
                if side == 0:
                    return lambda u: normed[:, r, u * C:(u + 1) * C]
                return lambda u: pairs[:, 0, :, bass.ds(t * U + u, 1)].rearrange("p c o -> p (c o)")

            def pair_weights(q):
                if q == 0:
                    dve.wait_ge(s_fold, 13)
                    dve.memset(wpair, 0.0).then_inc(w_step, 1)
                    dve.wait_ge(w_step, 1)
                for h in range(2):
                    rows = slice(C * h, C * h + C)
                    for lo, src, width in ((0, 0, VALUES // 2), (VALUES, 2 * C, GATES // 2), (2 * PROJ, PROJ, C)):
                        last = dve.tensor_copy(wpair[rows, lo + h * width:lo + (h + 1) * width], wfold[rows, q, src:src + width])
                last.then_inc(w_step, 1)

            def ln_moments(l, side, t, b, r):
                src = ln_source(side, t, r)
                if side == 0:
                    dve.wait_ge(x_scaled, x_base(l) + t + 1)
                for u in range(U):
                    last = dve.bn_stats(stats[:, b, u, :], src(u))
                last.then_inc(ln_step, 1)

            def small(b, k):
                return ln_s[:, b, k, :]

            def ln_combine(l, side, t, b):
                dve.wait_ge(ln_step, 3 * (ln_base(l, side) + t) + 1)
                wait_free(dve, xn_act, ln_base(l, side) + t - 1)
                dve.tensor_tensor(ln_s[:, b, SUM2:M2 + 1, :].rearrange("p k u -> p u k"),
                                  stats[:, b, :, 1:3], stats[:, b, :, 4:6], ALU.add)
                dve.tensor_tensor(small(b, DIFF), stats[:, b, :, 1], stats[:, b, :, 4], ALU.subtract).then_inc(ln_step, 1)

            def ln_diff2(l, side, t, b):
                dve.wait_ge(ln_step, 3 * (ln_base(l, side) + t) + 2)
                dve.scalar_tensor_tensor(out=small(b, DIFF2), in0=small(b, DIFF), scalar=C / 4.0, in1=small(b, DIFF),
                                         op0=ALU.mult, op1=ALU.mult).then_inc(ln_step, 1)

            def ln_var(l, side, t, b):
                dve.wait_ge(ln_step, 3 * (ln_base(l, side) + t) + 3)
                dve.scalar_tensor_tensor(out=small(b, VAR), in0=small(b, M2), scalar=C * LN_EPS, in1=small(b, DIFF2),
                                         op0=ALU.add, op1=ALU.add).then_inc(var_ready, 1)

            def ln_shift(l, side, t, b):
                n = ln_base(l, side) + t
                dve.wait_ge(rstd_ready, n + 1)
                wait_free(dve, xn_act, n - 1)
                dve.scalar_tensor_tensor(out=small(b, SHIFT), in0=small(b, SUM2), scalar=-0.5, in1=small(b, RSTD),
                                         op0=ALU.mult, op1=ALU.mult).then_inc(shift_step, 1)

            def normalise(l, side, dst, t, b, r):
                n = ln_base(l, side) + t
                src = ln_source(side, t, r)
                dve.wait_ge(shift_step, n + 1)
                if l in TRIANGLES:
                    wait_free(dve, xnT_psum, tr_base(l, side) + t + 1 - dst.shape[1])
                for u in range(DVE_TOKENS[l, side]):
                    last = dve.tensor_scalar(dst[:, r % dst.shape[1], u * C:(u + 1) * C], src(u), small(b, RSTD)[:, u:u + 1],
                                             small(b, SHIFT)[:, u:u + 1], ALU.mult, ALU.add)
                last.then_inc(xn_ready, 1)

            def layer_norm(l, side, dst, lead, big=()):
                big = list(big)
                at = lambda f: lambda t, b: f(l, side, t, b)
                return [(lead + 1, lambda t, b, r: ln_moments(l, side, t, b, r), RING), (lead + 1, at(ln_combine)),
                        (lead, at(ln_shift)), *big[:1], (lead + 1, at(ln_diff2)),
                        (lead, lambda t, b, r: normalise(l, side, dst, t, b, r), RING), (lead + 1, at(ln_var)), *big[1:]]

            def store_pairs(l, half, t, b):
                q = TRIANGLES[l]
                k = 2 * (TILES * q + t) + half
                dst = pairs[:].rearrange("p s c n -> p (s c) n")
                gates = sig[:, b, :].rearrange("p (u g) -> p u g", u=U)
                values = ps[:, half, :].rearrange("p (u k) -> p u k", u=HALF)
                u0 = HALF * half
                if l == 3 and half == 0:
                    dve.tensor_copy(mask_t[:, b, :], mask_sb[:, cols(t)]).then_inc(mask_ready, 1)
                    dve.wait_ge(mask_ready, t + 1)
                dve.wait_ge(proj_ready, k + 1)
                dve.wait_ge(sig_ready, k + 1)
                if l == 3:
                    for u in range(HALF):
                        last = dve.scalar_tensor_tensor(
                            out=dst[:, :, bass.ds(t * U + (u0 + u), 1)].rearrange("p k o -> p (k o)"),
                            in0=values[:, u, :], scalar=mask_t[:, b, u0 + u:u0 + u + 1],
                            in1=gates[:, u0 + u, 0:2 * C], op0=ALU.mult, op1=ALU.mult)
                else:
                    last = dve.tensor_tensor(dst[:, :, bass.ds(t * U + u0, HALF)].rearrange("p k u -> p u k"),
                                             values, gates[:, u0:u0 + HALF, 0:2 * C], ALU.mult)
                last.then_inc(pair_stored, 1)

            def stage_stationary(q, k, b):
                wait_free(dve, chan_done, 2 * (BLOCKS * q + k - 1))
                dve.tensor_copy(stat_a[:, b, :, :], pairs[:, 1, bass.ds(k * BLK, BLK), 0:N]).then_inc(stat_staged, 1)

            def move_products(q, k, b):
                dve.wait_ge(chan_done, 2 * (BLOCKS * q + k) + 2)
                dve.tensor_copy(pairs[:, 0, bass.ds(k * BLK + 2, 2), :], ps[:, 2:4, 0:COLS]).then_inc(z_dve, 1)

            def gated(l, t, b, r):
                q = TRIANGLES[l]
                dve.wait_ge(out_ready, TILES * q + t + 1)
                dve.wait_ge(res_loaded[r], tile_landed(RES_LOADS, l, t, r, RING))
                dve.tensor_tensor(gate[:, r, :], ps[:, b, :], gate[:, r, :], ALU.mult).then_inc(prod_ready, 1)

            def update(l, t, b, r):
                dve.wait_ge(prod_ready, x_base(l) + t + 1)
                wait_free(dve, xnew_stored[b], tile_landed(X_STORES, l, t - 2, b))
                if l != LAST:
                    wait_free(dve, shift_ready, sum_base(l) + t - 1)
                dve.tensor_tensor(xnew[:, b, :], gate[:, r, :], xres[:, r, :], ALU.add).then_inc(xnew_ready, 1)

            def h_weight(t, b):
                dve.wait_ge(xn_ready, ln_base(2, 0) + t + 1)
                dve.wait_ge(xn_act, ln_base(2, 0) + t + 1)
                wait_free(dve, h_ready, t - 1)
                dve.tensor_tensor(tokens(h_pre[:, b, :]), tokens(h_norm[:, b, :]), over_tokens(mlp_wb[:, 0, :]), ALU.mult)\
                    .then_inc(hw_ready, 1)

            def h_amax(t, b):
                dve.wait_ge(h_ready, t + 1)
                dve.tensor_reduce(tok[:, 0, :], tokens(h_act[:, b, :]), AX.X, ALU.max, apply_absolute_value=True)\
                    .then_inc(h_step, 1)

            def h_scale(t, b):
                dve.wait_ge(h_step, 3 * t + 1)
                dve.tensor_scalar(tok[:, 1, :], tok[:, 0, :], 1e-12, 1.0 / FP8_MAX, ALU.max, ALU.mult).then_inc(h_step, 1)

            def h_inverse(t, b):
                dve.wait_ge(h_step, 3 * t + 2)
                dve.tensor_copy(tile_row(sx_all, t), tok[:, 1, :])
                dve.reciprocal(tok[:, 2, :], tok[:, 1, :]).then_inc(h_step, 1)

            def h_rescale(t, b):
                dve.wait_ge(h_step, 3 * t + 3)
                dve.tensor_tensor(tokens(h_scaled[:, b, :]), tokens(h_act[:, b, :]), over_channels(tok[:, 2, :]), ALU.mult)\
                    .then_inc(hs_ready, 1)

            def h_max(t, b):
                dve.wait_ge(habs_ready, t + 1)
                dve.tensor_scalar(h_magic[:, b, :], h_magic[:, b, :], SUBNORMAL, None, ALU.max).then_inc(hadd_step, 1)

            def h_add(t, b):
                dve.wait_ge(hadd_step, t + 1)
                wait_free(dve, hq_ready, t - 1)
                dve.tensor_tensor(h_added[:, b, :], h_magic[:, b, :], h_scaled[:, b, :], ALU.add).then_inc(hadd_ready, 1)

            def hidden_rows(r):
                return hidden[:, r, :].rearrange("p (u f) -> p u f", f=HID)

            def hidden_product(pp, t, b, r):
                if pp == 0:
                    wait_free(dve, hid_scaled, t - 3)
                dve.wait_ge(relu_ready, PAIRS * t + pp + 1)
                bank = 2 * (pp % 2)
                dve.tensor_tensor(hidden_rows(r)[:, 2 * pp:2 * pp + 2, :], ps[:, bank:bank + 2, HID:2 * HID],
                                  relu_a[:, pp % 2, :].rearrange("p (u f) -> p u f", f=HID), ALU.mult).then_inc(acc_used, 1)

            def tile_row(ap, t):
                return ap[:, bass.ds(t, 1), :].rearrange("p o u -> p (o u)")

            def square_sx(t, b):
                wait_free(dve, hid_step, 6 * t)
                dve.tensor_tensor(tok[:, 4, :], tile_row(sx_all, t), tile_row(sx_all, t), ALU.mult).then_inc(hid_step, 1)

            def hidden_amax(half, t, b, r):
                if half == 0:
                    dve.wait_ge(acc_used, PAIRS * (t + 1))
                us = slice(HALF * half, HALF * half + HALF)
                last = dve.tensor_reduce(tok[:, 3, us], hidden_rows(r)[:, us, :], AX.X, ALU.max, apply_absolute_value=True)
                if half:
                    last.then_inc(hid_step, 1)

            def amax_of_product(t, b):
                dve.wait_ge(hid_step, 6 * t + 2)
                dve.tensor_tensor(tok[:, 5, :], tok[:, 3, :], tok[:, 4, :], ALU.mult).then_inc(hid_step, 1)

            def hidden_row_scale(t, b):
                dve.wait_ge(hid_step, 6 * t + 3)
                dve.tensor_scalar(tok[:, 6, :], tok[:, 5, :], 1e-12, 1.0 / FP8_MAX, ALU.max, ALU.mult).then_inc(hid_step, 1)

            def hidden_inverse(t, b):
                dve.wait_ge(hid_step, 6 * t + 4)
                dve.tensor_copy(tile_row(sg_all, t), tok[:, 6, :])
                dve.reciprocal(tok[:, 7, :], tok[:, 6, :]).then_inc(hid_step, 1)

            def hidden_rescale(t, b):
                dve.wait_ge(hid_step, 6 * t + 5)
                wait_free(dve, hid_scaled, t - 1)
                dve.tensor_tensor(rescale[:, b, :], tok[:, 7, :], tok[:, 4, :], ALU.mult).then_inc(hid_step, 1)

            def hidden_max(t, b):
                dve.wait_ge(hid_abs, 2 * (t + 1))
                dve.tensor_scalar(magic[:, b, :], magic[:, b, :], SUBNORMAL, None, ALU.max).then_inc(hid_max, 1)

            def hidden_add(half, t, b):
                part_ = slice(half * HALF * HID, (half + 1) * HALF * HID)
                dve.wait_ge(hid_max, t + 1)
                dve.tensor_tensor(scaled[:, b, part_], magic[:, b, part_], scaled[:, b, part_], ALU.add).then_inc(hid_added, 1)

            def mlp_update(l, t, b):
                dve.wait_ge(mlp_out_ready, t + 1)
                wait_free(dve, xnew_ready, x_base(l) + t - 1)
                dve.wait_ge(mres_loaded[b], landed(16, t, b))
                dve.tensor_tensor(tokens(prod_m[:, b, :]), tokens(ps[:, O_BANK, :]),
                                  sg_all[:, bass.ds(t, 1), :].rearrange("p o u -> p (o u)").unsqueeze(2).to_broadcast([P, U, C]),
                                  ALU.mult).then_inc(prod_ready, 1)

            for l in range(layers):
                group_norm(l)
                dve.wait_ge(gn_ready, l + 1)
                if l in TRIANGLES:
                    q = TRIANGLES[l]
                    pair_weights(q)
                    pipeline(dve, layer_norm(l, 0, xn, 2, [(0, lambda t, b: store_pairs(l, 0, t, b)),
                                                                (0, lambda t, b: store_pairs(l, 1, t, b))]))
                    dve.wait_ge(pair_stored, 2 * TILES * (q + 1))
                    pipeline(dve, [(1, lambda k, b: stage_stationary(q, k, b)),
                                   (0, lambda k, b: move_products(q, k, b))], BLOCKS)
                    dve.wait_ge(z_act, BLOCKS * (q + 1))
                    dve.wait_ge(z_dve, BLOCKS * (q + 1))
                    pipeline(dve, layer_norm(l, 1, xn_out, 3, [(0, lambda t, b, r: gated(l, t, b, r), RING),
                                                                (0, lambda t, b, r: update(l, t, b, r), RING)]))
                else:
                    pipeline(dve, layer_norm(l, 0, h_norm, 2, [(0, h_amax), (0, h_scale)]) + [
                                   (1, h_weight),
                                   (0, h_inverse),
                                   (-1, h_max),
                                   (0, h_rescale),
                                   (-1, h_add),
                                   (5, lambda t, b, r: centre(l, t, b, r), RING)])
                    dve.wait_ge(qT_ready, TILES)
                    pair = lambda pp: (0, lambda t, b, r: hidden_product(pp, t, b, r), RING)
                    amax = lambda half: (-1, lambda t, b, r: hidden_amax(half, t, b, r), RING)
                    add = lambda half: (-3, lambda t, b: hidden_add(half, t, b))
                    pipeline(dve, [pair(0), (-6, lambda t, b: mlp_update(l, t, b)), (-3, hidden_max),
                                   pair(1), add(0), add(1), (-1, square_sx),
                                   pair(2), amax(0), amax(1), (-1, amax_of_product),
                                   pair(3), (-1, hidden_row_scale), (-1, hidden_inverse), (-1, hidden_rescale)])

        @block.scalar
        def _(act):
            def square(r, b):
                act.wait_ge(shift_ready, r + 1)
                wait_free(act, sums_ready, r - 1)
                act.activation(squares[:, b, :], shifted[:, b, :], ACT.Square).then_inc(sq_ready, 1)

            def apart():
                act.sem_inc(s_apart, 1)

            def square_input(t, b):
                act.wait_ge(shift_ready, t + 1)
                wait_free(act, sums_ready, t - 1)
                apart()
                act.activation(squares[:, b, :], whole_tile(t), ACT.Square).then_inc(sq_ready, 1)

            for k, (lo, hi) in enumerate(SUM_PARTS):
                pipeline(act, [(0, square_input)], hi - lo, lo)
                if k == 0:
                    act.wait_ge(s_quant, 5)
                    act.activation(wq_magic, wq_y, ACT.Abs, scale=SPLIT).then_inc(s_quant_abs, 1)

            def evacuate_xnT(m, t, b, free_sem, free_value):
                act.wait_ge(xnT_psum, m + 1)
                if not (isinstance(t, int) and t < 2):
                    wait_free(act, free_sem, free_value)
                act.activation(xnT[:, b, :], ps[:, T_BANK + b, :], ACT.Copy, bias=1.0 / ROOT_C).then_inc(xnT_ready, 1)

            def normalise(l, side, dst, dst_used, t, b, r):
                n = ln_base(l, side) + t
                act.wait_ge(shift_step, n + 1)
                dst_used(t)
                if side:
                    apart()
                for u in range(DVE_TOKENS[l, side], U):
                    if side == 0:
                        src = normed[:, r, u * C:(u + 1) * C]
                    else:
                        src = pairs[:, 0, :, bass.ds(t * U + u, 1)].rearrange("p c o -> p (c o)")
                    last = act.activation(dst[:, r % dst.shape[1], u * C:(u + 1) * C], src, ACT.Identity,
                                          scale=ln_s[:, b, RSTD, u:u + 1], bias=ln_s[:, b, SHIFT, u:u + 1])
                last.then_inc(xn_act, 1)

            def gates(q, half, t, b):
                n = TILES * q + t
                if half == 0:
                    wait_free(act, gate_stored[b], landed(16, n - 2, b))
                    wait_free(act, pair_stored, 2 * (n - 1))
                act.wait_ge(gates_ready, 2 * n + half + 1)
                bank = GATE_BANK[half]
                act.activation(sig[:, b, :].rearrange("p (k g) -> p k g", k=PAIRS)[:, 2 * half:2 * half + 2, :],
                               ps[:, bank:bank + 2, 0:GATES], ACT.Sigmoid).then_inc(sig_ready, 1)

            def store_gate(q, t, b):
                act.wait_ge(sig_ready, 2 * (TILES * q + t + 1))
                act.dma_start(tokens(gate_dram[TILES * q + t]),
                             sig[:, b, :].rearrange("p (u g) -> p u g", u=U)[:, :, 2 * C:3 * C]).then_inc(gate_stored[b], 16)

            def stage_moving(q, k, b):
                wait_free(act, chan_done, 2 * (BLOCKS * q + k - 1))
                apart()
                act.activation(mov_a[:, b, :, :], pairs[:, 0, bass.ds(k * BLK, BLK), 0:N], ACT.Copy).then_inc(mov_staged, 1)

            def move_products(q, k, b):
                act.wait_ge(chan_done, 2 * (BLOCKS * q + k) + 1)
                apart()
                act.activation(pairs[:, 0, bass.ds(k * BLK, 2), :], ps[:, 0:2, 0:COLS], ACT.Copy).then_inc(z_act, 1)

            def h_abs(t, b):
                act.wait_ge(hs_ready, t + 1)
                wait_free(act, hq_ready, t - 1)
                act.activation(h_magic[:, b, :], h_scaled[:, b, :], ACT.Abs, scale=SPLIT).then_inc(habs_ready, 1)

            def evacuate_qT(t, b):
                act.wait_ge(qT_psum, t + 1)
                apart()
                act.activation(q_all[:, bass.ds(t, 1), :].rearrange("p o f -> p (o f)"),
                               ps[:, T_BANK + b, :].bitcast(BF16), ACT.Copy).then_inc(qT_ready, 1)

            def relu(pp, t, b):
                k = PAIRS * t + pp
                act.wait_ge(acc_ready, k + 1)
                wait_free(act, acc_used, k - 1)
                bank = 2 * (pp % 2)
                act.activation(relu_a[:, pp % 2, :].rearrange("p (u f) -> p u f", f=HID),
                               ps[:, bank:bank + 2, 0:HID], ACT.Relu).then_inc(relu_ready, 1)

            def hidden_scale(half, t, b, r):
                if half == 0:
                    act.wait_ge(hid_step, 6 * (t + 1))
                    wait_free(act, hid_q, 2 * (t - 1))
                for u in range(HALF * half, HALF * half + HALF):
                    last = act.activation(scaled[:, b, u * HID:(u + 1) * HID], hidden[:, r, u * HID:(u + 1) * HID],
                                          ACT.Copy, scale=rescale[:, b, u:u + 1])
                if half:
                    last.then_inc(hid_scaled, 1)

            def hidden_abs(half, t, b):
                part_ = slice(half * HALF * HID, (half + 1) * HALF * HID)
                act.wait_ge(hid_scaled, t + 1)
                act.activation(magic[:, b, part_], scaled[:, b, part_], ACT.Abs, scale=SPLIT).then_inc(hid_abs, 1)

            def evacuate_hqT(half, t, b):
                act.wait_ge(hqT_psum, 2 * t + half + 1)
                if half == 0:
                    wait_free(act, mlp_out_ready, t - 1)
                act.activation(q_hidT[:, b, half * 1024:(half + 1) * 1024], ps[:, H_BANK, :].bitcast(BF16), ACT.Copy)\
                    .then_inc(hqT_ready, 1)

            for l in range(layers):
                if l in TRIANGLES:
                    q = TRIANGLES[l]
                    xn_transposed = lambda side: lambda t: wait_free(act, xnT_psum, tr_base(l, side) + t - (1, 3)[side])
                    pipeline(act, [(0, lambda t, b: gates(q, 0, t, b)),
                                   (1, lambda t, b: evacuate_xnT(tr_base(l, 0) + t, t, b, proj_ready, 2 * (TILES * q + t - 1))),
                                   (0, lambda t, b: gates(q, 1, t, b)),
                                   (2, lambda t, b, r: normalise(l, 0, xn, xn_transposed(0), t, b, r), RING),
                                   (-1, lambda t, b: store_gate(q, t, b))])
                    act.wait_ge(pair_stored, 2 * TILES * (q + 1))
                    pipeline(act, [(1, lambda k, b: stage_moving(q, k, b)),
                                   (0, lambda k, b: move_products(q, k, b))], BLOCKS)
                    tail = [] if l == LAST else [(-1, lambda t, b: square(sum_base(l) + t, b))]
                    act.wait_ge(z_dve, BLOCKS * (q + 1))
                    act.wait_ge(z_act, BLOCKS * (q + 1))
                    pipeline(act, [(1, lambda t, b: evacuate_xnT(tr_base(l, 1) + t, t, b, out_ready, TILES * q + t - 1)),
                                   (3, lambda t, b, r: normalise(l, 1, xn_out, xn_transposed(1), t, b, r), RING)] + tail)
                else:
                    pipeline(act, [(2, lambda t, b, r: normalise(l, 0, h_norm, lambda t: wait_free(act, hw_ready, t - 1), t, b, r), RING),
                                   (0, h_abs), (-2, evacuate_qT)])
                    pair = lambda pp: (0, lambda t, b: relu(pp, t, b))
                    scale = lambda half: (-2, lambda t, b, r: hidden_scale(half, t, b, r), RING)
                    absolute = lambda half: (-2, lambda t, b: hidden_abs(half, t, b))
                    evacuate = lambda half: (-4, lambda t, b: evacuate_hqT(half, t, b))
                    pipeline(act, [pair(0), scale(0),
                                   pair(1), scale(1),
                                   pair(2), evacuate(0), absolute(0),
                                   pair(3), evacuate(1), absolute(1)])

        @block.tensor
        def _(pe):
            pe.wait_ge(s_const, 8)
            pe.wait_ge(x_whole[0], 16)
            pe.matmul(ps[:, 0, :], ones[:], x_all[:, 0, :], start=True, stop=True).then_inc(anchor_sum, 1)
            def add_to_sums(t, r, b, which=(SUM, SQ)):
                pe.wait_ge(sq_ready, r + 1)
                first = isinstance(t, int) and t == 0
                end = isinstance(t, int) and t == TILES - 1
                for bank in which:
                    src = shifted if bank == SUM else squares
                    last = pe.matmul(ps[:, bank, :], ones[:], src[:, b, :], start=first, stop=end, skip_group_check=True)
                if SQ in which:
                    last.then_inc(sums_ready, 1)

            for k, (lo, hi) in enumerate(SUM_PARTS):
                pipeline(pe, [(0, lambda t, b: add_to_sums(t, t, b, (SQ,)))], hi - lo, lo)
                if 1 <= k <= 3:
                    pe.wait_ge(s_fold, 4 * (k - 1) + 2)
                    pe.matmul(ps[:, 1, 0:PROJ + C], ones[0:C, :], fold_tmp[0:C, :], start=True, stop=True).then_inc(s_fold_pe, 1)
                if k == 3:
                    pe.wait_ge(s_quant, 9)
                    for j in range(4):
                        pe.transpose(ps[:, 2, j * P:(j + 1) * P], wq_y[:, j * P:(j + 1) * P], ident[:])
                    for j in range(2):
                        last = pe.transpose(ps[:, 3, j * C:(j + 1) * C], wq_y[0:C, 512 + j * P:512 + (j + 1) * P], ident[0:C, 0:C])
                    last.then_inc(s_quant_pe, 1)
            pe.wait_ge(input_acc, TILES - 1)
            pe.matmul(ps[:, SUM, :], ones[:], acc, start=True, stop=True, skip_group_check=True).then_inc(input_summed, 1)
            pe.wait_ge(s_fold, 13)
            pe.wait_ge(s_quant, 20)

            def transpose_xn(l, side, t, b, r):
                m = tr_base(l, side) + t
                src = xn_out[:, r, :] if side else xn[:, b, :]
                pe.wait_ge(xn_ready, ln_base(l, side) + t + 1)
                pe.wait_ge(xn_act, ln_base(l, side) + t + 1)
                wait_free(pe, xnT_ready, m - 1)
                for k in range(PAIRS):
                    last = pe.transpose(ps[:, T_BANK + b, k * P:(k + 1) * P], src[:, k * P:(k + 1) * P], ident[:])
                last.then_inc(xnT_psum, 1)

            def project(l, half, t, b):
                n = 2 * (TILES * TRIANGLES[l] + t) + half
                if half == 0:
                    pe.wait_ge(xnT_ready, tr_base(l, 0) + t + 1)
                wait_free(pe, sig_ready, n - 1)
                for k in range(2):
                    last = pe.matmul(ps[:, GATE_BANK[half] + k, 0:GATES], xnT[:, b, (2 * half + k) * P:(2 * half + k + 1) * P],
                                     wpair[:, VALUES:VALUES + GATES], start=True, stop=True)
                last.then_inc(gates_ready, 1)
                wait_free(pe, pair_stored, n - 1)
                for k in range(2):
                    last = pe.matmul(ps[:, half, k * VALUES:(k + 1) * VALUES], xnT[:, b, (2 * half + k) * P:(2 * half + k + 1) * P],
                                     wpair[:, 0:VALUES], start=True, stop=True)
                last.then_inc(proj_ready, 1)

            def multiply(q, k, b):
                n = BLOCKS * q + k
                pe.wait_ge(stat_staged, n + 1)
                pe.wait_ge(mov_staged, n + 1)

                def product(c, part_):
                    stat, mov = ((stat_a, mov_a), (stat_b, mov_b))[part_]
                    pe.matmul(ps[:, c, 0:N], stat[:, b, c, 0:P], mov[:, b, c, :], start=part_ == 0, stop=part_ == 1)

                def rest(c):
                    for h in range(2):
                        for part_, (stat, mov) in enumerate(((stat_a, mov_a), (stat_b, mov_b))):
                            last = pe.matmul(ps[64 * h:64 * h + 64, c, N:COLS], stat[:, b, c, P:N], mov[:, b, c, 96 * h:96 * h + 96],
                                             start=part_ == 0, stop=part_ == 1)
                    if c % 2:
                        last.then_inc(chan_done, 1)

                def banks_moved(c):
                    if c == 0:
                        wait_free(pe, z_act, n)
                    if c == 2:
                        wait_free(pe, z_dve, n)

                first = isinstance(k, int) and k == 0
                if first:
                    for c in range(BLK):
                        banks_moved(c)
                        product(c, 0)
                    pe.wait_ge(b_padded, 2 * (q + 1))
                pe.wait_ge(b_staged[b], landed(64, n, b))
                for c in range(BLK):
                    if not first:
                        banks_moved(c)
                        product(c, 0)
                    product(c, 1)
                    rest(c)

            def project_out(l, t, b):
                q = TRIANGLES[l]
                pe.wait_ge(xnT_ready, tr_base(l, 1) + t + 1)
                wait_free(pe, prod_ready, x_base(l) + t - 1)
                for k in range(PAIRS):
                    last = pe.matmul(ps[:, b, k * P:(k + 1) * P], xnT[:, b, k * P:(k + 1) * P],
                                     wpair[:, 2 * PROJ:], start=True, stop=True)
                last.then_inc(out_ready, 1)

            def transpose_q(t, b):
                pe.wait_ge(hq_ready, t + 1)
                wait_free(pe, qT_ready, t - 1)
                pe.sem_inc(s_pe_apart, 1)
                for u in range(U):
                    for copy in range(2):
                        last = pe.transpose(ps[copy * C:copy * C + C, T_BANK + b, :].bitcast(BF16)[:, u * P:(u + 1) * P],
                                            q_in[:, b, u * C:(u + 1) * C], ident16[:])
                last.then_inc(qT_psum, 1)

            def hidden_layer(pp, t, b):
                if isinstance(t, int) and t == 0 and pp == 0:
                    pe.wait_ge(qT_ready, TILES)
                k = PAIRS * t + pp
                wait_free(pe, acc_used, k - 1)
                for h in range(2):
                    out_ab = ps[:, 2 * (pp % 2) + h, :]
                    u = 2 * pp + h
                    q_token = q_all[:, bass.ds(t, 1), u * P:(u + 1) * P].rearrange("p o n -> p (o n)")
                    pe.matmul(out_ab, q_token, w1s[:, 0, :], start=True, stop=False)
                    last = pe.matmul(out_ab, q_token[0:C], w1s[0:C, 2, :], start=False, stop=True)
                last.then_inc(acc_ready, 1)

            def transpose_hidden(half, t, b):
                pe.wait_ge(hid_q, 2 * t + half + 1)
                wait_free(pe, hqT_ready, 2 * t + half)
                for k in range(8):
                    last = pe.transpose(ps[:, H_BANK, :].bitcast(BF16)[:, k * P:(k + 1) * P],
                                        q_hid[:, b, (8 * half + k) * P:(8 * half + k + 1) * P], ident16[:])
                last.then_inc(hqT_psum, 1)

            def mlp_out(l, half, t, b):
                if half == 0:
                    pe.wait_ge(hqT_ready, 2 * (t + 1))
                    wait_free(pe, prod_ready, x_base(l) + t)
                for u in range(HALF * half, HALF * half + HALF):
                    for part_ in range(3):
                        for chunk in range(2):
                            last = pe.matmul(ps[:, O_BANK, u * C:(u + 1) * C], q_hidT[:, b, (2 * u + chunk) * P:(2 * u + chunk + 1) * P],
                                             w2s[:, part_, chunk * C:(chunk + 1) * C],
                                             start=(part_ == 0 and chunk == 0), stop=(part_ == 2 and chunk == 1))
                if half:
                    last.then_inc(mlp_out_ready, 1)

            for l in range(layers):
                pe.wait_ge(gn_picked, l + 1)
                pe.matmul(ps[:, 0, 0:GROUPS], ones[:], gn_roots[:], start=True, stop=True).then_inc(gn_spread, 1)
                if l in TRIANGLES:
                    q = TRIANGLES[l]
                    pe.wait_ge(w_step, q + 2)
                    pipeline(pe, [(0, lambda t, b: project(l, 0, t, b)),
                                  (1, lambda t, b, r: transpose_xn(l, 0, t, b, r), RING),
                                  (0, lambda t, b: project(l, 1, t, b))])
                    pipeline(pe, [(0, lambda k, b: multiply(q, k, b))], BLOCKS)
                    tail = [] if l == LAST else [(-2, lambda t, b: add_to_sums(t, sum_base(l) + t, b))]
                    pipeline(pe, [(0, lambda t, b: project_out(l, t, b)),
                                  (1, lambda t, b, r: transpose_xn(l, 1, t, b, r), RING)] + tail)
                else:
                    pipeline(pe, [(-1, transpose_q)])
                    pair = lambda pp: (0, lambda t, b: hidden_layer(pp, t, b))
                    turn = lambda half: (-4, lambda t, b: transpose_hidden(half, t, b))
                    out_half = lambda half: (-5, lambda t, b: mlp_out(l, half, t, b))
                    sums = lambda bank: (-7, lambda t, b: add_to_sums(t, sum_base(l) + t, b, (bank,)))
                    pipeline(pe, [pair(0), pair(1), sums(SUM), turn(0), out_half(0),
                                  pair(2), sums(SQ), pair(3), turn(1), out_half(1)])


def tiles_of(a):
    rest = a.shape[2:]
    part_a = a[:, :P].reshape(TILES_A, U, P, *rest).swapaxes(1, 2)
    part_b = a[:, P:].reshape(2, TILES - TILES_A, U, N - P, *rest)
    part_b = np.moveaxis(part_b, (0, 3), (1, 2)).reshape(TILES - TILES_A, P, U, *rest)
    return np.ascontiguousarray(np.concatenate([part_a, part_b]))


def image_of(tiles):
    part_a = tiles[:TILES_A].swapaxes(1, 2).reshape(N, P, C)
    part_b = tiles[TILES_A:].reshape(TILES - TILES_A, 2, N - P, U, C)
    part_b = np.moveaxis(part_b, (1, 2), (0, 3)).reshape(N, N - P, C)
    return np.ascontiguousarray(np.concatenate([part_a, part_b], axis=1))


def kernel(**inputs):
    import concourse.bacc as bacc
    from concourse.bass_utils import run_bass_kernel_spmd

    a = {k: np.asarray(v) for k, v in inputs.items()}
    zeros = np.zeros(C, np.float32)
    g = lambda l, names: [a[f"L{l}_conv_{n}"] for n in names.split()]
    w_l0 = [w.T for w in g(0, "left_w right_w lgate_w rgate_w ogate_w out_w")]
    proj = a["L1_conv_W_proj"]
    w_l1 = [proj[:, C:2 * C], proj[:, 3 * C:], proj[:, :C], proj[:, 2 * C:3 * C], *g(1, "W_gate W_ab")]
    w_l3 = g(3, "Wa Wb Wga Wgb Wgo Wo")
    w = np.stack([np.concatenate(x, 1) for x in (w_l0, w_l1, w_l3)], 1)
    b = [g(0, "left_b right_b lgate_b rgate_b ogate_b out_b"), [zeros] * 6, g(3, "ba bb bga bgb bgo bo")]
    n = [g(0, "norm_w norm_b ton_w ton_b"), g(1, "ln1_g ln1_b ln2_g ln2_b"), g(3, "norm_g norm_b norm_out_g norm_out_b")]
    norms = np.stack([np.stack(x, 1) for x in n], 1)
    w1 = a["L2_conv_w1"].reshape(4, P, 1, C)
    arrays = {
        "x_in": tiles_of(a["x"][0].swapaxes(0, 1)).reshape(TILES, P, ROW),
        "weights": np.concatenate([w, w]),
        "biases": np.stack([np.concatenate(x) for x in b]),
        "norms": np.concatenate([norms, norms]),
        "mask": tiles_of(a["L3_conv_mask"][0]).swapaxes(0, 1).reshape(P, COLS),
        "mlp_norm": np.stack(g(2, "ln_w ln_b")),
        "w1": np.concatenate([w1, w1], 2).swapaxes(0, 1).reshape(P, 4 * P),
        "w2": a["L2_conv_w2"],
    }
    arrays = {f"in_{k}": np.ascontiguousarray(v) for k, v in arrays.items()}
    nc = bacc.Bacc("TRN2", target_bir_lowering=False, num_devices=1)
    args = [nc.dram_tensor(k, v.shape, mybir.dt.from_np(v.dtype), kind="ExternalInput").ap() for k, v in arrays.items()]
    args.append(nc.dram_tensor("out_x", (TILES, P, ROW), F32, kind="ExternalOutput").ap())
    build(nc, *args)
    r = run_bass_kernel_spmd(nc, [arrays], core_ids=[0])
    return image_of(r.results[0]["out_x"].reshape(TILES, P, U, C))[None]
```
